# Optimizing a Trainium2 kernel written in Bass

```python
import numpy as np
import jax
import jax.numpy as jnp

def _softmax(x, axis=-1):
    return jax.nn.softmax(x, axis=axis)

def _gelu(x):
    return jax.nn.gelu(x, approximate=True)

def _silu(x):
    return jax.nn.silu(x)

def _sigmoid(x):
    return jax.nn.sigmoid(x)

def _layernorm(x, axis=-1, eps=1e-05):
    m = jnp.mean(x, axis=axis, keepdims=True)
    v = jnp.var(x, axis=axis, keepdims=True)
    return (x - m) / jnp.sqrt(v + eps)

def _scatter_add(tgt, idx, src, axis=0):
    return tgt.at[idx].add(src)

def _segment_sum(src, seg, n):
    return jax.ops.segment_sum(src, seg, n)
kernel_name = 'mk_adj_seq_d4_adj_r2_9cd021'

def setup_inputs(seed: int=0):
    np.random.seed(seed)
    _w = jnp.asarray

    def _rec_inputs():
        import jax
        import jax.numpy as jnp
        _gk = jax.random.key(seed)
        x = -0.0005207 + 1.001 * jax.random.normal(jax.random.fold_in(_gk, 1), (8, 1024, 256), jnp.float32)
        _w = (1.0 + jnp.arange(1024, dtype=jnp.float32)) ** (-0.5)
        _w = _w / _w.mean()
        _pij = jnp.clip(0.015625 * _w[:, None] * _w[None, :], 0.0, 1.0)
        _a = jax.random.uniform(jax.random.fold_in(_gk, 2), (8, 1024, 1024)) < _pij
        _a = jnp.logical_or(_a, jnp.eye(1024, dtype=bool))
        adj = _a.astype(jnp.int32)
        return (x, adj)
    x, adj = _rec_inputs()

    def _L0_gnn_setup():
        import jax, jax.numpy as jnp
        import numpy as np
        B, S, D, H = (2, 1024, 256, 8)
        HD = D // H
        EPS = 1e-05

        def _ln(x, g, b):
            mu = jnp.mean(x, axis=-1, keepdims=True)
            var = jnp.mean((x - mu) ** 2, axis=-1, keepdims=True)
            return (x - mu) * jax.lax.rsqrt(var + EPS) * g + b
        key = jax.random.key(seed)
        ks = jax.random.split(key, 16)
        x = jax.random.normal(ks[0], (B, S, D), dtype=jnp.float32)
        adj = jax.random.randint(ks[1], (B, S, S), 0, 2, dtype=jnp.int32)
        adj = adj.at[:, jnp.arange(S), jnp.arange(S)].set(1)
        edge_attr = jax.random.normal(ks[2], (B, S, S), dtype=jnp.float32)
        sc = 1.0 / np.sqrt(D)
        p = lambda k, shp: jax.random.normal(k, shp, dtype=jnp.float32) * sc
        return {'x': x, 'adj_matrix': adj, 'edge_attr_matrix': edge_attr, 'ln1_g': jnp.ones((D,)), 'ln1_b': jnp.zeros((D,)), 'ln2_g': jnp.ones((D,)), 'ln2_b': jnp.zeros((D,)), 'wq': p(ks[3], (D, D)), 'bq': jnp.zeros((D,)), 'wk': p(ks[4], (D, D)), 'bk': jnp.zeros((D,)), 'wv': p(ks[5], (D, D)), 'bv': jnp.zeros((D,)), 'wo': p(ks[6], (D, D)), 'bo': jnp.zeros((D,)), 'w1': p(ks[7], (D, 4 * D)), 'b1': jnp.zeros((4 * D,)), 'w2': p(ks[8], (4 * D, D)), 'b2': jnp.zeros((D,))}
    _L0_gnn_all = _L0_gnn_setup()
    _L0_gnn_in = {k: v for k, v in _L0_gnn_all.items() if k in ('ln1_g', 'ln1_b', 'ln2_g', 'ln2_b', 'wq', 'bq', 'wk', 'bk', 'wv', 'bv', 'wo', 'bo', 'w1', 'b1', 'w2', 'b2')}
    del _L0_gnn_all

    def _L1_gnn_setup():
        import jax, jax.numpy as jnp
        import numpy as np
        import math
        D = 256
        B, L = (8, 1024)
        EPS = 1e-05

        def layer_norm(y, gamma, beta):
            mu = jnp.mean(y, axis=-1, keepdims=True)
            var = jnp.mean(jnp.square(y - mu), axis=-1, keepdims=True)
            return (y - mu) * jax.lax.rsqrt(var + EPS) * gamma + beta
        key = jax.random.key(seed)
        ks = jax.random.split(key, 8)
        s = 1.0 / math.sqrt(D)
        x = jax.random.normal(ks[0], (B, L, D), dtype=jnp.float32)
        adj = jax.random.randint(ks[1], (B, L, L), 0, 2, dtype=jnp.int32)
        Wq = jax.random.normal(ks[2], (D, D), dtype=jnp.float32) * s
        Wk = jax.random.normal(ks[3], (D, D), dtype=jnp.float32) * s
        Wv = jax.random.normal(ks[4], (D, D), dtype=jnp.float32) * s
        Wo = jax.random.normal(ks[5], (D, D), dtype=jnp.float32) * s
        bo = jnp.zeros((D,), dtype=jnp.float32)
        gamma = jnp.ones((D,), dtype=jnp.float32)
        beta = jnp.zeros((D,), dtype=jnp.float32)
        return {'x': x, 'adj': adj, 'Wq': Wq, 'Wk': Wk, 'Wv': Wv, 'Wo': Wo, 'bo': bo, 'gamma': gamma, 'beta': beta}
    _L1_gnn_all = _L1_gnn_setup()
    _L1_gnn_in = {k: v for k, v in _L1_gnn_all.items() if k in ('Wq', 'Wk', 'Wv', 'Wo', 'bo', 'gamma', 'beta')}
    del _L1_gnn_all

    def _L2_gnn_setup():
        import jax, jax.numpy as jnp
        import numpy as np
        import math
        D = 256
        B, L = (8, 1024)
        EPS = 1e-05

        def layer_norm(y, gamma, beta):
            mu = jnp.mean(y, axis=-1, keepdims=True)
            var = jnp.mean(jnp.square(y - mu), axis=-1, keepdims=True)
            return (y - mu) * jax.lax.rsqrt(var + EPS) * gamma + beta
        key = jax.random.key(seed)
        ks = jax.random.split(key, 8)
        s = 1.0 / math.sqrt(D)
        x = jax.random.normal(ks[0], (B, L, D), dtype=jnp.float32)
        adj = jax.random.randint(ks[1], (B, L, L), 0, 2, dtype=jnp.int32)
        Wq = jax.random.normal(ks[2], (D, D), dtype=jnp.float32) * s
        Wk = jax.random.normal(ks[3], (D, D), dtype=jnp.float32) * s
        Wv = jax.random.normal(ks[4], (D, D), dtype=jnp.float32) * s
        Wo = jax.random.normal(ks[5], (D, D), dtype=jnp.float32) * s
        bo = jnp.zeros((D,), dtype=jnp.float32)
        gamma = jnp.ones((D,), dtype=jnp.float32)
        beta = jnp.zeros((D,), dtype=jnp.float32)
        return {'x': x, 'adj': adj, 'Wq': Wq, 'Wk': Wk, 'Wv': Wv, 'Wo': Wo, 'bo': bo, 'gamma': gamma, 'beta': beta}
    _L2_gnn_all = _L2_gnn_setup()
    _L2_gnn_in = {k: v for k, v in _L2_gnn_all.items() if k in ('Wq', 'Wk', 'Wv', 'Wo', 'bo', 'gamma', 'beta')}
    del _L2_gnn_all

    def _L3_gnn_setup():
        import jax, jax.numpy as jnp
        import numpy as np
        B, N, D, H = (4, 1024, 256, 8)
        HD = D // H
        EPS = 1e-05
        key = jax.random.key(seed)
        ks = jax.random.split(key, 12)
        x = jax.random.normal(ks[0], (B, N, D), dtype=jnp.float32)
        adj = jax.random.randint(ks[1], (B, N, N), 0, 2, dtype=jnp.int32)
        adj = jnp.maximum(adj, jnp.eye(N, dtype=jnp.int32)[None, :, :])
        s = 1.0 / np.sqrt(D)
        Wq = jax.random.uniform(ks[2], (D, D), jnp.float32, -s, s)
        bq = jnp.zeros((D,), jnp.float32)
        Wk = jax.random.uniform(ks[3], (D, D), jnp.float32, -s, s)
        bk = jnp.zeros((D,), jnp.float32)
        Wv = jax.random.uniform(ks[4], (D, D), jnp.float32, -s, s)
        bv = jnp.zeros((D,), jnp.float32)
        Wo = jax.random.uniform(ks[5], (D, D), jnp.float32, -s, s)
        bo = jnp.zeros((D,), jnp.float32)
        gamma = jnp.ones((D,), jnp.float32)
        beta = jnp.zeros((D,), jnp.float32)
        return {'x': x, 'adj': adj, 'Wq': Wq, 'bq': bq, 'Wk': Wk, 'bk': bk, 'Wv': Wv, 'bv': bv, 'Wo': Wo, 'bo': bo, 'gamma': gamma, 'beta': beta}
    _L3_gnn_all = _L3_gnn_setup()
    _L3_gnn_in = {k: v for k, v in _L3_gnn_all.items() if k in ('Wq', 'bq', 'Wk', 'bk', 'Wv', 'bv', 'Wo', 'bo', 'gamma', 'beta')}
    del _L3_gnn_all
    return {'x': x, 'adj': adj, 'L0_gnn_ln1_g': _L0_gnn_in['ln1_g'], 'L0_gnn_ln1_b': _L0_gnn_in['ln1_b'], 'L0_gnn_ln2_g': _L0_gnn_in['ln2_g'], 'L0_gnn_ln2_b': _L0_gnn_in['ln2_b'], 'L0_gnn_wq': _L0_gnn_in['wq'], 'L0_gnn_bq': _L0_gnn_in['bq'], 'L0_gnn_wk': _L0_gnn_in['wk'], 'L0_gnn_bk': _L0_gnn_in['bk'], 'L0_gnn_wv': _L0_gnn_in['wv'], 'L0_gnn_bv': _L0_gnn_in['bv'], 'L0_gnn_wo': _L0_gnn_in['wo'], 'L0_gnn_bo': _L0_gnn_in['bo'], 'L0_gnn_w1': _L0_gnn_in['w1'], 'L0_gnn_b1': _L0_gnn_in['b1'], 'L0_gnn_w2': _L0_gnn_in['w2'], 'L0_gnn_b2': _L0_gnn_in['b2'], 'L1_gnn_Wq': _L1_gnn_in['Wq'], 'L1_gnn_Wk': _L1_gnn_in['Wk'], 'L1_gnn_Wv': _L1_gnn_in['Wv'], 'L1_gnn_Wo': _L1_gnn_in['Wo'], 'L1_gnn_bo': _L1_gnn_in['bo'], 'L1_gnn_gamma': _L1_gnn_in['gamma'], 'L1_gnn_beta': _L1_gnn_in['beta'], 'L2_gnn_Wq': _L2_gnn_in['Wq'], 'L2_gnn_Wk': _L2_gnn_in['Wk'], 'L2_gnn_Wv': _L2_gnn_in['Wv'], 'L2_gnn_Wo': _L2_gnn_in['Wo'], 'L2_gnn_bo': _L2_gnn_in['bo'], 'L2_gnn_gamma': _L2_gnn_in['gamma'], 'L2_gnn_beta': _L2_gnn_in['beta'], 'L3_gnn_Wq': _L3_gnn_in['Wq'], 'L3_gnn_bq': _L3_gnn_in['bq'], 'L3_gnn_Wk': _L3_gnn_in['Wk'], 'L3_gnn_bk': _L3_gnn_in['bk'], 'L3_gnn_Wv': _L3_gnn_in['Wv'], 'L3_gnn_bv': _L3_gnn_in['bv'], 'L3_gnn_Wo': _L3_gnn_in['Wo'], 'L3_gnn_bo': _L3_gnn_in['bo'], 'L3_gnn_gamma': _L3_gnn_in['gamma'], 'L3_gnn_beta': _L3_gnn_in['beta']}

def reference(x, adj, L0_gnn_ln1_g, L0_gnn_ln1_b, L0_gnn_ln2_g, L0_gnn_ln2_b, L0_gnn_wq, L0_gnn_bq, L0_gnn_wk, L0_gnn_bk, L0_gnn_wv, L0_gnn_bv, L0_gnn_wo, L0_gnn_bo, L0_gnn_w1, L0_gnn_b1, L0_gnn_w2, L0_gnn_b2, L1_gnn_Wq, L1_gnn_Wk, L1_gnn_Wv, L1_gnn_Wo, L1_gnn_bo, L1_gnn_gamma, L1_gnn_beta, L2_gnn_Wq, L2_gnn_Wk, L2_gnn_Wv, L2_gnn_Wo, L2_gnn_bo, L2_gnn_gamma, L2_gnn_beta, L3_gnn_Wq, L3_gnn_bq, L3_gnn_Wk, L3_gnn_bk, L3_gnn_Wv, L3_gnn_bv, L3_gnn_Wo, L3_gnn_bo, L3_gnn_gamma, L3_gnn_beta):
    import jax
    import jax.numpy as jnp

    def _L0_gnn_ref(x, adj_matrix, edge_attr_matrix, ln1_g, ln1_b, ln2_g, ln2_b, wq, bq, wk, bk, wv, bv, wo, bo, w1, b1, w2, b2):
        import jax, jax.numpy as jnp
        import numpy as np
        B, S, D, H = (2, 1024, 256, 8)
        HD = D // H
        EPS = 1e-05

        def _ln(x, g, b):
            mu = jnp.mean(x, axis=-1, keepdims=True)
            var = jnp.mean((x - mu) ** 2, axis=-1, keepdims=True)
            return (x - mu) * jax.lax.rsqrt(var + EPS) * g + b
        b, s, d = x.shape
        residual = x
        nx = _ln(x, ln1_g, ln1_b)
        q = (nx @ wq + bq).reshape(b, s, H, HD).transpose(0, 2, 1, 3)
        k = (nx @ wk + bk).reshape(b, s, H, HD).transpose(0, 2, 1, 3)
        v = (nx @ wv + bv).reshape(b, s, H, HD).transpose(0, 2, 1, 3)
        adjf = adj_matrix.astype(jnp.float32)
        bias = jnp.where(adj_matrix > 0, 0.1 * edge_attr_matrix * adjf, -jnp.inf)[:, None]
        scores = jnp.einsum('bhqd,bhkd->bhqk', q, k) / np.sqrt(HD) + bias
        attn = jax.nn.softmax(scores, axis=-1)
        out = jnp.einsum('bhqk,bhkd->bhqd', attn, v)
        out = out.transpose(0, 2, 1, 3).reshape(b, s, d)
        x1 = residual + (out @ wo + bo)
        n2 = _ln(x1, ln2_g, ln2_b)
        mlp = jax.nn.gelu(n2 @ w1 + b1, approximate=False) @ w2 + b2
        return x1 + mlp

    def _L1_gnn_ref(x, adj, Wq, Wk, Wv, Wo, bo, gamma, beta):
        import jax, jax.numpy as jnp
        import numpy as np
        import math
        D = 256
        B, L = (8, 1024)
        EPS = 1e-05

        def layer_norm(y, gamma, beta):
            mu = jnp.mean(y, axis=-1, keepdims=True)
            var = jnp.mean(jnp.square(y - mu), axis=-1, keepdims=True)
            return (y - mu) * jax.lax.rsqrt(var + EPS) * gamma + beta
        d_out = Wq.shape[1]
        scale = 1.0 / math.sqrt(d_out)
        Q = x @ Wq
        K = x @ Wk
        V = x @ Wv
        sc = jnp.einsum('bld,bmd->blm', Q, K) * scale
        mask = adj == 0
        sc = jnp.where(mask, -jnp.inf, sc)
        all_inf = jnp.all(mask, axis=-1, keepdims=True)
        sc = jnp.where(all_inf, 0.0, sc)
        w = jax.nn.softmax(sc, axis=-1)
        out = jnp.einsum('blm,bmd->bld', w, V)
        y = x + out @ Wo + bo
        return layer_norm(y, gamma, beta)

    def _L2_gnn_ref(x, adj, Wq, Wk, Wv, Wo, bo, gamma, beta):
        import jax, jax.numpy as jnp
        import numpy as np
        import math
        D = 256
        B, L = (8, 1024)
        EPS = 1e-05

        def layer_norm(y, gamma, beta):
            mu = jnp.mean(y, axis=-1, keepdims=True)
            var = jnp.mean(jnp.square(y - mu), axis=-1, keepdims=True)
            return (y - mu) * jax.lax.rsqrt(var + EPS) * gamma + beta
        d_out = Wq.shape[1]
        scale = 1.0 / math.sqrt(d_out)
        Q = x @ Wq
        K = x @ Wk
        V = x @ Wv
        sc = jnp.einsum('bld,bmd->blm', Q, K) * scale
        mask = adj == 0
        sc = jnp.where(mask, -jnp.inf, sc)
        all_inf = jnp.all(mask, axis=-1, keepdims=True)
        sc = jnp.where(all_inf, 0.0, sc)
        w = jax.nn.softmax(sc, axis=-1)
        out = jnp.einsum('blm,bmd->bld', w, V)
        y = x + out @ Wo + bo
        return layer_norm(y, gamma, beta)

    def _L3_gnn_ref(x, adj, Wq, bq, Wk, bk, Wv, bv, Wo, bo, gamma, beta):
        import jax, jax.numpy as jnp
        import numpy as np
        B, N, D, H = (4, 1024, 256, 8)
        HD = D // H
        EPS = 1e-05
        b, n, d = x.shape
        scale = 1.0 / np.sqrt(HD).astype(np.float32)
        q = (x @ Wq + bq).reshape(b, n, H, HD)
        k = (x @ Wk + bk).reshape(b, n, H, HD)
        v = (x @ Wv + bv).reshape(b, n, H, HD)
        scores = jnp.einsum('bnhd,bmhd->bhnm', q, k) * scale
        mask = (adj == 0)[:, None, :, :]
        scores = jnp.where(mask, jnp.float32(-jnp.inf), scores)
        attn = jax.nn.softmax(scores, axis=-1)
        h = jnp.einsum('bhnm,bmhd->bnhd', attn, v).reshape(b, n, d)
        h = h @ Wo + bo
        y = h + x
        mu = jnp.mean(y, axis=-1, keepdims=True)
        var = jnp.mean(jnp.square(y - mu), axis=-1, keepdims=True)
        return (y - mu) * jax.lax.rsqrt(var + EPS) * gamma + beta
    x = _L0_gnn_ref(x, adj, adj, L0_gnn_ln1_g, L0_gnn_ln1_b, L0_gnn_ln2_g, L0_gnn_ln2_b, L0_gnn_wq, L0_gnn_bq, L0_gnn_wk, L0_gnn_bk, L0_gnn_wv, L0_gnn_bv, L0_gnn_wo, L0_gnn_bo, L0_gnn_w1, L0_gnn_b1, L0_gnn_w2, L0_gnn_b2)
    x = _L1_gnn_ref(x, adj, L1_gnn_Wq, L1_gnn_Wk, L1_gnn_Wv, L1_gnn_Wo, L1_gnn_bo, L1_gnn_gamma, L1_gnn_beta)
    x = _L2_gnn_ref(x, adj, L2_gnn_Wq, L2_gnn_Wk, L2_gnn_Wv, L2_gnn_Wo, L2_gnn_bo, L2_gnn_gamma, L2_gnn_beta)
    x = _L3_gnn_ref(x, adj, L3_gnn_Wq, L3_gnn_bq, L3_gnn_Wk, L3_gnn_bk, L3_gnn_Wv, L3_gnn_bv, L3_gnn_Wo, L3_gnn_bo, L3_gnn_gamma, L3_gnn_beta)
    return x

_drawn_inputs = setup_inputs


def setup_inputs(seed=0):
    import zlib

    import numpy as np

    out = dict(_drawn_inputs(seed))
    spreads = {'L0_gnn_ln1_g': (1.0, 0.2),
     'L0_gnn_ln1_b': (0.0, 0.1),
     'L0_gnn_ln2_g': (1.0, 0.2),
     'L0_gnn_ln2_b': (0.0, 0.1),
     'L0_gnn_bq': (0.0, 0.1),
     'L0_gnn_bk': (0.0, 0.8),
     'L0_gnn_bv': (0.0, 0.1),
     'L0_gnn_bo': (0.0, 0.1),
     'L0_gnn_b1': (0.0, 0.1),
     'L0_gnn_b2': (0.0, 0.1),
     'L1_gnn_bo': (0.0, 0.1),
     'L1_gnn_gamma': (1.0, 0.2),
     'L1_gnn_beta': (0.0, 0.1),
     'L2_gnn_bo': (0.0, 0.1),
     'L2_gnn_gamma': (1.0, 0.2),
     'L2_gnn_beta': (0.0, 0.1),
     'L3_gnn_bq': (0.0, 0.8),
     'L3_gnn_bk': (0.0, 0.8),
     'L3_gnn_bv': (0.0, 0.1),
     'L3_gnn_bo': (0.0, 0.1),
     'L3_gnn_gamma': (1.0, 0.2),
     'L3_gnn_beta': (0.0, 0.1)}
    factors = {'L3_gnn_Wq': 3.083, 'L3_gnn_Wk': 3.133}
    for name, (base, spread) in spreads.items():
        noise = np.random.default_rng([zlib.crc32(name.encode()), seed]).standard_normal(out[name].shape)
        drawn = base * np.exp(spread * noise) if base else spread * noise
        out[name] = jnp.asarray(drawn.astype(out[name].dtype))
    for name, factor in factors.items():
        out[name] = (out[name] * factor).astype(out[name].dtype)
    return out
```

```python
from contextlib import ExitStack

import concourse.bass as bass
from concourse import mybir

F32 = mybir.dt.float32
F32R = mybir.dt.float32r
I32 = mybir.dt.int32
ALU = mybir.AluOpType
ACT = mybir.ActivationFunctionType

P = 128
BATCH, SEQ, DIM = 8, 1024, 256
HEADS = 8
HEAD_DIM = DIM // HEADS
HIDDEN = 4 * DIM
TILES = SEQ // P
DIM_TILES = DIM // P
GROUP = P // HEAD_DIM
GROUPS = HEADS // GROUP
STACK = 3 * HEAD_DIM
BANK = 512
HALVES = SEQ // BANK
PENALTY = 1.0e30
EPS = 1e-5
STATS = 6


class Pool:

    def __init__(self, nc, ctx, tag):
        self.nc, self.ctx, self.tag = nc, ctx, tag
        self.sems = []

    def sb(self, name, shape, dtype=F32):
        return self.ctx.enter_context(self.nc.sbuf_tensor(f"{self.tag}_{name}", shape, dtype))

    def ps(self, name, shape):
        return self.ctx.enter_context(self.nc.psum_tensor(f"{self.tag}_{name}", shape, F32))

    def sem(self, name):
        s = self.ctx.enter_context(self.nc.semaphore(f"{self.tag}_{name}"))
        self.sems.append(s)
        return s

    def clear(self):
        for s in self.sems:
            self.nc.gpsimd.sem_clear(s)
        self.nc.all_engine_barrier()


def of_batch(dram, b):
    return dram[bass.ds(b, 1)].rearrange("a s n -> (a s) n")


def split_matmul(nc, out, lhs_high, lhs_low, rhs_high, rhs_low, start, stop):
    nc.tensor.matmul(out, lhs_high, rhs_high, start=start, stop=False)
    nc.tensor.matmul(out, lhs_high, rhs_low, start=False, stop=False)
    return nc.tensor.matmul(out, lhs_low, rhs_high, start=False, stop=stop)


def split_weights(nc, weights, tag):
    with ExitStack() as ctx:
        m = Pool(nc, ctx, tag)
        s_scaled, s_high, s_low = m.sem("scaled"), m.sem("high"), m.sem("low")
        with nc.Block() as block:

            @block.vector
            def _(dve):
                for n, (raw, high, low, factor, gain) in enumerate(weights):
                    for k in range(raw.shape[1]):
                        if gain is None:
                            op = nc.vector.tensor_scalar(raw[:, k, :], raw[:, k, :], factor, None, ALU.mult)
                        else:
                            op = nc.vector.tensor_scalar(raw[:, k, :], raw[:, k, :], gain[:, k:k + 1], factor,
                                                         ALU.mult, ALU.mult)
                    op.then_inc(s_scaled, 1)
                for n, (raw, high, low, factor, gain) in enumerate(weights):
                    dve.wait_ge(s_scaled, n + 1)
                    dve.wait_ge(s_high, n + 1)
                    nc.vector.tensor_tensor(low, raw, high.bitcast(F32), ALU.subtract).then_inc(s_low, 1)
                dve.wait_ge(s_low, len(weights))

            @block.scalar
            def _(act):
                for n, (raw, high, low, factor, gain) in enumerate(weights):
                    act.wait_ge(s_scaled, n + 1)
                    nc.scalar.copy(high, raw).then_inc(s_high, 1)
                act.wait_ge(s_high, len(weights))

        m.clear()


def load_all(nc, pairs, tag):
    with ExitStack() as ctx:
        m = Pool(nc, ctx, tag)
        s_loaded = m.sem("loaded")
        with nc.Block() as block:

            @block.sync
            def _(sp):
                for destination, source in pairs:
                    sp.dma_start(destination, source, allow_slow_non_contiguous=True).then_inc(s_loaded, 16)
                sp.wait_ge(s_loaded, 16 * len(pairs))

        m.clear()


def matrix(dram):
    return dram.rearrange("(k p) n -> p k n", p=P)


def column(dram):
    return dram.rearrange("(k p) -> p k", p=P)


def spread(dram):
    return dram.rearrange("(a n) -> a n", a=1).partition_broadcast(P)


def fold_shift(nc, ident, shift, columns, rows, tag):
    with ExitStack() as ctx:
        m = Pool(nc, ctx, tag)
        spread_shift = m.sb("spread_shift", [P, DIM_TILES, P])
        ones = m.sb("ones", [P, P])
        n_cols = sum(bias.shape[1] for _, bias in columns)
        col = m.ps("col", [P, n_cols])
        row = [m.ps(f"row{n}", [P, DIM]) for n in range(len(rows))]
        s_ones, s_spread, s_product, s_added = m.sem("ones"), m.sem("spread"), m.sem("product"), m.sem("added")
        with nc.Block() as block:

            @block.vector
            def _(dve):
                nc.vector.memset(ones[:], 1.0).then_inc(s_ones, 1)
                dve.wait_ge(s_ones, 1)
                for k in range(DIM_TILES):
                    nc.vector.tensor_scalar(spread_shift[:, k, :], ones[:], shift[:, k:k + 1], None,
                                            ALU.mult).then_inc(s_spread, 1)
                dve.wait_ge(s_product, 1)
                at = 0
                for _, bias in columns:
                    w = bias.shape[1]
                    nc.vector.tensor_tensor(bias[:, :], bias[:, :], col[:, at:at + w], ALU.add).then_inc(s_added, 1)
                    at += w
                for n, (_, bias) in enumerate(rows):
                    nc.vector.tensor_tensor(bias[:], bias[:], row[n][:], ALU.add).then_inc(s_added, 1)
                dve.wait_ge(s_added, len(columns) + len(rows))

            @block.tensor
            def _(pe):
                at = 0
                for raw, bias in columns:
                    for j in range(bias.shape[1]):
                        for k in range(DIM_TILES):
                            op = nc.tensor.matmul(col[:, at:at + 1], raw[:, k, j * P:(j + 1) * P], shift[:, k:k + 1],
                                                  start=(k == 0), stop=(k == DIM_TILES - 1))
                        at += 1
                pe.wait_ge(s_spread, DIM_TILES)
                for n, (raw, _) in enumerate(rows):
                    for k in range(DIM_TILES):
                        op = nc.tensor.matmul(row[n][:], spread_shift[:, k, :], raw[:, k, :],
                                              start=(k == 0), stop=(k == DIM_TILES - 1))
                op.then_inc(s_product, 1)

        m.clear()


def tile_moments(nc, dve, source, stats, moments, s_stats, i, s_moments):
    nc.vector.bn_stats(stats, source).then_inc(s_stats, 1)
    dve.wait_ge(s_stats, i + 1)
    nc.vector.bn_aggr(moments, stats).then_inc(s_moments, 1)


def inverse_deviation(nc, pool, variance, exponent, s_shifted, i, s_deviation):
    nc.gpsimd.tensor_scalar(variance, variance, EPS, None, ALU.add).then_inc(s_shifted, 1)
    pool.wait_ge(s_shifted, i + 1)
    nc.gpsimd.tensor_tensor(variance, variance, exponent, ALU.pow).then_inc(s_deviation, 1)


def center_and_scale(nc, out, source, moments):
    return nc.vector.tensor_scalar(out, source, moments[:, 0:1], moments[:, 1:2], ALU.subtract, ALU.mult)


def fill(nc, tile, value, tag):
    with ExitStack() as ctx:
        m = Pool(nc, ctx, tag)
        s_filled = m.sem("filled")
        with nc.Block() as block:

            @block.gpsimd
            def _(pool):
                nc.gpsimd.memset(tile, value).then_inc(s_filled, 1)
                pool.wait_ge(s_filled, 1)

        m.clear()



ITEMS = TILES * HEADS
UNITS = ITEMS // GROUP
RING = 3
TURN_LAG = 2
VALUE_LAG = 6


def halves_on_act(n):
    return sum(on_act(i) for i in range(n))


def on_act(n):
    return n % 2 == 0 or n % 8 == 7


def multi_head_layer(nc, tag, x_dram, adj_dram, ident_dram, w, out_dram, pre_norm):
    scale = float(HEAD_DIM) ** -0.5
    with ExitStack() as ctx:
        m = Pool(nc, ctx, tag)
        ident = m.sb("ident", [P, P])
        names = ["q", "k", "v", "o"]
        high = {n: m.sb(f"w{n}_high", [P, DIM_TILES, DIM], F32R) for n in names}
        low = {n: m.sb(f"w{n}_low", [P, DIM_TILES, DIM], F32R) for n in names}
        bias_q, bias_k = m.sb("bias_q", [P, DIM_TILES]), m.sb("bias_k", [P, DIM_TILES])
        bias_v, bias_o = m.sb("bias_v", [P, DIM]), m.sb("bias_o", [P, DIM])
        if not pre_norm:
            gamma, beta = m.sb("gamma", [P, DIM]), m.sb("beta", [P, DIM])

        with ExitStack() as prep:
            t = Pool(nc, prep, tag + "_prep")
            raw = {n: t.sb(f"raw_{n}", [P, DIM_TILES, DIM]) for n in names}
            loads = [(raw[n][:], matrix(w["w" + n])) for n in names]
            loads += [(ident[:], ident_dram), (bias_q[:], column(w["bq"])), (bias_k[:], column(w["bk"])),
                      (bias_v[:], spread(w["bv"])), (bias_o[:], spread(w["bo"]))]
            gain = None
            if pre_norm:
                gain, shift = t.sb("gain", [P, DIM_TILES]), t.sb("shift", [P, DIM_TILES])
                loads += [(gain[:], column(w["g"])), (shift[:], column(w["b"]))]
            else:
                loads += [(gamma[:], spread(w["g"])), (beta[:], spread(w["b"]))]
            load_all(nc, loads, tag + "_load")
            if pre_norm:
                fold_shift(nc, ident, shift, [(raw["q"], bias_q), (raw["k"], bias_k)], [(raw["v"], bias_v)],
                           tag + "_fold")
            split_weights(nc, [(raw[n][:], high[n][:], low[n][:], -scale if n == "q" else 1.0,
                                gain if n != "o" else None) for n in names], tag + "_split")
            s_bias = t.sem("bias")
            with nc.Block() as block:

                @block.vector
                def _(dve):
                    nc.vector.tensor_scalar(bias_q[:], bias_q[:], -scale, None, ALU.mult).then_inc(s_bias, 1)
                    dve.wait_ge(s_bias, 1)

            t.clear()

        x_sb = m.sb("x", [P, TILES, DIM])
        adj_sb = m.sb("adj", [P, 2, SEQ], I32)
        penalty = m.sb("penalty", [P, 2, SEQ])
        q_stack = m.sb("q_stack", [P, HEADS, SEQ], F32R)
        k_stack = m.sb("k_stack", [P, HEADS, SEQ], F32R)
        values = m.sb("values", [P, TILES, DIM])
        row_sum = m.sb("row_sum", [P, TILES, HEADS])
        row_min = m.sb("row_min", [P, HEADS])
        exponent = m.sb("exponent", [P, 4])
        fill(nc, exponent[:], -0.5, tag + "_exponent")
        s_x, s_out = m.sem("x"), m.sem("out")
        s_adj = [m.sem(f"adj{i}") for i in range(2)]
        s_stack = [m.sem(f"stack{h}") for h in range(HEADS)]
        out_view = out_dram.rearrange("b (t p) d -> b p t d", p=P)

        with nc.Fori(0, BATCH) as b:
            x_view = of_batch(x_dram, b).rearrange("(t p) d -> p t d", p=P)
            adj_view = of_batch(adj_dram, b).rearrange("(t p) k -> p t k", p=P)
            y_view = of_batch(out_dram, b).rearrange("(t p) d -> p t d", p=P)

            with ExitStack() as scope:
                t = Pool(nc, scope, tag + "_proj")
                parts = {n: t.sb(n, [P, DIM_TILES, SEQ], F32R) for n in ("q_high", "q_low", "k_high", "k_low")}
                xt_high = t.sb("xt_high", [P, DIM_TILES, SEQ], F32R)
                xt_low = t.sb("xt_low", [P, DIM_TILES, SEQ], F32R)
                if pre_norm:
                    normed = t.sb("normed", [P, TILES, DIM])
                    stats = t.sb("stats", [P, TILES, STATS])
                    moments = t.sb("moments", [P, TILES, 2])
                else:
                    normed = x_sb
                turned = [t.ps(f"turned{i}", [P, BANK]) for i in range(4)]
                product = [t.ps(f"product{i}", [P, BANK]) for i in range(4)]
                s_stats, s_normed, s_moments = t.sem("stats"), t.sem("normed"), t.sem("moments")
                s_shifted, s_deviation = t.sem("shifted"), t.sem("deviation")
                s_turned, s_turned_high, s_turned_low = t.sem("turned"), t.sem("turned_high"), t.sem("turned_low")
                s_product, s_high, s_low, s_values = t.sem("product"), t.sem("high"), t.sem("low"), t.sem("values")
                blocks = [(side, d, n) for d in range(DIM_TILES) for side in "kq" for n in range(HALVES)]
                QK = len(blocks)
                VB = TILES * DIM // BANK

                with nc.Block() as block:

                    if pre_norm:
                        @block.gpsimd
                        def _(pool):
                            for n in range(HALVES):
                                pool.wait_ge(s_moments, 4 * n + 4)
                                inverse_deviation(nc, pool, moments[:, 4 * n:4 * n + 4, 1], exponent[:, 0:4],
                                                  s_shifted, n, s_deviation)

                    @block.sync
                    def _(sp):
                        sp.dma_start(x_sb[:], x_view).then_inc(s_x, 16)
                        for i in range(2):
                            sp.dma_start(adj_sb[:, i, :], adj_view[:, i, :]).then_inc(s_adj[i], 16)
                        for d in range(DIM_TILES):
                            for n, side in enumerate("kq"):
                                sp.wait_ge(s_high, HALVES * (2 * d + n + 1))
                                sp.wait_ge(s_low, HALVES * (2 * d + n + 1))
                                stack = k_stack if side == "k" else q_stack
                                order = ("high", "low", "high") if side == "k" else ("high", "high", "low")
                                for j in range(GROUP):
                                    rows = slice(j * HEAD_DIM, (j + 1) * HEAD_DIM)
                                    for s, part in enumerate(order):
                                        sp.dma_start(stack[s * HEAD_DIM:(s + 1) * HEAD_DIM, d * GROUP + j, :].bitcast(F32),
                                                     parts[f"{side}_{part}"][rows, d, :].bitcast(F32)
                                                     ).then_inc(s_stack[d * GROUP + j], 16)
                        for h in range(HEADS):
                            sp.wait_ge(s_stack[h], 16 * 6)

                    @block.vector
                    def _(dve):
                        dve.wait_ge(s_x, 16)
                        if pre_norm:
                            for i in range(TILES):
                                tile_moments(nc, dve, x_sb[:, i, :], stats[:, i, :], moments[:, i, :], s_stats, i,
                                             s_moments)
                            for i in range(TILES):
                                if i % 4 == 0:
                                    dve.wait_ge(s_deviation, i // 4 + 1)
                                center_and_scale(nc, normed[:, i, :], x_sb[:, i, :],
                                                 moments[:, i, :]).then_inc(s_normed, 1)
                        for i in range(DIM_TILES * HALVES):
                            d, n = i % DIM_TILES, i // DIM_TILES
                            dve.wait_ge(s_turned_high, i + 1)
                            cols = slice(n * BANK, (n + 1) * BANK)
                            nc.vector.tensor_tensor(xt_low[:, d, cols], turned[i][:], xt_high[:, d, cols].bitcast(F32),
                                                    ALU.subtract).then_inc(s_turned_low, 1)
                        for i, (side, d, n) in enumerate(blocks):
                            cols = slice(n * BANK, (n + 1) * BANK)
                            bias = bias_k if side == "k" else bias_q
                            dve.wait_ge(s_high, i + 1)
                            nc.vector.scalar_tensor_tensor(
                                parts[f"{side}_low"][:, d, cols], product[i % 4][:], bias[:, d:d + 1],
                                parts[f"{side}_high"][:, d, cols].bitcast(F32), ALU.add,
                                ALU.subtract).then_inc(s_low, 1)
                        for i in range(VB):
                            dve.wait_ge(s_product, QK + i + 1)
                            for j in range(BANK // DIM):
                                nc.vector.tensor_tensor(values[:, i * (BANK // DIM) + j, :],
                                                        product[(QK + i) % 4][:, j * DIM:(j + 1) * DIM], bias_v[:],
                                                        ALU.add).then_inc(s_values, 1)
                        dve.wait_ge(s_values, TILES)

                    @block.scalar
                    def _(act):
                        for i in range(DIM_TILES * HALVES):
                            d, n = i % DIM_TILES, i // DIM_TILES
                            act.wait_ge(s_turned, i + 1)
                            nc.scalar.copy(xt_high[:, d, n * BANK:(n + 1) * BANK], turned[i][:]
                                           ).then_inc(s_turned_high, 1)
                        for i, (side, d, n) in enumerate(blocks):
                            bias = bias_k if side == "k" else bias_q
                            act.wait_ge(s_product, i + 1)
                            nc.scalar.activation(parts[f"{side}_high"][:, d, n * BANK:(n + 1) * BANK],
                                                 product[i % 4][:], ACT.Identity,
                                                 bias=bias[:, d:d + 1]).then_inc(s_high, 1)

                    @block.tensor
                    def _(pe):
                        if not pre_norm:
                            pe.wait_ge(s_x, 16)
                        for i in range(DIM_TILES * HALVES):
                            d, n = i % DIM_TILES, i // DIM_TILES
                            if pre_norm:
                                pe.wait_ge(s_normed, 4 * n + 4)
                            for j in range(4):
                                op = nc.tensor.transpose(turned[i][:, j * P:(j + 1) * P],
                                                         normed[:, 4 * n + j, d * P:(d + 1) * P], ident[:])
                            op.then_inc(s_turned, 1)
                        for i, (side, d, n) in enumerate(blocks):
                            pe.wait_ge(s_turned_low, DIM_TILES * (n + 1) if i < HALVES else DIM_TILES * HALVES)
                            if i >= 4:
                                pe.wait_ge(s_low, i - 3)
                            cols = slice(n * BANK, (n + 1) * BANK)
                            for k in range(DIM_TILES):
                                op = split_matmul(nc, product[i % 4][:], high[side][:, k, d * P:(d + 1) * P],
                                                  low[side][:, k, d * P:(d + 1) * P], xt_high[:, k, cols],
                                                  xt_low[:, k, cols], k == 0, k == DIM_TILES - 1)
                            op.then_inc(s_product, 1)
                        for i in range(VB):
                            pe.wait_ge(s_low, QK + i - 3 if QK + i - 3 < QK else QK)
                            for j in range(BANK // DIM):
                                tile = i * (BANK // DIM) + j
                                for k in range(DIM_TILES):
                                    op = split_matmul(nc, product[(QK + i) % 4][:, j * DIM:(j + 1) * DIM],
                                                      xt_high[:, k, tile * P:(tile + 1) * P],
                                                      xt_low[:, k, tile * P:(tile + 1) * P],
                                                      high["v"][:, k, :], low["v"][:, k, :],
                                                      k == 0, k == DIM_TILES - 1)
                            op.then_inc(s_product, 1)

                sems_proj = t.sems
                for s in sems_proj:
                    nc.gpsimd.sem_clear(s)

            with ExitStack() as scope:
                t = Pool(nc, scope, tag + "_attn")
                probs = t.sb("probs", [P, RING, SEQ])
                probs_t = t.sb("probs_t", [P, 2, TILES, GROUP, P])
                inverse = t.sb("inverse", [P, GROUPS, TILES, P])
                heads_t = t.sb("heads_t", [P, GROUPS, SEQ])
                edge = t.sb("edge", [P, 2, SEQ]) if pre_norm else None
                inner = ExitStack()
                tp = Pool(nc, inner, tag + "_attn_ps")
                scores = [tp.ps(f"scores{i}", [P, SEQ]) for i in range(2)]
                turned = [tp.ps(f"turned{i}", [P, BANK]) for i in range(2)]
                summed = [tp.ps(f"summed{i}", [P, P]) for i in range(2)]
                s_penalty, s_pool = t.sem("penalty"), t.sem("pool")
                s_scores, s_min, s_probs = t.sem("scores"), t.sem("min"), t.sem("probs")
                s_turned, s_copied_act, s_copied_dve = t.sem("turned"), t.sem("copied_act"), t.sem("copied_dve")
                s_summed, s_heads, s_inverse, s_residual = (t.sem("summed"), t.sem("heads"), t.sem("inverse"),
                                                            t.sem("residual"))

                with nc.Block() as block:

                    @block.sync
                    def _(sp):
                        for i in range(2, TILES):
                            sp.wait_ge(s_penalty, i - 1)
                            sp.dma_start(adj_sb[:, i % 2, :], adj_view[:, i, :]).then_inc(s_adj[i % 2], 16)

                    @block.gpsimd
                    def _(pool):
                        for i in range(TILES):
                            pool.wait_ge(s_adj[i % 2], 16 * (i // 2 + 1))
                            if i >= 2:
                                pool.wait_ge(s_min, HEADS * (i - 1))
                            adj = adj_sb[:, i % 2, :]
                            if pre_norm:
                                value, bonus = edge[:, 0, :], edge[:, 1, :]
                                nc.gpsimd.tensor_scalar(value, adj, 1.0, None, ALU.mult).then_inc(s_pool, 1)
                                pool.wait_ge(s_pool, 4 * i + 1)
                                nc.gpsimd.tensor_scalar(bonus, value, -0.1, None, ALU.mult).then_inc(s_pool, 1)
                                pool.wait_ge(s_pool, 4 * i + 2)
                                nc.gpsimd.tensor_tensor(bonus, bonus, value, ALU.mult).then_inc(s_pool, 1)
                                nc.gpsimd.tensor_scalar(penalty[:, i % 2, :], value, 0.0, PENALTY, ALU.is_le,
                                                        ALU.mult).then_inc(s_pool, 1)
                                pool.wait_ge(s_pool, 4 * i + 4)
                                nc.gpsimd.tensor_tensor(penalty[:, i % 2, :], penalty[:, i % 2, :], bonus,
                                                        ALU.add).then_inc(s_penalty, 1)
                                pool.wait_ge(s_penalty, i + 1)
                            else:
                                nc.gpsimd.tensor_scalar(penalty[:, i % 2, :], adj, 0.0, PENALTY, ALU.is_equal,
                                                        ALU.mult).then_inc(s_penalty, 1)
                        for i in range(TILES):
                            nc.gpsimd.tensor_tensor(x_sb[:, i, :], x_sb[:, i, :], bias_o[:],
                                                    ALU.add).then_inc(s_residual, 1)
                        pool.wait_ge(s_residual, TILES)

                    @block.tensor
                    def _(pe):
                        for step in range(ITEMS + VALUE_LAG + GROUP):
                            if step < ITEMS:
                                tile, head = step // HEADS, step % HEADS
                                if step >= 2:
                                    pe.wait_ge(s_min, step - 1)
                                for n in range(HALVES):
                                    op = nc.tensor.matmul(scores[step % 2][:, n * BANK:(n + 1) * BANK],
                                                          q_stack[0:STACK, head, tile * P:(tile + 1) * P],
                                                          k_stack[0:STACK, head, n * BANK:(n + 1) * BANK],
                                                          start=True, stop=True)
                                op.then_inc(s_scores, 1)
                            item = step - TURN_LAG
                            if 0 <= item < ITEMS:
                                pe.wait_ge(s_probs, item + 1)
                                for half in range(2):
                                    n = 2 * item + half
                                    if n >= 2:
                                        if on_act(n - 2):
                                            pe.wait_ge(s_copied_act, halves_on_act(n - 1))
                                        else:
                                            pe.wait_ge(s_copied_dve, n - 1 - halves_on_act(n - 1))
                                    for j in range(4):
                                        k = 4 * half + j
                                        op = nc.tensor.transpose(turned[n % 2][:, j * P:(j + 1) * P],
                                                                 probs[:, item % RING, k * P:(k + 1) * P], ident[:])
                                    op.then_inc(s_turned, 1)
                            unit, part = divmod(step - VALUE_LAG, GROUP)
                            if 0 <= unit < UNITS:
                                if part == 0:
                                    n = 2 * GROUP * (unit + 1)
                                    pe.wait_ge(s_copied_act, halves_on_act(n))
                                    pe.wait_ge(s_copied_dve, n - halves_on_act(n))
                                    if unit >= 2:
                                        pe.wait_ge(s_heads, unit - 1)
                                for k in (2 * part, 2 * part + 1):
                                    for j in range(GROUP):
                                        head = unit % GROUPS * GROUP + j
                                        op = nc.tensor.matmul(summed[unit % 2][j * HEAD_DIM:(j + 1) * HEAD_DIM, :],
                                                              values[:, k, head * HEAD_DIM:(head + 1) * HEAD_DIM],
                                                              probs_t[:, unit % 2, k, j, :],
                                                              start=(k == 0), stop=(k == TILES - 1))
                                if part == GROUP - 1:
                                    op.then_inc(s_summed, 1)

                    def copy_half(eng, copy, n, sem):
                        item, half = n // 2, n % 2
                        unit = item // GROUP
                        eng.wait_ge(s_turned, n + 1)
                        if unit >= 2:
                            eng.wait_ge(s_summed, unit - 1)
                        copy(probs_t[:, unit % 2, 4 * half:4 * half + 4, item % GROUP, :],
                             turned[n % 2][:].rearrange("p (k q) -> p k q", q=P)).then_inc(sem, 1)

                    @block.vector
                    def _(dve):
                        for step in range(ITEMS + TURN_LAG):
                            if step < ITEMS:
                                tile, head = step // HEADS, step % HEADS
                                dve.wait_ge(s_scores, step + 1)
                                if head == 0:
                                    dve.wait_ge(s_penalty, tile + 1)
                                if step >= RING:
                                    dve.wait_ge(s_turned, 2 * (step - RING + 1))
                                nc.vector.tensor_tensor_reduce(
                                    out=probs[:, step % RING, :], in0=scores[step % 2][:],
                                    in1=penalty[:, tile % 2, :], scale=1.0, scalar=3.0e38, op0=ALU.add, op1=ALU.min,
                                    accum_out=row_min[:, head:head + 1]).then_inc(s_min, 1)
                            item = step - TURN_LAG
                            if item >= 0:
                                for n in (2 * item, 2 * item + 1):
                                    if not on_act(n):
                                        copy_half(dve, nc.vector.tensor_copy, n, s_copied_dve)
                            if item >= 0 and item % HEADS == HEADS - 1:
                                tile = item // HEADS
                                dve.wait_ge(s_probs, item + 1)
                                nc.vector.reciprocal(
                                    inverse[:, :, tile, :].rearrange("p g (h d) -> p g h d", d=HEAD_DIM),
                                    row_sum[:, tile, :].rearrange("p (g h) -> p g h", h=GROUP).unsqueeze(3)
                                    .to_broadcast([P, GROUPS, GROUP, HEAD_DIM])).then_inc(s_inverse, 1)
                        dve.wait_ge(s_inverse, TILES)

                    @block.scalar
                    def _(act):
                        for step in range(ITEMS + VALUE_LAG + GROUP):
                            item = step - 1
                            if 0 <= item < ITEMS:
                                tile, head = item // HEADS, item % HEADS
                                act.wait_ge(s_min, item + 1)
                                nc.scalar.activation(probs[:, item % RING, :], probs[:, item % RING, :], ACT.Exp,
                                                     bias=row_min[:, head:head + 1], scale=-1.0,
                                                     accum_out=row_sum[:, tile, head:head + 1]).then_inc(s_probs, 1)
                            item = step - TURN_LAG
                            if 0 <= item < ITEMS:
                                for n in (2 * item, 2 * item + 1):
                                    if on_act(n):
                                        copy_half(act, nc.scalar.copy, n, s_copied_act)
                            unit, part = divmod(step - VALUE_LAG, GROUP)
                            if 0 <= unit < UNITS and part == GROUP - 1:
                                act.wait_ge(s_summed, unit + 1)
                                tile, g = divmod(unit, GROUPS)
                                nc.scalar.copy(heads_t[:, g, tile * P:(tile + 1) * P],
                                               summed[unit % 2][:]).then_inc(s_heads, 1)
                        act.wait_ge(s_heads, UNITS)

                inner.close()
                for s in t.sems:
                    nc.gpsimd.sem_clear(s)

                o = Pool(nc, scope, tag + "_outp")
                heads_high = o.sb("heads_high", [P, GROUPS, SEQ], F32R)
                heads_low = o.sb("heads_low", [P, GROUPS, SEQ], F32R)
                result = o.sb("result", [P, TILES, DIM])
                stats = o.sb("stats", [P, TILES, STATS])
                moments = o.sb("moments", [P, TILES, 2])
                factor = [o.ps(f"factor{i}", [P, BANK]) for i in range(4)]
                projected = [o.ps(f"projected{i}", [P, DIM]) for i in range(4)]
                s_factor, s_scaled, s_high, s_low = o.sem("factor"), o.sem("scaled"), o.sem("high"), o.sem("low")
                s_projected, s_sum, s_normed = o.sem("projected"), o.sem("sum"), o.sem("normed")
                s_stats, s_moments, s_shifted, s_deviation = (o.sem("stats"), o.sem("moments"), o.sem("shifted"),
                                                              o.sem("deviation"))
                s_gained, s_result = o.sem("gained"), o.sem("result")
                quads = [(g, n) for n in range(HALVES) for g in range(GROUPS)]

                with nc.Block() as block:

                    @block.tensor
                    def _(pe):
                        for i, (g, n) in enumerate(quads):
                            for j in range(4):
                                op = nc.tensor.transpose(factor[i][:, j * P:(j + 1) * P], inverse[:, g, 4 * n + j, :],
                                                         ident[:])
                            op.then_inc(s_factor, 1)
                        for i in range(TILES):
                            pe.wait_ge(s_low, GROUPS * (i // 4 + 1))
                            if i >= 4:
                                pe.wait_ge(s_sum, i - 3)
                            for g in range(GROUPS):
                                op = split_matmul(nc, projected[i % 4][:], heads_high[:, g, i * P:(i + 1) * P],
                                                  heads_low[:, g, i * P:(i + 1) * P], high["o"][:, g, :],
                                                  low["o"][:, g, :], g == 0, g == GROUPS - 1)
                            op.then_inc(s_projected, 1)

                    @block.scalar
                    def _(act):
                        for i, (g, n) in enumerate(quads):
                            cols = slice(n * BANK, (n + 1) * BANK)
                            act.wait_ge(s_scaled, i + 1)
                            nc.scalar.copy(heads_high[:, g, cols], heads_t[:, g, cols]).then_inc(s_high, 1)

                    @block.vector
                    def _(dve):
                        for i, (g, n) in enumerate(quads):
                            cols = slice(n * BANK, (n + 1) * BANK)
                            dve.wait_ge(s_factor, i + 1)
                            nc.vector.tensor_tensor(heads_t[:, g, cols], heads_t[:, g, cols], factor[i][:],
                                                    ALU.mult).then_inc(s_scaled, 1)
                        for i, (g, n) in enumerate(quads):
                            cols = slice(n * BANK, (n + 1) * BANK)
                            dve.wait_ge(s_scaled, i + 1)
                            dve.wait_ge(s_high, i + 1)
                            nc.vector.tensor_tensor(heads_low[:, g, cols], heads_t[:, g, cols],
                                                    heads_high[:, g, cols].bitcast(F32),
                                                    ALU.subtract).then_inc(s_low, 1)
                        for step in range(TILES + 2):
                            if step < TILES:
                                i = step
                                dve.wait_ge(s_projected, i + 1)
                                nc.vector.tensor_tensor(result[:, i, :], projected[i % 4][:], x_sb[:, i, :],
                                                        ALU.add).then_inc(s_sum, 1)
                                if not pre_norm:
                                    dve.wait_ge(s_sum, i + 1)
                                    tile_moments(nc, dve, result[:, i, :], stats[:, i, :], moments[:, i, :], s_stats,
                                                 i, s_moments)
                            if not pre_norm and step >= 2:
                                i = step - 2
                                dve.wait_ge(s_deviation, i + 1)
                                center_and_scale(nc, result[:, i, :], result[:, i, :],
                                                 moments[:, i, :]).then_inc(s_normed, 1)

                    @block.gpsimd
                    def _(pool):
                        if not pre_norm:
                            for step in range(TILES + 2):
                                if step < TILES:
                                    pool.wait_ge(s_moments, step + 1)
                                    inverse_deviation(nc, pool, moments[:, step, 1:2], exponent[:, 0:1], s_shifted,
                                                      step, s_deviation)
                                i = step - 2
                                if i < 0:
                                    continue
                                pool.wait_ge(s_normed, i + 1)
                                nc.gpsimd.tensor_tensor(result[:, i, :], result[:, i, :], gamma[:],
                                                        ALU.mult).then_inc(s_gained, 1)
                                pool.wait_ge(s_gained, i + 1)
                                nc.gpsimd.tensor_tensor(result[:, i, :], result[:, i, :], beta[:],
                                                        ALU.add).then_inc(s_result, 1)

                    @block.sync
                    def _(sp):
                        for i in range(TILES):
                            sp.wait_ge(s_sum if pre_norm else s_result, i + 1)
                            sp.dma_start(y_view[:, i, :], result[:, i, :]).then_inc(s_out, 16)
                        sp.wait_ge(s_out, 16 * TILES)

                for s in o.sems:
                    nc.gpsimd.sem_clear(s)
            m.clear()



def mlp_layer(nc, tag, x_dram, ident_dram, w, out_dram):
    hid_tiles = HIDDEN // P
    with ExitStack() as ctx:
        m = Pool(nc, ctx, tag)
        ident = m.sb("ident", [P, P])
        w1_high, w1_low = (m.sb(f"w1_{s}", [P, DIM_TILES, HIDDEN], F32R) for s in ("high", "low"))
        w2_high, w2_low = (m.sb(f"w2_{s}", [P, hid_tiles, DIM], F32R) for s in ("high", "low"))
        bias_1, bias_2 = m.sb("bias_1", [P, hid_tiles]), m.sb("bias_2", [P, DIM])
        with ExitStack() as prep:
            t = Pool(nc, prep, tag + "_prep")
            raw_1, raw_2 = t.sb("raw_1", [P, DIM_TILES, HIDDEN]), t.sb("raw_2", [P, hid_tiles, DIM])
            gain, shift = t.sb("gain", [P, DIM_TILES]), t.sb("shift", [P, DIM_TILES])
            load_all(nc, [(raw_1[:], matrix(w["w1"])), (raw_2[:], matrix(w["w2"])), (gain[:], column(w["g"])),
                          (shift[:], column(w["b"])), (bias_1[:], column(w["b1"])), (bias_2[:], spread(w["b2"])),
                          (ident[:], ident_dram)], tag + "_load")
            fold_shift(nc, ident, shift, [(raw_1, bias_1)], [], tag + "_fold")
            split_weights(nc, [(raw_1[:], w1_high[:], w1_low[:], 1.0, gain),
                               (raw_2[:], w2_high[:], w2_low[:], 1.0, None)], tag + "_split")

        x_sb = m.sb("x", [P, TILES, DIM])
        normed = m.sb("normed", [P, TILES, DIM])
        result = m.sb("result", [P, TILES, DIM])
        stats, moments = m.sb("stats", [P, TILES, STATS]), m.sb("moments", [P, TILES, 2])
        xt_high, xt_low = (m.sb(f"xt_{s}", [P, DIM_TILES, SEQ], F32R) for s in ("high", "low"))
        act_full = m.sb("act_full", [P, 2, BANK])
        act_high, act_low = (m.sb(f"act_{s}", [P, hid_tiles, BANK], F32R) for s in ("high", "low"))
        turned = [m.ps(f"turned{i}", [P, BANK]) for i in range(2)]
        hidden = [m.ps(f"hidden{i}", [P, BANK]) for i in range(3)]
        projected = [m.ps(f"projected{i}", [P, DIM]) for i in range(3)]
        exponent = m.sb("exponent", [P, 4])
        fill(nc, exponent[:], -0.5, tag + "_exponent")
        s_x, s_stats, s_normed, s_moments = m.sem("x"), m.sem("stats"), m.sem("normed"), m.sem("moments")
        s_shifted, s_deviation = m.sem("shifted"), m.sem("deviation")
        s_turned, s_turned_high, s_turned_low = m.sem("turned"), m.sem("turned_high"), m.sem("turned_low")
        s_hidden, s_gelu, s_high, s_low = m.sem("hidden"), m.sem("gelu"), m.sem("high"), m.sem("low")
        s_projected, s_sum, s_out, s_residual = m.sem("projected"), m.sem("sum"), m.sem("out"), m.sem("residual")

        with nc.Fori(0, BATCH) as b:
            x_view = of_batch(x_dram, b).rearrange("(t p) d -> p t d", p=P)
            y_view = of_batch(out_dram, b).rearrange("(t p) d -> p t d", p=P)
            with nc.Block() as block:

                @block.sync
                def _(sp):
                    sp.dma_start(x_sb[:], x_view).then_inc(s_x, 16)
                    for i in range(TILES):
                        sp.wait_ge(s_sum, i + 1)
                        sp.dma_start(y_view[:, i, :], result[:, i, :]).then_inc(s_out, 16)
                    sp.wait_ge(s_out, 16 * TILES)

                @block.gpsimd
                def _(pool):
                    for n in range(HALVES):
                        pool.wait_ge(s_moments, 4 * n + 4)
                        inverse_deviation(nc, pool, moments[:, 4 * n:4 * n + 4, 1], exponent[:], s_shifted, n,
                                          s_deviation)
                    for i in range(TILES):
                        pool.wait_ge(s_normed, i + 1)
                        nc.gpsimd.tensor_tensor(x_sb[:, i, :], x_sb[:, i, :], bias_2[:],
                                                ALU.add).then_inc(s_residual, 1)

                @block.tensor
                def _(pe):
                    for i in range(DIM_TILES * HALVES):
                        d, n = i % DIM_TILES, i // DIM_TILES
                        pe.wait_ge(s_normed, 4 * n + 4)
                        if i >= 2:
                            pe.wait_ge(s_turned_low, i - 1)
                        for j in range(4):
                            op = nc.tensor.transpose(turned[i % 2][:, j * P:(j + 1) * P],
                                                     normed[:, 4 * n + j, d * P:(d + 1) * P], ident[:])
                        op.then_inc(s_turned, 1)
                    for n in range(HALVES):
                        cols = slice(n * BANK, (n + 1) * BANK)
                        pe.wait_ge(s_turned_low, DIM_TILES * (n + 1))
                        for f in range(hid_tiles):
                            i = n * hid_tiles + f
                            if i >= 3:
                                pe.wait_ge(s_gelu, i - 2)
                            for k in range(DIM_TILES):
                                op = split_matmul(nc, hidden[i % 3][:], w1_high[:, k, f * P:(f + 1) * P],
                                                  w1_low[:, k, f * P:(f + 1) * P], xt_high[:, k, cols],
                                                  xt_low[:, k, cols], k == 0, k == DIM_TILES - 1)
                            op.then_inc(s_hidden, 1)
                        for j in range(BANK // P):
                            i = n * (BANK // P) + j
                            if i >= 3:
                                pe.wait_ge(s_sum, i - 2)
                            for f in range(hid_tiles):
                                if j == 0:
                                    pe.wait_ge(s_low, n * hid_tiles + f + 1)
                                op = split_matmul(nc, projected[i % 3][:], act_high[:, f, j * P:(j + 1) * P],
                                                  act_low[:, f, j * P:(j + 1) * P], w2_high[:, f, :],
                                                  w2_low[:, f, :], f == 0, f == hid_tiles - 1)
                            op.then_inc(s_projected, 1)

                @block.scalar
                def _(act):
                    for i in range(DIM_TILES * HALVES):
                        d, n = i % DIM_TILES, i // DIM_TILES
                        act.wait_ge(s_turned, i + 1)
                        nc.scalar.copy(xt_high[:, d, n * BANK:(n + 1) * BANK], turned[i % 2][:]
                                       ).then_inc(s_turned_high, 1)
                    for i in range(HALVES * hid_tiles):
                        act.wait_ge(s_hidden, i + 1)
                        if i >= 2:
                            act.wait_ge(s_low, i - 1)
                        f = i % hid_tiles
                        nc.scalar.activation(act_full[:, i % 2, :], hidden[i % 3][:], ACT.Gelu,
                                             bias=bias_1[:, f:f + 1]).then_inc(s_gelu, 1)

                @block.vector
                def _(dve):
                    dve.wait_ge(s_x, 16)
                    for i in range(TILES):
                        tile_moments(nc, dve, x_sb[:, i, :], stats[:, i, :], moments[:, i, :], s_stats, i,
                                     s_moments)
                    for i in range(TILES):
                        if i % 4 == 0:
                            dve.wait_ge(s_deviation, i // 4 + 1)
                        center_and_scale(nc, normed[:, i, :], x_sb[:, i, :],
                                         moments[:, i, :]).then_inc(s_normed, 1)
                    for i in range(DIM_TILES * HALVES):
                        d, n = i % DIM_TILES, i // DIM_TILES
                        dve.wait_ge(s_turned_high, i + 1)
                        cols = slice(n * BANK, (n + 1) * BANK)
                        nc.vector.tensor_tensor(xt_low[:, d, cols], turned[i % 2][:], xt_high[:, d, cols].bitcast(F32),
                                                ALU.subtract).then_inc(s_turned_low, 1)
                    for n in range(HALVES):
                        for f in range(hid_tiles):
                            i = n * hid_tiles + f
                            dve.wait_ge(s_gelu, i + 1)
                            if n and f == 0:
                                dve.wait_ge(s_projected, BANK // P)
                            nc.vector.tensor_copy(act_high[:, f, :], act_full[:, i % 2, :]).then_inc(s_high, 1)
                            dve.wait_ge(s_high, i + 1)
                            nc.vector.tensor_tensor(act_low[:, f, :], act_full[:, i % 2, :],
                                                    act_high[:, f, :].bitcast(F32), ALU.subtract).then_inc(s_low, 1)
                        for j in range(BANK // P):
                            i = n * (BANK // P) + j
                            dve.wait_ge(s_projected, i + 1)
                            dve.wait_ge(s_residual, i + 1)
                            nc.vector.tensor_tensor(result[:, i, :], projected[i % 3][:], x_sb[:, i, :],
                                                    ALU.add).then_inc(s_sum, 1)

            m.clear()



def single_head_layer(nc, tag, x_dram, adj_dram, ident_dram, w, out_dram):
    scale = float(DIM) ** -0.5
    with ExitStack() as ctx:
        m = Pool(nc, ctx, tag)
        ident = m.sb("ident", [P, P])
        qk_high, qk_low, vo_high, vo_low = (m.sb(n, [P, DIM_TILES, DIM], F32R)
                                            for n in ("qk_high", "qk_low", "vo_high", "vo_low"))
        bias_o, gamma, beta = m.sb("bias_o", [P, DIM]), m.sb("gamma", [P, DIM]), m.sb("beta", [P, DIM])
        with ExitStack() as prep:
            t = Pool(nc, prep, tag + "_prep")
            wq_t, wk_t, wv_t, wo = (t.sb(n, [P, DIM_TILES, DIM]) for n in ("wq_t", "wk_t", "wv_t", "wo"))
            raw_qk, raw_vo = t.sb("raw_qk", [P, DIM_TILES, DIM]), t.sb("raw_vo", [P, DIM_TILES, DIM])
            load_all(nc, [(wq_t[:], matrix(w["wq_t"])), (wk_t[:], matrix(w["wk_t"])), (wv_t[:], matrix(w["wv_t"])),
                          (wo[:], matrix(w["wo"])), (bias_o[:], spread(w["bo"])), (gamma[:], spread(w["g"])),
                          (beta[:], spread(w["b"])), (ident[:], ident_dram)], tag + "_load")
            product = [t.ps(f"product{i}", [P, DIM]) for i in range(4)]
            s_product, s_copied = t.sem("product"), t.sem("copied")
            with nc.Block() as block:

                @block.tensor
                def _(pe):
                    for i, (left, right) in enumerate(((wq_t, wk_t), (wv_t, wo))):
                        for r in range(DIM_TILES):
                            for k in range(DIM_TILES):
                                op = nc.tensor.matmul(product[2 * i + r][:], left[:, k, r * P:(r + 1) * P],
                                                      right[:, k, :], start=(k == 0), stop=(k == DIM_TILES - 1))
                            op.then_inc(s_product, 1)

                @block.vector
                def _(dve):
                    for i, raw in enumerate((raw_qk, raw_vo)):
                        for r in range(DIM_TILES):
                            dve.wait_ge(s_product, 2 * i + r + 1)
                            nc.vector.tensor_copy(raw[:, r, :], product[2 * i + r][:]).then_inc(s_copied, 1)
                    dve.wait_ge(s_copied, 4)

            t.clear()
            split_weights(nc, [(raw_qk[:], qk_high[:], qk_low[:], -scale, None),
                               (raw_vo[:], vo_high[:], vo_low[:], 1.0, None)], tag + "_split")

        x_sb = m.sb("x", [P, TILES, DIM])
        adj_sb = m.sb("adj", [P, 2, SEQ], I32)
        penalty = m.sb("penalty", [P, 2, SEQ])
        xt_high, xt_low, q_high, q_low = (m.sb(n, [P, DIM_TILES, SEQ], F32R)
                                          for n in ("xt_high", "xt_low", "q_high", "q_low"))
        v_high, v_low = (m.sb(n, [P, TILES, DIM], F32R) for n in ("v_high", "v_low"))
        probs = m.sb("probs", [P, 3, SEQ])
        probs_t_high, probs_t_low = (m.sb(n, [P, 2, TILES, P], F32R) for n in ("probs_t_high", "probs_t_low"))
        row_min, row_sum, inverse = (m.sb(n, [P, TILES]) for n in ("row_min", "row_sum", "inverse"))
        result = m.sb("result", [P, TILES, DIM])
        stats, moments = m.sb("stats", [P, TILES, STATS]), m.sb("moments", [P, TILES, 2])
        bank = [m.ps(f"bank{i}", [P, BANK]) for i in range(4)]
        turned = [m.ps(f"turned{i}", [P, BANK]) for i in range(2)]
        summed = [m.ps(f"summed{i}", [P, DIM]) for i in range(2)]
        s_x, s_out, s_residual = m.sem("x"), m.sem("out"), m.sem("residual")
        s_adj = [m.sem(f"adj{i}") for i in range(2)]
        s_penalty = m.sem("penalty")
        s_xt, s_xt_high, s_xt_low = m.sem("xt"), m.sem("xt_high"), m.sem("xt_low")
        s_product, s_high, s_low = m.sem("product"), m.sem("high"), m.sem("low")
        s_scores, s_min, s_probs = m.sem("scores"), m.sem("min"), m.sem("probs")
        s_turned, s_turned_high, s_turned_low = m.sem("turned"), m.sem("turned_high"), m.sem("turned_low")
        exponent = m.sb("exponent", [P, 1])
        fill(nc, exponent[:], -0.5, tag + "_exponent")
        s_inverse, s_summed, s_sum, s_normed = m.sem("inverse"), m.sem("summed"), m.sem("sum"), m.sem("normed")
        s_first_min = m.sem("first_min")
        s_stats, s_moments, s_shifted, s_deviation = (m.sem("stats"), m.sem("moments"), m.sem("shifted"),
                                                      m.sem("deviation"))
        s_gained, s_result = m.sem("gained"), m.sem("result")
        XT = DIM_TILES * HALVES
        QB = DIM_TILES * HALVES
        VB = TILES * DIM // BANK
        PB = QB + VB

        with nc.Fori(0, BATCH) as b:
            x_view = of_batch(x_dram, b).rearrange("(t p) d -> p t d", p=P)
            adj_view = of_batch(adj_dram, b).rearrange("(t p) k -> p t k", p=P)
            y_view = of_batch(out_dram, b).rearrange("(t p) d -> p t d", p=P)
            with nc.Block() as block:

                @block.sync
                def _(sp):
                    sp.dma_start(x_sb[:], x_view).then_inc(s_x, 16)
                    for i in range(TILES):
                        if i >= 2:
                            sp.wait_ge(s_penalty, i - 1)
                        sp.dma_start(adj_sb[:, i % 2, :], adj_view[:, i, :]).then_inc(s_adj[i % 2], 16)
                    for i in range(TILES):
                        sp.wait_ge(s_result, i + 1)
                        sp.dma_start(y_view[:, i, :], result[:, i, :]).then_inc(s_out, 16)
                    sp.wait_ge(s_out, 16 * TILES)

                @block.gpsimd
                def _(pool):
                    def deviation(i):
                        pool.wait_ge(s_moments, i + 1)
                        inverse_deviation(nc, pool, moments[:, i, 1:2], exponent[:], s_shifted, i, s_deviation)

                    def gain_and_shift(i):
                        pool.wait_ge(s_normed, i + 1)
                        nc.gpsimd.tensor_tensor(result[:, i, :], result[:, i, :], gamma[:],
                                                ALU.mult).then_inc(s_gained, 1)
                        pool.wait_ge(s_gained, i + 1)
                        nc.gpsimd.tensor_tensor(result[:, i, :], result[:, i, :], beta[:],
                                                ALU.add).then_inc(s_result, 1)

                    for i in range(TILES):
                        pool.wait_ge(s_adj[i % 2], 16 * (i // 2 + 1))
                        if i >= 2:
                            pool.wait_ge(s_min, i - 1)
                        nc.gpsimd.tensor_scalar(penalty[:, i % 2, :], adj_sb[:, i % 2, :], 0.0, PENALTY,
                                                ALU.is_equal, ALU.mult).then_inc(s_penalty, 1)
                        if i == 1:
                            pool.wait_ge(s_xt, XT)
                            for j in range(TILES):
                                nc.gpsimd.tensor_tensor(x_sb[:, j, :], x_sb[:, j, :], bias_o[:],
                                                        ALU.add).then_inc(s_residual, 1)
                        if i >= 4:
                            deviation(i - 4)
                        if i >= 5:
                            gain_and_shift(i - 5)
                    for i in range(TILES, TILES + 5):
                        if i - 4 < TILES:
                            deviation(i - 4)
                        gain_and_shift(i - 5)

                @block.tensor
                def _(pe):
                    pe.wait_ge(s_x, 16)
                    for i in range(XT):
                        d, n = i % DIM_TILES, i // DIM_TILES
                        for j in range(4):
                            op = nc.tensor.transpose(bank[i][:, j * P:(j + 1) * P],
                                                     x_sb[:, 4 * n + j, d * P:(d + 1) * P], ident[:])
                        op.then_inc(s_xt, 1)
                    for i in range(PB):
                        pe.wait_ge(s_xt_low, min(XT, i + 1) if i >= 2 else DIM_TILES)
                        if i >= 4:
                            pe.wait_ge(s_low, i - 3)
                        if i < QB:
                            d, n = i % DIM_TILES, i // DIM_TILES
                            cols = slice(n * BANK, (n + 1) * BANK)
                            if n:
                                pe.wait_ge(s_xt_low, XT)
                            for k in range(DIM_TILES):
                                op = split_matmul(nc, bank[i % 4][:], qk_high[:, k, d * P:(d + 1) * P],
                                                  qk_low[:, k, d * P:(d + 1) * P], xt_high[:, k, cols],
                                                  xt_low[:, k, cols], k == 0, k == DIM_TILES - 1)
                        else:
                            for j in range(BANK // DIM):
                                tile = (i - QB) * (BANK // DIM) + j
                                for k in range(DIM_TILES):
                                    op = split_matmul(nc, bank[i % 4][:, j * DIM:(j + 1) * DIM],
                                                      xt_high[:, k, tile * P:(tile + 1) * P],
                                                      xt_low[:, k, tile * P:(tile + 1) * P],
                                                      vo_high[:, k, :], vo_low[:, k, :], k == 0, k == DIM_TILES - 1)
                        op.then_inc(s_product, 1)

                    def score(i):
                        if i < 2:
                            pe.wait_ge(s_low, PB - 2 + 2 * i if i == 0 else PB)
                        else:
                            pe.wait_ge(s_min, i - 1)
                        for n in range(HALVES):
                            out = bank[2 * (i % 2) + n][:]
                            for k in range(DIM_TILES):
                                op = split_matmul(nc, out, q_high[:, k, i * P:(i + 1) * P],
                                                  q_low[:, k, i * P:(i + 1) * P],
                                                  xt_high[:, k, n * BANK:(n + 1) * BANK],
                                                  xt_low[:, k, n * BANK:(n + 1) * BANK], k == 0, k == DIM_TILES - 1)
                        op.then_inc(s_scores, 1)

                    def turn(i):
                        pe.wait_ge(s_probs, i + 1)
                        for half in range(2):
                            n = 2 * i + half
                            if n >= 2:
                                pe.wait_ge(s_turned_low, n - 1)
                            for j in range(4):
                                k = 4 * half + j
                                op = nc.tensor.transpose(turned[n % 2][:, j * P:(j + 1) * P],
                                                         probs[:, i % 3, k * P:(k + 1) * P], ident[:])
                            op.then_inc(s_turned, 1)

                    def weigh(i):
                        if i >= 2:
                            pe.wait_ge(s_sum, i - 1)
                        for k in range(TILES):
                            if k % 4 == 0:
                                pe.wait_ge(s_turned_low, 2 * i + k // 4 + 1)
                            op = split_matmul(nc, summed[i % 2][:], probs_t_high[:, i % 2, k, :],
                                              probs_t_low[:, i % 2, k, :], v_high[:, k, :], v_low[:, k, :],
                                              k == 0, k == TILES - 1)
                        op.then_inc(s_summed, 1)

                    for step in range(TILES + 2):
                        if step < TILES:
                            score(step)
                        if 1 <= step <= TILES:
                            turn(step - 1)
                        if step >= 2:
                            weigh(step - 2)

                @block.scalar
                def _(act):
                    for i in range(XT):
                        d, n = i % DIM_TILES, i // DIM_TILES
                        act.wait_ge(s_xt, i + 1)
                        nc.scalar.copy(xt_high[:, d, n * BANK:(n + 1) * BANK], bank[i][:]).then_inc(s_xt_high, 1)
                    for i in range(PB):
                        act.wait_ge(s_product, i + 1)
                        if i < QB:
                            d, n = i % DIM_TILES, i // DIM_TILES
                            to = q_high[:, d, n * BANK:(n + 1) * BANK]
                        else:
                            to = v_high[:, 2 * (i - QB):2 * (i - QB) + 2, :].rearrange("p t d -> p (t d)")
                        nc.scalar.copy(to, bank[i % 4][:]).then_inc(s_high, 1)
                    for step in range(TILES + 1):
                        if step < TILES:
                            act.wait_ge(s_min, step + 1)
                            nc.scalar.activation(probs[:, step % 3, :], probs[:, step % 3, :], ACT.Exp,
                                                 bias=row_min[:, step:step + 1], scale=-1.0,
                                                 accum_out=row_sum[:, step:step + 1]).then_inc(s_probs, 1)
                        if step >= 1:
                            i = step - 1
                            for half in range(2):
                                n = 2 * i + half
                                act.wait_ge(s_turned, n + 1)
                                if i >= 2:
                                    act.wait_ge(s_summed, i - 1)
                                nc.scalar.copy(
                                    probs_t_high[:, i % 2, 4 * half:4 * half + 4, :].rearrange("p k q -> p (k q)"),
                                    turned[n % 2][:]).then_inc(s_turned_high, 1)

                @block.vector
                def _(dve):
                    for i in range(XT):
                        d, n = i % DIM_TILES, i // DIM_TILES
                        cols = slice(n * BANK, (n + 1) * BANK)
                        dve.wait_ge(s_xt_high, i + 1)
                        nc.vector.tensor_tensor(xt_low[:, d, cols], bank[i][:], xt_high[:, d, cols].bitcast(F32),
                                                ALU.subtract).then_inc(s_xt_low, 1)
                    for i in range(PB):
                        dve.wait_ge(s_high, i + 1)
                        if i < QB:
                            d, n = i % DIM_TILES, i // DIM_TILES
                            cols = slice(n * BANK, (n + 1) * BANK)
                            to, of = q_low[:, d, cols], q_high[:, d, cols]
                        else:
                            rows = slice(2 * (i - QB), 2 * (i - QB) + 2)
                            to = v_low[:, rows, :].rearrange("p t d -> p (t d)")
                            of = v_high[:, rows, :].rearrange("p t d -> p (t d)")
                        nc.vector.tensor_tensor(to, bank[i % 4][:], of.bitcast(F32), ALU.subtract).then_inc(s_low, 1)
                    for step in range(TILES + 3):
                        if step < TILES:
                            dve.wait_ge(s_scores, step + 1)
                            dve.wait_ge(s_penalty, step + 1)
                            if step >= 3:
                                dve.wait_ge(s_turned, 2 * (step - 2))
                            for n in range(HALVES):
                                cols = slice(n * BANK, (n + 1) * BANK)
                                nc.vector.tensor_tensor_reduce(
                                    out=probs[:, step % 3, cols], in0=bank[2 * (step % 2) + n][:],
                                    in1=penalty[:, step % 2, cols], scale=1.0,
                                    scalar=3.0e38 if n == 0 else row_min[:, step:step + 1], op0=ALU.add, op1=ALU.min,
                                    accum_out=row_min[:, step:step + 1]).then_inc(s_first_min if n == 0 else s_min, 1)
                                if n == 0:
                                    dve.wait_ge(s_first_min, step + 1)
                        if 1 <= step <= TILES:
                            i = step - 1
                            for half in range(2):
                                n = 2 * i + half
                                dve.wait_ge(s_turned_high, n + 1)
                                part = slice(4 * half, 4 * half + 4)
                                nc.vector.tensor_tensor(
                                    probs_t_low[:, i % 2, part, :].rearrange("p k q -> p (k q)"), turned[n % 2][:],
                                    probs_t_high[:, i % 2, part, :].rearrange("p k q -> p (k q)").bitcast(F32),
                                    ALU.subtract).then_inc(s_turned_low, 1)
                            dve.wait_ge(s_probs, i + 1)
                            nc.vector.reciprocal(inverse[:, i:i + 1], row_sum[:, i:i + 1]).then_inc(s_inverse, 1)
                        if step >= 3:
                            i = step - 3
                            dve.wait_ge(s_deviation, i + 1)
                            center_and_scale(nc, result[:, i, :], result[:, i, :], moments[:, i, :]
                                             ).then_inc(s_normed, 1)
                        if 2 <= step < TILES + 2:
                            i = step - 2
                            dve.wait_ge(s_summed, i + 1)
                            dve.wait_ge(s_inverse, i + 1)
                            dve.wait_ge(s_residual, i + 1)
                            nc.vector.scalar_tensor_tensor(result[:, i, :], summed[i % 2][:], inverse[:, i:i + 1],
                                                           x_sb[:, i, :], ALU.mult, ALU.add).then_inc(s_sum, 1)
                            dve.wait_ge(s_sum, i + 1)
                            tile_moments(nc, dve, result[:, i, :], stats[:, i, :], moments[:, i, :], s_stats, i,
                                         s_moments)

            m.clear()


def graph_layers(nc, a, out):
    def scratch(name):
        return nc.dram_tensor(name, [BATCH, SEQ, DIM], F32).ap()

    attended, after_0, after_1, after_2 = (scratch(n) for n in ("attended", "after_0", "after_1", "after_2"))
    adj, ident = a["adj"], a["ident"]
    w0 = {k: a["L0_gnn_" + k] for k in ("wq", "wk", "wv", "wo", "bq", "bk", "bv", "bo")}
    multi_head_layer(nc, "l0", a["x"], adj, ident, w0 | {"g": a["L0_gnn_ln1_g"], "b": a["L0_gnn_ln1_b"]}, attended,
                     True)
    mlp_layer(nc, "mlp", attended, ident,
              {k: a["L0_gnn_" + k] for k in ("w1", "b1", "w2", "b2")} |
              {"g": a["L0_gnn_ln2_g"], "b": a["L0_gnn_ln2_b"]}, after_0)
    for n, source, target in ((1, after_0, after_1), (2, after_1, after_2)):
        single_head_layer(nc, f"l{n}", source, adj, ident,
                          {"wq_t": a[f"L{n}_gnn_Wq_t"], "wk_t": a[f"L{n}_gnn_Wk_t"], "wv_t": a[f"L{n}_gnn_Wv_t"],
                           "wo": a[f"L{n}_gnn_Wo"], "bo": a[f"L{n}_gnn_bo"], "g": a[f"L{n}_gnn_gamma"],
                           "b": a[f"L{n}_gnn_beta"]}, target)
    w3 = {k.lower(): a["L3_gnn_" + k] for k in ("Wq", "Wk", "Wv", "Wo", "bq", "bk", "bv", "bo")}
    multi_head_layer(nc, "l3", after_2, adj, ident, w3 | {"g": a["L3_gnn_gamma"], "b": a["L3_gnn_beta"]}, out, False)


def kernel(**inputs):
    import numpy as np
    import concourse.bacc as bacc
    from concourse.bass_utils import run_bass_kernel_spmd

    nc = bacc.Bacc("TRN2", target_bir_lowering=False, num_devices=1)
    turned = {f"L{n}_gnn_{w}" for n in (1, 2) for w in ("Wq", "Wk", "Wv")}
    arrays = {}
    for name, value in inputs.items():
        value = np.asarray(value)
        if name in turned:
            name, value = name + "_t", value.T
        arrays[name] = np.ascontiguousarray(value)
    arrays["ident"] = np.eye(P, dtype=np.float32)
    drams = {name: nc.dram_tensor(name, value.shape, mybir.dt.from_np(value.dtype), kind="ExternalInput").ap()
             for name, value in arrays.items()}
    out = nc.dram_tensor("hidden_out", (BATCH, SEQ, DIM), F32, kind="ExternalOutput").ap()
    graph_layers(nc, drams, out)
    r = run_bass_kernel_spmd(nc, [arrays], core_ids=[0])
    return r.results[0]["hidden_out"]
```

```python
from contextlib import ExitStack

import concourse.bass as bass
from concourse import mybir

F32 = mybir.dt.float32
F32R = mybir.dt.float32r
I32 = mybir.dt.int32
ALU = mybir.AluOpType
ACT = mybir.ActivationFunctionType

P = 128
BATCH, SEQ, DIM = 8, 1024, 256
HEADS = 8
HEAD_DIM = DIM // HEADS
HIDDEN = 4 * DIM
TILES = SEQ // P
DIM_TILES = DIM // P
GROUP = P // HEAD_DIM
GROUPS = HEADS // GROUP
STACK = 3 * HEAD_DIM
BANK = 512
HALVES = SEQ // BANK
PENALTY = 1.0e30
MASK = 1.0e28
EPS = 1e-5
STATS = 6


class Pool:

    def __init__(self, nc, ctx, tag):
        self.nc, self.ctx, self.tag = nc, ctx, tag
        self.sems = []

    def sb(self, name, shape, dtype=F32):
        return self.ctx.enter_context(self.nc.sbuf_tensor(f"{self.tag}_{name}", shape, dtype))

    def ps(self, name, shape):
        return self.ctx.enter_context(self.nc.psum_tensor(f"{self.tag}_{name}", shape, F32))

    def sem(self, name):
        s = self.ctx.enter_context(self.nc.semaphore(f"{self.tag}_{name}"))
        self.sems.append(s)
        return s

    def clear(self):
        for s in self.sems:
            self.nc.gpsimd.sem_clear(s)
        self.nc.all_engine_barrier()


def of_batch(dram, b):
    return dram[bass.ds(b, 1)].rearrange("a s n -> (a s) n")


def split_matmul(nc, out, lhs_high, lhs_low, rhs_high, rhs_low, start, stop):
    nc.tensor.matmul(out, lhs_high, rhs_high, start=start, stop=False)
    nc.tensor.matmul(out, lhs_high, rhs_low, start=False, stop=False)
    return nc.tensor.matmul(out, lhs_low, rhs_high, start=False, stop=stop)


def split_weights(nc, weights, tag):
    with ExitStack() as ctx:
        m = Pool(nc, ctx, tag)
        s_scaled, s_high, s_low = m.sem("scaled"), m.sem("high"), m.sem("low")
        with nc.Block() as block:

            @block.vector
            def _(dve):
                for n, (raw, high, low, factor, gain) in enumerate(weights):
                    for k in range(raw.shape[1]):
                        if gain is None:
                            op = nc.vector.tensor_scalar(raw[:, k, :], raw[:, k, :], factor, None, ALU.mult)
                        else:
                            op = nc.vector.tensor_scalar(raw[:, k, :], raw[:, k, :], gain[:, k:k + 1], factor,
                                                         ALU.mult, ALU.mult)
                    op.then_inc(s_scaled, 1)
                for n, (raw, high, low, factor, gain) in enumerate(weights):
                    dve.wait_ge(s_scaled, n + 1)
                    dve.wait_ge(s_high, n + 1)
                    nc.vector.tensor_tensor(low, raw, high.bitcast(F32), ALU.subtract).then_inc(s_low, 1)
                dve.wait_ge(s_low, len(weights))

            @block.scalar
            def _(act):
                for n, (raw, high, low, factor, gain) in enumerate(weights):
                    act.wait_ge(s_scaled, n + 1)
                    nc.scalar.copy(high, raw).then_inc(s_high, 1)
                act.wait_ge(s_high, len(weights))

        m.clear()


def load_all(nc, pairs, tag):
    with ExitStack() as ctx:
        m = Pool(nc, ctx, tag)
        s_loaded = m.sem("loaded")
        with nc.Block() as block:

            @block.sync
            def _(sp):
                for destination, source in pairs:
                    sp.dma_start(destination, source, allow_slow_non_contiguous=True).then_inc(s_loaded, 16)
                sp.wait_ge(s_loaded, 16 * len(pairs))

        m.clear()


def matrix(dram):
    return dram.rearrange("(k p) n -> p k n", p=P)


def column(dram):
    return dram.rearrange("(k p) -> p k", p=P)


def spread(dram):
    return dram.rearrange("(a n) -> a n", a=1).partition_broadcast(P)


def fold_shift(nc, shift, columns, rows, tag):
    with ExitStack() as ctx:
        m = Pool(nc, ctx, tag)
        spread_shift = m.sb("spread_shift", [P, DIM_TILES, P])
        ones = m.sb("ones", [P, P])
        col = m.ps("col", [P, BANK])
        row = [m.ps(f"row{n}", [P, DIM]) for n in range(len(rows))]
        s_ones, s_spread, s_product, s_added = m.sem("ones"), m.sem("spread"), m.sem("product"), m.sem("added")
        with nc.Block() as block:

            @block.vector
            def _(dve):
                nc.vector.memset(ones[:], 1.0).then_inc(s_ones, 1)
                dve.wait_ge(s_ones, 1)
                for k in range(DIM_TILES):
                    nc.vector.tensor_scalar(spread_shift[:, k, :], ones[:], shift[:, k:k + 1], None,
                                            ALU.mult).then_inc(s_spread, 1)
                dve.wait_ge(s_product, 1)
                at = 0
                for _, bias in columns:
                    w = bias.shape[1]
                    nc.vector.tensor_tensor(bias[:, :], bias[:, :], col[:, at:at + w], ALU.add).then_inc(s_added, 1)
                    at += w
                for n, (_, bias) in enumerate(rows):
                    nc.vector.tensor_tensor(bias[:], bias[:], row[n][:], ALU.add).then_inc(s_added, 1)
                dve.wait_ge(s_added, len(columns) + len(rows))

            @block.tensor
            def _(pe):
                pe.wait_ge(s_spread, DIM_TILES)
                at = 0
                for raw, bias in columns:
                    for j in range(bias.shape[1]):
                        for k in range(DIM_TILES):
                            op = nc.tensor.matmul(col[:, at:at + 1], raw[:, k, j * P:(j + 1) * P], shift[:, k:k + 1],
                                                  start=(k == 0), stop=(k == DIM_TILES - 1))
                        at += 1
                for n, (raw, _) in enumerate(rows):
                    for k in range(DIM_TILES):
                        op = nc.tensor.matmul(row[n][:], spread_shift[:, k, :], raw[:, k, :],
                                              start=(k == 0), stop=(k == DIM_TILES - 1))
                op.then_inc(s_product, 1)

        m.clear()


def tile_moments(nc, dve, source, stats, moments, s_stats, i, s_moments):
    nc.vector.bn_stats(stats, source).then_inc(s_stats, 1)
    dve.wait_ge(s_stats, i + 1)
    nc.vector.bn_aggr(moments, stats).then_inc(s_moments, 1)


def inverse_deviation(nc, pool, variance, exponent, s_shifted, i, s_deviation):
    nc.gpsimd.tensor_scalar(variance, variance, EPS, None, ALU.add).then_inc(s_shifted, 1)
    pool.wait_ge(s_shifted, i + 1)
    nc.gpsimd.tensor_tensor(variance, variance, exponent, ALU.pow).then_inc(s_deviation, 1)


def center_and_scale(nc, out, source, moments):
    return nc.vector.tensor_scalar(out, source, moments[:, 0:1], moments[:, 1:2], ALU.subtract, ALU.mult)


def fill(nc, tile, value, tag):
    with ExitStack() as ctx:
        m = Pool(nc, ctx, tag)
        s_filled = m.sem("filled")
        with nc.Block() as block:

            @block.gpsimd
            def _(pool):
                nc.gpsimd.memset(tile, value).then_inc(s_filled, 1)
                pool.wait_ge(s_filled, 1)

        m.clear()



ITEMS = TILES * HEADS
GROUP_ITEMS = ITEMS // GROUPS
UNITS = ITEMS // GROUP
RING = 3
TURN_LAG = 2
VALUE_LAG = 6
STEPS = ITEMS + VALUE_LAG + 2 * GROUP
EARLY = TILES // 2
MOVES = 3 * GROUP
INPUT_RING = 3

BLOCKS = [("k", 0), ("k", 1), ("q", 0), ("q", 1)]
SIDE = {1 + 4 * n: ("block", n) for n in range(4)}
SIDE |= {3 + 4 * n: ("value", n) for n in range(2)}
TURN_STEP = 17
SIDE |= {TURN_STEP + 2 * t: ("turn", t) for t in range(TILES)}
SIDE |= {GROUP_ITEMS + step: ("block", 4 + n) for n, step in enumerate((1, 4, 7, 9))}
SIDE |= {GROUP_ITEMS + step: ("value", 2 + n) for n, step in enumerate((6, 11))}
FACTOR_STEP = GROUP_ITEMS + VALUE_LAG + GROUP
SIDE |= {FACTOR_STEP + 4 * t: ("factor", t) for t in range(TILES)}
SIDE |= {FACTOR_STEP + 3 + 4 * t: ("output", t) for t in range(TILES)}


def on_act(n):
    return n % 2 == 0 or n % 16 in (3, 7, 11)


def halves_on_act(n):
    return sum(on_act(i) for i in range(n))


def place(item):
    group, rest = divmod(item, GROUP_ITEMS)
    return rest // GROUP, group * GROUP + rest % GROUP


def multi_head_layer(nc, tag, x_dram, adj_dram, ident_dram, w, out_dram, pre_norm):
    scale = float(HEAD_DIM) ** -0.5
    OUT_RING = 2 if pre_norm else 4
    with ExitStack() as ctx:
        m = Pool(nc, ctx, tag)
        ident = m.sb("ident", [P, P])
        names = ["q", "k", "v", "o"]
        high = {n: m.sb(f"w{n}_high", [P, DIM_TILES, DIM], F32R) for n in names}
        low = {n: m.sb(f"w{n}_low", [P, DIM_TILES, DIM], F32R) for n in names}
        bias_q, bias_k = m.sb("bias_q", [P, DIM_TILES]), m.sb("bias_k", [P, DIM_TILES])
        bias_o = m.sb("bias_o", [P, DIM])
        exponent = m.sb("exponent", [P, 1])
        fill(nc, exponent[:], -0.5, tag + "_exponent")
        if not pre_norm:
            gamma, beta = m.sb("gamma", [P, DIM]), m.sb("beta", [P, DIM])

        with ExitStack() as prep:
            t = Pool(nc, prep, tag + "_prep")
            raw = {n: t.sb(f"raw_{n}", [P, DIM_TILES, DIM]) for n in names}
            bias_v = t.sb("bias_v", [P, DIM_TILES])
            loads = [(raw[n][:], matrix(w["w" + n])) for n in names]
            loads += [(ident[:], ident_dram), (bias_q[:], column(w["bq"])), (bias_k[:], column(w["bk"])),
                      (bias_v[:], column(w["bv"])), (bias_o[:], spread(w["bo"]))]
            gain = None
            if pre_norm:
                gain, shift = t.sb("gain", [P, DIM_TILES]), t.sb("shift", [P, DIM_TILES])
                loads += [(gain[:], column(w["g"])), (shift[:], column(w["b"]))]
            else:
                loads += [(gamma[:], spread(w["g"])), (beta[:], spread(w["b"]))]
            load_all(nc, loads, tag + "_load")
            if pre_norm:
                fold_shift(nc, shift, [(raw["q"], bias_q), (raw["k"], bias_k), (raw["v"], bias_v)], [],
                           tag + "_fold")
            fold_shift(nc, bias_v, [], [(raw["o"], bias_o)], tag + "_fold_v")
            split_weights(nc, [(raw[n][:], high[n][:], low[n][:], -scale if n == "q" else 1.0,
                                gain if n != "o" else None) for n in names], tag + "_split")
            s_bias = t.sem("bias")
            with nc.Block() as block:

                @block.vector
                def _(dve):
                    nc.vector.tensor_scalar(bias_q[:], bias_q[:], -scale, None, ALU.mult).then_inc(s_bias, 1)
                    dve.wait_ge(s_bias, 1)

            t.clear()

        q_stack = m.sb("q_stack", [P, HEADS, SEQ], F32R)
        k_stack = m.sb("k_stack", [P, HEADS, SEQ], F32R)
        part_high, part_low = (m.sb(f"part_{s}", [P, 2, BANK], F32R) for s in ("high", "low"))
        xt_high, xt_low = (m.sb(f"xt_{s}", [P, DIM_TILES, SEQ], F32R) for s in ("high", "low"))
        values = m.sb("values", [P, GROUPS, TILES, P])
        penalty = m.sb("penalty", [P, TILES, SEQ])
        x_in = m.sb("x_in", [P, INPUT_RING, DIM])
        probs = m.sb("probs", [P, RING, SEQ])
        probs_t = m.sb("probs_t", [P, 2, TILES, GROUP, P])
        row_min, row_sum = m.sb("row_min", [P, HEADS]), m.sb("row_sum", [P, TILES, HEADS])
        inverse = m.sb("inverse", [P, GROUPS, P])
        heads_0, heads_1 = m.sb("heads_0", [P, TILES, P]), m.sb("heads_1", [P, 2, P])
        heads_high, heads_low = (m.sb(f"heads_{s}", [P, GROUPS, P], F32R) for s in ("high", "low"))
        rows = m.sb("rows", [P, OUT_RING, DIM])
        stats = m.sb("stats", [P, TILES, STATS])
        moments = m.sb("moments", [P, TILES, 2])
        if pre_norm:
            edge, mask = m.sb("edge", [P, SEQ]), m.sb("mask", [P, 1])
            fill(nc, mask[:], MASK, tag + "_mask")
        scores = [m.ps(f"scores{i}", [P, SEQ]) for i in range(2)]
        turned = [m.ps(f"turned{i}", [P, BANK]) for i in range(2)]
        summed = m.ps("summed", [P, P])
        side = m.ps("side", [P, BANK])

        s_scores, s_min, s_probs = m.sem("scores"), m.sem("min"), m.sem("probs")
        s_turned, s_copied_act, s_copied_dve = m.sem("turned"), m.sem("copied_act"), m.sem("copied_dve")
        s_summed, s_heads, s_inverse = m.sem("summed"), m.sem("heads"), m.sem("inverse")
        s_reciprocal = m.sem("reciprocal")
        s_side, s_rounded, s_side_free = m.sem("side"), m.sem("rounded"), m.sem("side_free")
        s_moved = [m.sem(f"moved{i}") for i in range(2)]
        s_x = [m.sem(f"x{i}") for i in range(INPUT_RING)]
        s_adj = [m.sem(f"adj{i}") for i in range(EARLY)]
        s_penalty, s_value, s_squared, s_edge, s_mask = (m.sem("penalty"), m.sem("value"), m.sem("squared"),
                                                        m.sem("edge"), m.sem("mask"))
        s_stats, s_moments, s_shifted, s_deviation = (m.sem("stats"), m.sem("moments"), m.sem("shifted"),
                                                      m.sem("deviation"))
        s_normed = m.sem("normed")
        s_heads_high, s_heads_low = m.sem("heads_high"), m.sem("heads_low")
        s_rows = [m.sem(f"rows{i}") for i in range(OUT_RING)]
        s_residual, s_gained, s_result = m.sem("residual"), m.sem("gained"), m.sem("result")
        s_out = [m.sem(f"out{i}") for i in range(OUT_RING)]

        def iteration(b, b_next, attend):
            work = {s: v for s, v in SIDE.items()
                    if attend or v[0] == "turn" or (v[0] == "block" and v[1] >= 4) or (v[0] == "value" and v[1] >= 2)}
            order = sorted(work)
            index = {work[s]: n for n, s in enumerate(order)}
            first_block = 0 if attend else 4

            penalty_at = {3 * n: EARLY + n for n in range(TILES - EARLY)} if attend else {}
            penalty_at |= {GROUP_ITEMS + 6 + 4 * t: t for t in range(EARLY)}

            def penalty_index(t):
                return [penalty_at[s] for s in sorted(penalty_at)].index(t)

            def rounded_before(what):
                return sum(work[s][0] in ("block", "turn") for s in order[:index[what]])

            n_in = TILES if pre_norm else 0
            x_next = of_batch(x_dram, b_next).rearrange("(t p) d -> p t d", p=P)
            adj_next = of_batch(adj_dram, b_next).rearrange("(t p) k -> p t k", p=P)
            if attend:
                x_now = of_batch(x_dram, b).rearrange("(t p) d -> p t d", p=P)
                adj_now = of_batch(adj_dram, b).rearrange("(t p) k -> p t k", p=P)
                y_now = of_batch(out_dram, b).rearrange("(t p) d -> p t d", p=P)

            with nc.Block() as block:

                @block.sync
                def _(sp):
                    def load_x(t):
                        sp.dma_start(x_in[:, t % INPUT_RING, :], x_next[:, t, :]).then_inc(s_x[t % INPUT_RING], 16)

                    def load_adj(view, t):
                        sp.dma_start(penalty[:, t, :].bitcast(I32), view[:, t, :]).then_inc(s_adj[t % EARLY], 16)

                    for t in range(INPUT_RING):
                        load_x(t)
                    if attend:
                        for t in range(EARLY, TILES):
                            load_adj(adj_now, t)
                    for step in range(STEPS + 12):
                        what, n = work.get(step - 1, (None, 0))
                        if what == "block":
                            which, half = BLOCKS[n % 4]
                            stack, parts = ((k_stack, (part_high, part_low, part_high)) if which == "k" else
                                            (q_stack, (part_high, part_high, part_low)))
                            sp.wait_ge(s_side_free, index["block", n] + 1)
                            if n == 4 and attend:
                                sp.wait_ge(s_scores, GROUP_ITEMS)
                            cols = slice(half * BANK, (half + 1) * BANK)
                            for j in range(GROUP):
                                head = (GROUP if n < 4 else 0) + j
                                for s, part in enumerate(parts):
                                    sp.dma_start(stack[s * HEAD_DIM:(s + 1) * HEAD_DIM, head, cols].bitcast(F32),
                                                 part[j * HEAD_DIM:(j + 1) * HEAD_DIM, n % 2, :].bitcast(F32)
                                                 ).then_inc(s_moved[n % 2], 16)
                        if what == "turn" and n + INPUT_RING < TILES:
                            sp.wait_ge(s_side, index["turn", n] + 1)
                            load_x(n + INPUT_RING)
                        t, part = divmod(step - GROUP_ITEMS - 4, 4)
                        if part == 0 and 0 <= t < EARLY:
                            if attend:
                                sp.wait_ge(s_min, GROUP_ITEMS + GROUP * (t + 1))
                            load_adj(adj_next, t)
                        if not attend:
                            continue
                        t, part = divmod(step - (FACTOR_STEP - 2), 4)
                        if part == 0 and 0 <= t < TILES:
                            slot = t % OUT_RING
                            if t >= OUT_RING:
                                sp.wait_ge(s_out[slot], 16 * (t // OUT_RING))
                            sp.dma_start(rows[:, slot, :], x_now[:, t, :]).then_inc(s_rows[slot], 16)
                        t, part = divmod(step - (FACTOR_STEP + (5 if pre_norm else 11)), 4)
                        if part == 0 and 0 <= t < TILES:
                            if pre_norm:
                                sp.wait_ge(s_side_free, index["output", t] + 1)
                            else:
                                sp.wait_ge(s_result, t + 1)
                            sp.dma_start(y_now[:, t, :], rows[:, t % OUT_RING, :]).then_inc(s_out[t % OUT_RING], 16)
                    if attend:
                        for i in range(OUT_RING):
                            sp.wait_ge(s_out[i], 16 * (TILES // OUT_RING))
                    for i in range(2):
                        sp.wait_ge(s_moved[i], 16 * MOVES * (8 - first_block) // 2)

                @block.gpsimd
                def _(pool):
                    def make_penalty(t):
                        n = penalty_index(t)
                        adj = penalty[:, t, :].bitcast(I32)
                        pool.wait_ge(s_adj[n % EARLY], 16 * (n // EARLY + 1))
                        if pre_norm:
                            if n:
                                pool.wait_ge(s_penalty, n)
                            nc.gpsimd.tensor_scalar(edge[:], adj, 1.0, 0.0, ALU.mult, ALU.add).then_inc(s_value, 1)
                            pool.wait_ge(s_value, n + 1)
                            nc.gpsimd.tensor_tensor(edge[:], edge[:], edge[:], ALU.mult).then_inc(s_squared, 1)
                            pool.wait_ge(s_squared, n + 1)
                            nc.gpsimd.tensor_scalar(edge[:], edge[:], -0.1, 0.0, ALU.mult, ALU.add).then_inc(s_edge, 1)
                            pool.wait_ge(s_edge, n + 1)
                            pool.wait_ge(s_mask, n + 1)
                            nc.gpsimd.tensor_tensor(penalty[:, t, :], penalty[:, t, :], edge[:],
                                                    ALU.add).then_inc(s_penalty, 1)
                        else:
                            nc.gpsimd.tensor_scalar(penalty[:, t, :], adj, 0.0, PENALTY, ALU.is_equal,
                                                    ALU.mult).then_inc(s_penalty, 1)

                    for step in range(STEPS + 12):
                        t = penalty_at.get(step)
                        if t is not None:
                            make_penalty(t)
                        t, part = divmod(step - (TURN_STEP - 3), 2)
                        if pre_norm and part == 0 and 0 <= t < TILES:
                            pool.wait_ge(s_moments, t + 1)
                            inverse_deviation(nc, pool, moments[:, t, 1:2], exponent[:], s_shifted, t, s_deviation)
                        if not attend:
                            continue
                        t, part = divmod(step - FACTOR_STEP, 4)
                        if part == 0 and 0 <= t < TILES:
                            pool.wait_ge(s_rows[t % OUT_RING], 16 * (t // OUT_RING + 1))
                            nc.gpsimd.tensor_tensor(rows[:, t % OUT_RING, :], rows[:, t % OUT_RING, :], bias_o[:],
                                                    ALU.add).then_inc(s_residual, 1)
                        t, part = divmod(step - (FACTOR_STEP + 5), 4)
                        if not pre_norm and part == 0 and 0 <= t < TILES:
                            pool.wait_ge(s_moments, t + 1)
                            inverse_deviation(nc, pool, moments[:, t, 1:2], exponent[:], s_shifted, t, s_deviation)
                        t, part = divmod(step - (FACTOR_STEP + 8), 4)
                        if not pre_norm and part == 0 and 0 <= t < TILES:
                            row = rows[:, t % OUT_RING, :]
                            pool.wait_ge(s_normed, t + 1)
                            nc.gpsimd.tensor_tensor(row, row, gamma[:], ALU.mult).then_inc(s_gained, 1)
                            pool.wait_ge(s_gained, t + 1)
                            nc.gpsimd.tensor_tensor(row, row, beta[:], ALU.add).then_inc(s_result, 1)

                @block.tensor
                def _(pe):
                    for step in range(STEPS):
                        if attend and step < ITEMS:
                            tile, head = place(step)
                            if step >= 2:
                                pe.wait_ge(s_min, step - 1)
                            if step == GROUP_ITEMS:
                                for i in range(2):
                                    pe.wait_ge(s_moved[i], 16 * MOVES * 2)
                            for n in range(HALVES):
                                op = nc.tensor.matmul(scores[step % 2][:, n * BANK:(n + 1) * BANK],
                                                      q_stack[0:STACK, head, tile * P:(tile + 1) * P],
                                                      k_stack[0:STACK, head, n * BANK:(n + 1) * BANK],
                                                      start=True, stop=True)
                            op.then_inc(s_scores, 1)
                        item = step - TURN_LAG
                        if attend and 0 <= item < ITEMS:
                            pe.wait_ge(s_probs, item + 1)
                            for half in range(2):
                                n = 2 * item + half
                                if n >= 2:
                                    if on_act(n - 2):
                                        pe.wait_ge(s_copied_act, halves_on_act(n - 1))
                                    else:
                                        pe.wait_ge(s_copied_dve, n - 1 - halves_on_act(n - 1))
                                for j in range(4):
                                    k = 4 * half + j
                                    op = nc.tensor.transpose(turned[n % 2][:, j * P:(j + 1) * P],
                                                             probs[:, item % RING, k * P:(k + 1) * P], ident[:])
                                op.then_inc(s_turned, 1)
                        unit, part = divmod(step - VALUE_LAG, GROUP)
                        if attend and 0 <= unit < UNITS:
                            group = unit // TILES
                            if part == 0:
                                n = 2 * GROUP * (unit + 1)
                                pe.wait_ge(s_copied_act, halves_on_act(n))
                                pe.wait_ge(s_copied_dve, n - halves_on_act(n))
                                if unit >= 1:
                                    pe.wait_ge(s_heads, unit)
                                if unit == TILES:
                                    pe.wait_ge(s_side_free, index["value", 1] + 1)
                            for k in (2 * part, 2 * part + 1):
                                for j in range(GROUP):
                                    op = nc.tensor.matmul(summed[j * HEAD_DIM:(j + 1) * HEAD_DIM, :],
                                                          values[:, group, k, j * HEAD_DIM:(j + 1) * HEAD_DIM],
                                                          probs_t[:, unit % 2, k, j, :],
                                                          start=(k == 0), stop=(k == TILES - 1))
                            if part == GROUP - 1:
                                op.then_inc(s_summed, 1)
                        what, n = work.get(step, (None, 0))
                        if what is None:
                            continue
                        if index[what, n]:
                            pe.wait_ge(s_side_free, index[what, n])
                        if what == "block":
                            which, half = BLOCKS[n % 4]
                            group = 1 if n < 4 else 0
                            cols = slice(half * BANK, (half + 1) * BANK)
                            for k in range(DIM_TILES):
                                op = split_matmul(nc, side[:], high[which][:, k, group * P:(group + 1) * P],
                                                  low[which][:, k, group * P:(group + 1) * P], xt_high[:, k, cols],
                                                  xt_low[:, k, cols], k == 0, k == DIM_TILES - 1)
                        if what == "value":
                            group = 1 if n < 2 else 0
                            for j in range(4):
                                tile = 4 * (n % 2) + j
                                for k in range(DIM_TILES):
                                    op = split_matmul(nc, side[:, j * P:(j + 1) * P],
                                                      xt_high[:, k, tile * P:(tile + 1) * P],
                                                      xt_low[:, k, tile * P:(tile + 1) * P],
                                                      high["v"][:, k, group * P:(group + 1) * P],
                                                      low["v"][:, k, group * P:(group + 1) * P],
                                                      k == 0, k == DIM_TILES - 1)
                        if what == "turn":
                            if pre_norm:
                                pe.wait_ge(s_normed, n + 1)
                            else:
                                pe.wait_ge(s_x[n % INPUT_RING], 16 * (n // INPUT_RING + 1))
                            for k in range(DIM_TILES):
                                op = nc.tensor.transpose(side[:, k * P:(k + 1) * P],
                                                         x_in[:, n % INPUT_RING, k * P:(k + 1) * P], ident[:])
                        if what == "factor":
                            pe.wait_ge(s_inverse, n + 1)
                            for g in range(GROUPS):
                                op = nc.tensor.transpose(side[:, g * P:(g + 1) * P], inverse[:, g, :], ident[:])
                        if what == "output":
                            pe.wait_ge(s_heads_low, n + 1)
                            for g in range(GROUPS):
                                op = split_matmul(nc, side[:, 0:DIM], heads_high[:, g, :], heads_low[:, g, :],
                                                  high["o"][:, g, :], low["o"][:, g, :], g == 0, g == GROUPS - 1)
                        op.then_inc(s_side, 1)

                def copy_half(eng, copy, n, sem):
                    item, half = n // 2, n % 2
                    unit = item // GROUP
                    eng.wait_ge(s_turned, n + 1)
                    if unit >= 2:
                        eng.wait_ge(s_summed, unit - 1)
                    copy(probs_t[:, unit % 2, 4 * half:4 * half + 4, item % GROUP, :],
                         turned[n % 2][:].rearrange("p (k q) -> p k q", q=P)).then_inc(sem, 1)

                def side_views(what, n, highs):
                    if what == "block":
                        return (part_high if highs else part_low)[:, n % 2, :], side[:]
                    xt = xt_high if highs else xt_low
                    return xt[:, :, n * P:(n + 1) * P], side[:, 0:DIM].rearrange("p (k q) -> p k q", q=P)

                @block.vector
                def _(dve):
                    for step in range(STEPS + 12):
                        what, n = work.get(step - 1, (None, 0))
                        if what == "value":
                            group = 1 if n < 2 else 0
                            dve.wait_ge(s_side, index["value", n] + 1)
                            if n == 2 and attend:
                                dve.wait_ge(s_summed, TILES)
                            nc.vector.tensor_copy(
                                values[:, group, 4 * (n % 2):4 * (n % 2) + 4, :].rearrange("p t d -> p (t d)"),
                                side[:]).then_inc(s_side_free, 1)
                        if what == "factor":
                            dve.wait_ge(s_side, index["factor", n] + 1)
                            dve.wait_ge(s_heads, TILES + n + 1)
                            nc.vector.tensor_tensor(heads_0[:, n, :], heads_0[:, n, :], side[:, 0:P], ALU.mult)
                            nc.vector.tensor_tensor(heads_1[:, n % 2, :], heads_1[:, n % 2, :], side[:, P:2 * P],
                                                    ALU.mult).then_inc(s_side_free, 1)
                        if what == "output":
                            slot = n % OUT_RING
                            dve.wait_ge(s_side, index["output", n] + 1)
                            dve.wait_ge(s_residual, n + 1)
                            nc.vector.tensor_tensor(rows[:, slot, :], rows[:, slot, :], side[:, 0:DIM],
                                                    ALU.add).then_inc(s_side_free, 1)
                            if not pre_norm:
                                dve.wait_ge(s_side_free, index["output", n] + 1)
                                tile_moments(nc, dve, rows[:, slot, :], stats[:, n, :], moments[:, n, :], s_stats, n,
                                             s_moments)
                        if attend and step < ITEMS:
                            tile, head = place(step)
                            dve.wait_ge(s_scores, step + 1)
                            if EARLY * GROUP <= step < GROUP_ITEMS and step % GROUP == 0:
                                dve.wait_ge(s_penalty, tile - EARLY + 1)
                            if step >= RING:
                                dve.wait_ge(s_turned, 2 * (step - RING + 1))
                            nc.vector.tensor_tensor_reduce(
                                out=probs[:, step % RING, :], in0=scores[step % 2][:], in1=penalty[:, tile, :],
                                scale=1.0, scalar=3.0e38, op0=ALU.add, op1=ALU.min,
                                accum_out=row_min[:, head:head + 1]).then_inc(s_min, 1)
                        if what in ("block", "turn"):
                            dve.wait_ge(s_rounded, rounded_before((what, n)) + 1)
                            if what == "block" and n >= first_block + 2:
                                dve.wait_ge(s_moved[n % 2], 16 * MOVES * ((n - first_block) // 2))
                            to, source = side_views(what, n, False)
                            of, _ = side_views(what, n, True)
                            if what == "block":
                                bias = bias_k if BLOCKS[n % 4][0] == "k" else bias_q
                                group = 1 if n < 4 else 0
                                nc.vector.scalar_tensor_tensor(to, source, bias[:, group:group + 1], of.bitcast(F32),
                                                               ALU.add, ALU.subtract).then_inc(s_side_free, 1)
                            else:
                                nc.vector.tensor_tensor(to, source, of.bitcast(F32),
                                                        ALU.subtract).then_inc(s_side_free, 1)
                        item = step - TURN_LAG
                        if attend and 0 <= item < ITEMS:
                            for half in (2 * item, 2 * item + 1):
                                if not on_act(half):
                                    copy_half(dve, nc.vector.tensor_copy, half, s_copied_dve)
                        what, n = work.get(step - 2, (None, 0))
                        if what == "factor":
                            dve.wait_ge(s_heads_high, n + 1)
                            nc.vector.tensor_tensor(heads_low[:, 0, :], heads_0[:, n, :],
                                                    heads_high[:, 0, :].bitcast(F32), ALU.subtract)
                            nc.vector.tensor_tensor(heads_low[:, 1, :], heads_1[:, n % 2, :],
                                                    heads_high[:, 1, :].bitcast(F32),
                                                    ALU.subtract).then_inc(s_heads_low, 1)
                        t, part = divmod(step - (FACTOR_STEP - 1), 4)
                        if attend and part == 0 and 0 <= t < TILES:
                            dve.wait_ge(s_probs, GROUP_ITEMS + GROUP * (t + 1))
                            if t:
                                dve.wait_ge(s_side, index["factor", t - 1] + 1)
                            nc.vector.reciprocal(row_sum[:, t, :], row_sum[:, t, :]).then_inc(s_reciprocal, 1)
                            dve.wait_ge(s_reciprocal, t + 1)
                            nc.vector.tensor_copy(
                                inverse[:].rearrange("p g (h d) -> p g h d", d=HEAD_DIM),
                                row_sum[:, t, :].rearrange("p (g h) -> p g h", h=GROUP).unsqueeze(3)
                                .to_broadcast([P, GROUPS, GROUP, HEAD_DIM])).then_inc(s_inverse, 1)
                        t, part = divmod(step - (TURN_STEP - 4), 2)
                        if pre_norm and part == 0 and 0 <= t < TILES:
                            dve.wait_ge(s_x[t % INPUT_RING], 16 * (t // INPUT_RING + 1))
                            tile_moments(nc, dve, x_in[:, t % INPUT_RING, :], stats[:, t, :], moments[:, t, :],
                                         s_stats, t, s_moments)
                        t, part = divmod(step - (TURN_STEP - 1), 2)
                        if pre_norm and part == 0 and 0 <= t < TILES:
                            x = x_in[:, t % INPUT_RING, :]
                            dve.wait_ge(s_deviation, t + 1)
                            center_and_scale(nc, x, x, moments[:, t, :]).then_inc(s_normed, 1)
                        t, part = divmod(step - (FACTOR_STEP + 6), 4)
                        if attend and not pre_norm and part == 0 and 0 <= t < TILES:
                            row = rows[:, t % OUT_RING, :]
                            dve.wait_ge(s_deviation, t + 1)
                            center_and_scale(nc, row, row, moments[:, t, :]).then_inc(s_normed, 1)

                @block.scalar
                def _(act):
                    for step in range(STEPS + 12):
                        unit, part = divmod(step - VALUE_LAG - GROUP, GROUP)
                        if attend and 0 <= unit < UNITS and part == 0:
                            act.wait_ge(s_summed, unit + 1)
                            group, tile = divmod(unit, TILES)
                            if group == 1 and tile >= 2:
                                act.wait_ge(s_heads_low, tile - 1)
                            nc.scalar.copy(heads_0[:, tile, :] if group == 0 else heads_1[:, tile % 2, :],
                                           summed[:]).then_inc(s_heads, 1)
                        item = step - 1
                        if attend and 0 <= item < ITEMS:
                            tile, head = place(item)
                            act.wait_ge(s_min, item + 1)
                            nc.scalar.activation(probs[:, item % RING, :], probs[:, item % RING, :], ACT.Exp,
                                                 bias=row_min[:, head:head + 1], scale=-1.0,
                                                 accum_out=row_sum[:, tile, head:head + 1]).then_inc(s_probs, 1)
                        what, n = work.get(step - 1, (None, 0))
                        if what in ("block", "turn"):
                            act.wait_ge(s_side, index[what, n] + 1)
                            if what == "block" and n >= first_block + 2:
                                act.wait_ge(s_moved[n % 2], 16 * MOVES * ((n - first_block) // 2))
                            to, source = side_views(what, n, True)
                            if what == "block":
                                bias = bias_k if BLOCKS[n % 4][0] == "k" else bias_q
                                group = 1 if n < 4 else 0
                                nc.scalar.activation(to, source, ACT.Identity,
                                                     bias=bias[:, group:group + 1]).then_inc(s_rounded, 1)
                            else:
                                nc.scalar.copy(to, source).then_inc(s_rounded, 1)
                        if what == "factor":
                            act.wait_ge(s_side_free, index["factor", n] + 1)
                            if n:
                                act.wait_ge(s_side, index["output", n - 1] + 1)
                            nc.scalar.copy(heads_high[:, 0, :], heads_0[:, n, :])
                            nc.scalar.copy(heads_high[:, 1, :], heads_1[:, n % 2, :]).then_inc(s_heads_high, 1)
                        item = step - TURN_LAG
                        if attend and 0 <= item < ITEMS:
                            for half in (2 * item, 2 * item + 1):
                                if on_act(half):
                                    copy_half(act, nc.scalar.copy, half, s_copied_act)
                        t = penalty_at.get(step - 1)
                        if pre_norm and t is not None:
                            act.wait_ge(s_value, penalty_index(t) + 1)
                            nc.scalar.activation(penalty[:, t, :], penalty[:, t, :].bitcast(I32), ACT.Relu,
                                                 bias=mask[:], scale=-MASK).then_inc(s_mask, 1)

        iteration(None, 0, False)
        m.clear()
        with nc.Fori(0, BATCH) as b:
            iteration(b, (b + 1) % BATCH, True)
            m.clear()



def mlp_layer(nc, tag, x_dram, ident_dram, w, out_dram):
    hid_tiles = HIDDEN // P
    with ExitStack() as ctx:
        m = Pool(nc, ctx, tag)
        ident = m.sb("ident", [P, P])
        w1_high, w1_low = (m.sb(f"w1_{s}", [P, DIM_TILES, HIDDEN], F32R) for s in ("high", "low"))
        w2_high, w2_low = (m.sb(f"w2_{s}", [P, hid_tiles, DIM], F32R) for s in ("high", "low"))
        bias_1, bias_2 = m.sb("bias_1", [P, hid_tiles]), m.sb("bias_2", [P, DIM])
        with ExitStack() as prep:
            t = Pool(nc, prep, tag + "_prep")
            raw_1, raw_2 = t.sb("raw_1", [P, DIM_TILES, HIDDEN]), t.sb("raw_2", [P, hid_tiles, DIM])
            gain, shift = t.sb("gain", [P, DIM_TILES]), t.sb("shift", [P, DIM_TILES])
            load_all(nc, [(raw_1[:], matrix(w["w1"])), (raw_2[:], matrix(w["w2"])), (gain[:], column(w["g"])),
                          (shift[:], column(w["b"])), (bias_1[:], column(w["b1"])), (bias_2[:], spread(w["b2"])),
                          (ident[:], ident_dram)], tag + "_load")
            fold_shift(nc, shift, [(raw_1, bias_1)], [], tag + "_fold")
            split_weights(nc, [(raw_1[:], w1_high[:], w1_low[:], 1.0, gain),
                               (raw_2[:], w2_high[:], w2_low[:], 1.0, None)], tag + "_split")

        x_sb = m.sb("x", [P, TILES, DIM])
        normed = m.sb("normed", [P, TILES, DIM])
        result = m.sb("result", [P, TILES, DIM])
        stats, moments = m.sb("stats", [P, TILES, STATS]), m.sb("moments", [P, TILES, 2])
        xt_high, xt_low = (m.sb(f"xt_{s}", [P, DIM_TILES, SEQ], F32R) for s in ("high", "low"))
        act_full = m.sb("act_full", [P, 2, BANK])
        act_high, act_low = (m.sb(f"act_{s}", [P, hid_tiles, BANK], F32R) for s in ("high", "low"))
        turned = [m.ps(f"turned{i}", [P, BANK]) for i in range(2)]
        hidden = [m.ps(f"hidden{i}", [P, BANK]) for i in range(3)]
        projected = [m.ps(f"projected{i}", [P, DIM]) for i in range(3)]
        exponent = m.sb("exponent", [P, 4])
        fill(nc, exponent[:], -0.5, tag + "_exponent")
        s_x, s_stats, s_normed, s_moments = m.sem("x"), m.sem("stats"), m.sem("normed"), m.sem("moments")
        s_shifted, s_deviation = m.sem("shifted"), m.sem("deviation")
        s_turned, s_turned_high, s_turned_low = m.sem("turned"), m.sem("turned_high"), m.sem("turned_low")
        s_hidden, s_gelu, s_high, s_low = m.sem("hidden"), m.sem("gelu"), m.sem("high"), m.sem("low")
        s_projected, s_sum, s_out, s_residual = m.sem("projected"), m.sem("sum"), m.sem("out"), m.sem("residual")

        with nc.Fori(0, BATCH) as b:
            x_view = of_batch(x_dram, b).rearrange("(t p) d -> p t d", p=P)
            y_view = of_batch(out_dram, b).rearrange("(t p) d -> p t d", p=P)
            with nc.Block() as block:

                @block.sync
                def _(sp):
                    sp.dma_start(x_sb[:], x_view).then_inc(s_x, 16)
                    for i in range(TILES):
                        sp.wait_ge(s_sum, i + 1)
                        sp.dma_start(y_view[:, i, :], result[:, i, :]).then_inc(s_out, 16)
                    sp.wait_ge(s_out, 16 * TILES)

                @block.gpsimd
                def _(pool):
                    for n in range(HALVES):
                        pool.wait_ge(s_moments, 4 * n + 4)
                        inverse_deviation(nc, pool, moments[:, 4 * n:4 * n + 4, 1], exponent[:], s_shifted, n,
                                          s_deviation)
                    for i in range(TILES):
                        pool.wait_ge(s_normed, i + 1)
                        nc.gpsimd.tensor_tensor(x_sb[:, i, :], x_sb[:, i, :], bias_2[:],
                                                ALU.add).then_inc(s_residual, 1)

                @block.tensor
                def _(pe):
                    for i in range(DIM_TILES * HALVES):
                        d, n = i % DIM_TILES, i // DIM_TILES
                        pe.wait_ge(s_normed, 4 * n + 4)
                        if i >= 2:
                            pe.wait_ge(s_turned_low, i - 1)
                        for j in range(4):
                            op = nc.tensor.transpose(turned[i % 2][:, j * P:(j + 1) * P],
                                                     normed[:, 4 * n + j, d * P:(d + 1) * P], ident[:])
                        op.then_inc(s_turned, 1)
                    for n in range(HALVES):
                        cols = slice(n * BANK, (n + 1) * BANK)
                        pe.wait_ge(s_turned_low, DIM_TILES * (n + 1))
                        for f in range(hid_tiles):
                            i = n * hid_tiles + f
                            if i >= 3:
                                pe.wait_ge(s_gelu, i - 2)
                            for k in range(DIM_TILES):
                                op = split_matmul(nc, hidden[i % 3][:], w1_high[:, k, f * P:(f + 1) * P],
                                                  w1_low[:, k, f * P:(f + 1) * P], xt_high[:, k, cols],
                                                  xt_low[:, k, cols], k == 0, k == DIM_TILES - 1)
                            op.then_inc(s_hidden, 1)
                        for j in range(BANK // P):
                            i = n * (BANK // P) + j
                            if i >= 3:
                                pe.wait_ge(s_sum, i - 2)
                            for f in range(hid_tiles):
                                if j == 0:
                                    pe.wait_ge(s_low, n * hid_tiles + f + 1)
                                op = split_matmul(nc, projected[i % 3][:], act_high[:, f, j * P:(j + 1) * P],
                                                  act_low[:, f, j * P:(j + 1) * P], w2_high[:, f, :],
                                                  w2_low[:, f, :], f == 0, f == hid_tiles - 1)
                            op.then_inc(s_projected, 1)

                @block.scalar
                def _(act):
                    for i in range(DIM_TILES * HALVES):
                        d, n = i % DIM_TILES, i // DIM_TILES
                        act.wait_ge(s_turned, i + 1)
                        nc.scalar.copy(xt_high[:, d, n * BANK:(n + 1) * BANK], turned[i % 2][:]
                                       ).then_inc(s_turned_high, 1)
                    for i in range(HALVES * hid_tiles):
                        act.wait_ge(s_hidden, i + 1)
                        if i >= 2:
                            act.wait_ge(s_low, i - 1)
                        f = i % hid_tiles
                        nc.scalar.activation(act_full[:, i % 2, :], hidden[i % 3][:], ACT.Gelu,
                                             bias=bias_1[:, f:f + 1]).then_inc(s_gelu, 1)

                @block.vector
                def _(dve):
                    dve.wait_ge(s_x, 16)
                    for i in range(TILES):
                        tile_moments(nc, dve, x_sb[:, i, :], stats[:, i, :], moments[:, i, :], s_stats, i,
                                     s_moments)
                    for i in range(TILES):
                        if i % 4 == 0:
                            dve.wait_ge(s_deviation, i // 4 + 1)
                        center_and_scale(nc, normed[:, i, :], x_sb[:, i, :],
                                         moments[:, i, :]).then_inc(s_normed, 1)
                    for i in range(DIM_TILES * HALVES):
                        d, n = i % DIM_TILES, i // DIM_TILES
                        dve.wait_ge(s_turned_high, i + 1)
                        cols = slice(n * BANK, (n + 1) * BANK)
                        nc.vector.tensor_tensor(xt_low[:, d, cols], turned[i % 2][:], xt_high[:, d, cols].bitcast(F32),
                                                ALU.subtract).then_inc(s_turned_low, 1)
                    for n in range(HALVES):
                        for f in range(hid_tiles):
                            i = n * hid_tiles + f
                            dve.wait_ge(s_gelu, i + 1)
                            if n and f == 0:
                                dve.wait_ge(s_projected, BANK // P)
                            nc.vector.tensor_copy(act_high[:, f, :], act_full[:, i % 2, :]).then_inc(s_high, 1)
                            dve.wait_ge(s_high, i + 1)
                            nc.vector.tensor_tensor(act_low[:, f, :], act_full[:, i % 2, :],
                                                    act_high[:, f, :].bitcast(F32), ALU.subtract).then_inc(s_low, 1)
                        for j in range(BANK // P):
                            i = n * (BANK // P) + j
                            dve.wait_ge(s_projected, i + 1)
                            dve.wait_ge(s_residual, i + 1)
                            nc.vector.tensor_tensor(result[:, i, :], projected[i % 3][:], x_sb[:, i, :],
                                                    ALU.add).then_inc(s_sum, 1)

            m.clear()



def single_head_layer(nc, tag, x_dram, adj_dram, ident_dram, w, out_dram):
    scale = float(DIM) ** -0.5
    with ExitStack() as ctx:
        m = Pool(nc, ctx, tag)
        ident = m.sb("ident", [P, P])
        qk_high, qk_low, vo_high, vo_low = (m.sb(n, [P, DIM_TILES, DIM], F32R)
                                            for n in ("qk_high", "qk_low", "vo_high", "vo_low"))
        bias_o, gamma, beta = m.sb("bias_o", [P, DIM]), m.sb("gamma", [P, DIM]), m.sb("beta", [P, DIM])
        with ExitStack() as prep:
            t = Pool(nc, prep, tag + "_prep")
            wq_t, wk_t, wv_t, wo = (t.sb(n, [P, DIM_TILES, DIM]) for n in ("wq_t", "wk_t", "wv_t", "wo"))
            raw_qk, raw_vo = t.sb("raw_qk", [P, DIM_TILES, DIM]), t.sb("raw_vo", [P, DIM_TILES, DIM])
            load_all(nc, [(wq_t[:], matrix(w["wq_t"])), (wk_t[:], matrix(w["wk_t"])), (wv_t[:], matrix(w["wv_t"])),
                          (wo[:], matrix(w["wo"])), (bias_o[:], spread(w["bo"])), (gamma[:], spread(w["g"])),
                          (beta[:], spread(w["b"])), (ident[:], ident_dram)], tag + "_load")
            product = [t.ps(f"product{i}", [P, DIM]) for i in range(4)]
            s_product, s_copied = t.sem("product"), t.sem("copied")
            with nc.Block() as block:

                @block.tensor
                def _(pe):
                    for i, (left, right) in enumerate(((wq_t, wk_t), (wv_t, wo))):
                        for r in range(DIM_TILES):
                            for k in range(DIM_TILES):
                                op = nc.tensor.matmul(product[2 * i + r][:], left[:, k, r * P:(r + 1) * P],
                                                      right[:, k, :], start=(k == 0), stop=(k == DIM_TILES - 1))
                            op.then_inc(s_product, 1)

                @block.vector
                def _(dve):
                    for i, raw in enumerate((raw_qk, raw_vo)):
                        for r in range(DIM_TILES):
                            dve.wait_ge(s_product, 2 * i + r + 1)
                            nc.vector.tensor_copy(raw[:, r, :], product[2 * i + r][:]).then_inc(s_copied, 1)
                    dve.wait_ge(s_copied, 4)

            t.clear()
            split_weights(nc, [(raw_qk[:], qk_high[:], qk_low[:], -scale, None),
                               (raw_vo[:], vo_high[:], vo_low[:], 1.0, None)], tag + "_split")

        x_sb = m.sb("x", [P, TILES, DIM])
        adj_sb = m.sb("adj", [P, 2, SEQ], I32)
        penalty = m.sb("penalty", [P, 2, SEQ])
        xt_high, xt_low, q_high, q_low = (m.sb(n, [P, DIM_TILES, SEQ], F32R)
                                          for n in ("xt_high", "xt_low", "q_high", "q_low"))
        v_high, v_low = (m.sb(n, [P, TILES, DIM], F32R) for n in ("v_high", "v_low"))
        probs = m.sb("probs", [P, 3, SEQ])
        probs_t_high, probs_t_low = (m.sb(n, [P, 2, TILES, P], F32R) for n in ("probs_t_high", "probs_t_low"))
        row_min, row_sum, inverse = (m.sb(n, [P, TILES]) for n in ("row_min", "row_sum", "inverse"))
        result = m.sb("result", [P, TILES, DIM])
        stats, moments = m.sb("stats", [P, TILES, STATS]), m.sb("moments", [P, TILES, 2])
        bank = [m.ps(f"bank{i}", [P, BANK]) for i in range(4)]
        turned = [m.ps(f"turned{i}", [P, BANK]) for i in range(2)]
        summed = [m.ps(f"summed{i}", [P, DIM]) for i in range(2)]
        s_x, s_out, s_residual = m.sem("x"), m.sem("out"), m.sem("residual")
        s_adj = [m.sem(f"adj{i}") for i in range(2)]
        s_penalty = m.sem("penalty")
        s_xt, s_xt_high, s_xt_low = m.sem("xt"), m.sem("xt_high"), m.sem("xt_low")
        s_product, s_high, s_low = m.sem("product"), m.sem("high"), m.sem("low")
        s_scores, s_min, s_probs = m.sem("scores"), m.sem("min"), m.sem("probs")
        s_turned, s_turned_high, s_turned_low = m.sem("turned"), m.sem("turned_high"), m.sem("turned_low")
        exponent = m.sb("exponent", [P, 1])
        fill(nc, exponent[:], -0.5, tag + "_exponent")
        s_inverse, s_summed, s_sum, s_normed = m.sem("inverse"), m.sem("summed"), m.sem("sum"), m.sem("normed")
        s_first_min = m.sem("first_min")
        s_stats, s_moments, s_shifted, s_deviation = (m.sem("stats"), m.sem("moments"), m.sem("shifted"),
                                                      m.sem("deviation"))
        s_gained, s_result = m.sem("gained"), m.sem("result")
        XT = DIM_TILES * HALVES
        QB = DIM_TILES * HALVES
        VB = TILES * DIM // BANK
        PB = QB + VB

        with nc.Fori(0, BATCH) as b:
            x_view = of_batch(x_dram, b).rearrange("(t p) d -> p t d", p=P)
            adj_view = of_batch(adj_dram, b).rearrange("(t p) k -> p t k", p=P)
            y_view = of_batch(out_dram, b).rearrange("(t p) d -> p t d", p=P)
            with nc.Block() as block:

                @block.sync
                def _(sp):
                    sp.dma_start(x_sb[:], x_view).then_inc(s_x, 16)
                    for i in range(TILES):
                        if i >= 2:
                            sp.wait_ge(s_penalty, i - 1)
                        sp.dma_start(adj_sb[:, i % 2, :], adj_view[:, i, :]).then_inc(s_adj[i % 2], 16)
                    for i in range(TILES):
                        sp.wait_ge(s_result, i + 1)
                        sp.dma_start(y_view[:, i, :], result[:, i, :]).then_inc(s_out, 16)
                    sp.wait_ge(s_out, 16 * TILES)

                @block.gpsimd
                def _(pool):
                    def deviation(i):
                        pool.wait_ge(s_moments, i + 1)
                        inverse_deviation(nc, pool, moments[:, i, 1:2], exponent[:], s_shifted, i, s_deviation)

                    def gain_and_shift(i):
                        pool.wait_ge(s_normed, i + 1)
                        nc.gpsimd.tensor_tensor(result[:, i, :], result[:, i, :], gamma[:],
                                                ALU.mult).then_inc(s_gained, 1)
                        pool.wait_ge(s_gained, i + 1)
                        nc.gpsimd.tensor_tensor(result[:, i, :], result[:, i, :], beta[:],
                                                ALU.add).then_inc(s_result, 1)

                    for i in range(TILES):
                        pool.wait_ge(s_adj[i % 2], 16 * (i // 2 + 1))
                        if i >= 2:
                            pool.wait_ge(s_min, i - 1)
                        nc.gpsimd.tensor_scalar(penalty[:, i % 2, :], adj_sb[:, i % 2, :], 0.0, PENALTY,
                                                ALU.is_equal, ALU.mult).then_inc(s_penalty, 1)
                        if i == 1:
                            pool.wait_ge(s_xt, XT)
                            for j in range(TILES):
                                nc.gpsimd.tensor_tensor(x_sb[:, j, :], x_sb[:, j, :], bias_o[:],
                                                        ALU.add).then_inc(s_residual, 1)
                        if i >= 4:
                            deviation(i - 4)
                        if i >= 5:
                            gain_and_shift(i - 5)
                    for i in range(TILES, TILES + 5):
                        if i - 4 < TILES:
                            deviation(i - 4)
                        gain_and_shift(i - 5)

                @block.tensor
                def _(pe):
                    pe.wait_ge(s_x, 16)
                    for i in range(XT):
                        d, n = i % DIM_TILES, i // DIM_TILES
                        for j in range(4):
                            op = nc.tensor.transpose(bank[i][:, j * P:(j + 1) * P],
                                                     x_sb[:, 4 * n + j, d * P:(d + 1) * P], ident[:])
                        op.then_inc(s_xt, 1)
                    for i in range(PB):
                        pe.wait_ge(s_xt_low, min(XT, i + 1) if i >= 2 else DIM_TILES)
                        if i >= 4:
                            pe.wait_ge(s_low, i - 3)
                        if i < QB:
                            d, n = i % DIM_TILES, i // DIM_TILES
                            cols = slice(n * BANK, (n + 1) * BANK)
                            if n:
                                pe.wait_ge(s_xt_low, XT)
                            for k in range(DIM_TILES):
                                op = split_matmul(nc, bank[i % 4][:], qk_high[:, k, d * P:(d + 1) * P],
                                                  qk_low[:, k, d * P:(d + 1) * P], xt_high[:, k, cols],
                                                  xt_low[:, k, cols], k == 0, k == DIM_TILES - 1)
                        else:
                            for j in range(BANK // DIM):
                                tile = (i - QB) * (BANK // DIM) + j
                                for k in range(DIM_TILES):
                                    op = split_matmul(nc, bank[i % 4][:, j * DIM:(j + 1) * DIM],
                                                      xt_high[:, k, tile * P:(tile + 1) * P],
                                                      xt_low[:, k, tile * P:(tile + 1) * P],
                                                      vo_high[:, k, :], vo_low[:, k, :], k == 0, k == DIM_TILES - 1)
                        op.then_inc(s_product, 1)

                    def score(i):
                        if i < 2:
                            pe.wait_ge(s_low, PB - 2 + 2 * i if i == 0 else PB)
                        else:
                            pe.wait_ge(s_min, i - 1)
                        for n in range(HALVES):
                            out = bank[2 * (i % 2) + n][:]
                            for k in range(DIM_TILES):
                                op = split_matmul(nc, out, q_high[:, k, i * P:(i + 1) * P],
                                                  q_low[:, k, i * P:(i + 1) * P],
                                                  xt_high[:, k, n * BANK:(n + 1) * BANK],
                                                  xt_low[:, k, n * BANK:(n + 1) * BANK], k == 0, k == DIM_TILES - 1)
                        op.then_inc(s_scores, 1)

                    def turn(i):
                        pe.wait_ge(s_probs, i + 1)
                        for half in range(2):
                            n = 2 * i + half
                            if n >= 2:
                                pe.wait_ge(s_turned_low, n - 1)
                            for j in range(4):
                                k = 4 * half + j
                                op = nc.tensor.transpose(turned[n % 2][:, j * P:(j + 1) * P],
                                                         probs[:, i % 3, k * P:(k + 1) * P], ident[:])
                            op.then_inc(s_turned, 1)

                    def weigh(i):
                        if i >= 2:
                            pe.wait_ge(s_sum, i - 1)
                        for k in range(TILES):
                            if k % 4 == 0:
                                pe.wait_ge(s_turned_low, 2 * i + k // 4 + 1)
                            op = split_matmul(nc, summed[i % 2][:], probs_t_high[:, i % 2, k, :],
                                              probs_t_low[:, i % 2, k, :], v_high[:, k, :], v_low[:, k, :],
                                              k == 0, k == TILES - 1)
                        op.then_inc(s_summed, 1)

                    for step in range(TILES + 2):
                        if step < TILES:
                            score(step)
                        if 1 <= step <= TILES:
                            turn(step - 1)
                        if step >= 2:
                            weigh(step - 2)

                @block.scalar
                def _(act):
                    for i in range(XT):
                        d, n = i % DIM_TILES, i // DIM_TILES
                        act.wait_ge(s_xt, i + 1)
                        nc.scalar.copy(xt_high[:, d, n * BANK:(n + 1) * BANK], bank[i][:]).then_inc(s_xt_high, 1)
                    for i in range(PB):
                        act.wait_ge(s_product, i + 1)
                        if i < QB:
                            d, n = i % DIM_TILES, i // DIM_TILES
                            to = q_high[:, d, n * BANK:(n + 1) * BANK]
                        else:
                            to = v_high[:, 2 * (i - QB):2 * (i - QB) + 2, :].rearrange("p t d -> p (t d)")
                        nc.scalar.copy(to, bank[i % 4][:]).then_inc(s_high, 1)
                    for step in range(TILES + 1):
                        if step < TILES:
                            act.wait_ge(s_min, step + 1)
                            nc.scalar.activation(probs[:, step % 3, :], probs[:, step % 3, :], ACT.Exp,
                                                 bias=row_min[:, step:step + 1], scale=-1.0,
                                                 accum_out=row_sum[:, step:step + 1]).then_inc(s_probs, 1)
                        if step >= 1:
                            i = step - 1
                            for half in range(2):
                                n = 2 * i + half
                                act.wait_ge(s_turned, n + 1)
                                if i >= 2:
                                    act.wait_ge(s_summed, i - 1)
                                nc.scalar.copy(
                                    probs_t_high[:, i % 2, 4 * half:4 * half + 4, :].rearrange("p k q -> p (k q)"),
                                    turned[n % 2][:]).then_inc(s_turned_high, 1)

                @block.vector
                def _(dve):
                    for i in range(XT):
                        d, n = i % DIM_TILES, i // DIM_TILES
                        cols = slice(n * BANK, (n + 1) * BANK)
                        dve.wait_ge(s_xt_high, i + 1)
                        nc.vector.tensor_tensor(xt_low[:, d, cols], bank[i][:], xt_high[:, d, cols].bitcast(F32),
                                                ALU.subtract).then_inc(s_xt_low, 1)
                    for i in range(PB):
                        dve.wait_ge(s_high, i + 1)
                        if i < QB:
                            d, n = i % DIM_TILES, i // DIM_TILES
                            cols = slice(n * BANK, (n + 1) * BANK)
                            to, of = q_low[:, d, cols], q_high[:, d, cols]
                        else:
                            rows = slice(2 * (i - QB), 2 * (i - QB) + 2)
                            to = v_low[:, rows, :].rearrange("p t d -> p (t d)")
                            of = v_high[:, rows, :].rearrange("p t d -> p (t d)")
                        nc.vector.tensor_tensor(to, bank[i % 4][:], of.bitcast(F32), ALU.subtract).then_inc(s_low, 1)
                    for step in range(TILES + 3):
                        if step < TILES:
                            dve.wait_ge(s_scores, step + 1)
                            dve.wait_ge(s_penalty, step + 1)
                            if step >= 3:
                                dve.wait_ge(s_turned, 2 * (step - 2))
                            for n in range(HALVES):
                                cols = slice(n * BANK, (n + 1) * BANK)
                                nc.vector.tensor_tensor_reduce(
                                    out=probs[:, step % 3, cols], in0=bank[2 * (step % 2) + n][:],
                                    in1=penalty[:, step % 2, cols], scale=1.0,
                                    scalar=3.0e38 if n == 0 else row_min[:, step:step + 1], op0=ALU.add, op1=ALU.min,
                                    accum_out=row_min[:, step:step + 1]).then_inc(s_first_min if n == 0 else s_min, 1)
                                if n == 0:
                                    dve.wait_ge(s_first_min, step + 1)
                        if 1 <= step <= TILES:
                            i = step - 1
                            for half in range(2):
                                n = 2 * i + half
                                dve.wait_ge(s_turned_high, n + 1)
                                part = slice(4 * half, 4 * half + 4)
                                nc.vector.tensor_tensor(
                                    probs_t_low[:, i % 2, part, :].rearrange("p k q -> p (k q)"), turned[n % 2][:],
                                    probs_t_high[:, i % 2, part, :].rearrange("p k q -> p (k q)").bitcast(F32),
                                    ALU.subtract).then_inc(s_turned_low, 1)
                            dve.wait_ge(s_probs, i + 1)
                            nc.vector.reciprocal(inverse[:, i:i + 1], row_sum[:, i:i + 1]).then_inc(s_inverse, 1)
                        if step >= 3:
                            i = step - 3
                            dve.wait_ge(s_deviation, i + 1)
                            center_and_scale(nc, result[:, i, :], result[:, i, :], moments[:, i, :]
                                             ).then_inc(s_normed, 1)
                        if 2 <= step < TILES + 2:
                            i = step - 2
                            dve.wait_ge(s_summed, i + 1)
                            dve.wait_ge(s_inverse, i + 1)
                            dve.wait_ge(s_residual, i + 1)
                            nc.vector.scalar_tensor_tensor(result[:, i, :], summed[i % 2][:], inverse[:, i:i + 1],
                                                           x_sb[:, i, :], ALU.mult, ALU.add).then_inc(s_sum, 1)
                            dve.wait_ge(s_sum, i + 1)
                            tile_moments(nc, dve, result[:, i, :], stats[:, i, :], moments[:, i, :], s_stats, i,
                                         s_moments)

            m.clear()


def graph_layers(nc, a, out):
    def scratch(name):
        return nc.dram_tensor(name, [BATCH, SEQ, DIM], F32).ap()

    attended, after_0, after_1, after_2 = (scratch(n) for n in ("attended", "after_0", "after_1", "after_2"))
    adj, ident = a["adj"], a["ident"]
    w0 = {k: a["L0_gnn_" + k] for k in ("wq", "wk", "wv", "wo", "bq", "bk", "bv", "bo")}
    multi_head_layer(nc, "l0", a["x"], adj, ident, w0 | {"g": a["L0_gnn_ln1_g"], "b": a["L0_gnn_ln1_b"]}, attended,
                     True)
    mlp_layer(nc, "mlp", attended, ident,
              {k: a["L0_gnn_" + k] for k in ("w1", "b1", "w2", "b2")} |
              {"g": a["L0_gnn_ln2_g"], "b": a["L0_gnn_ln2_b"]}, after_0)
    for n, source, target in ((1, after_0, after_1), (2, after_1, after_2)):
        single_head_layer(nc, f"l{n}", source, adj, ident,
                          {"wq_t": a[f"L{n}_gnn_Wq_t"], "wk_t": a[f"L{n}_gnn_Wk_t"], "wv_t": a[f"L{n}_gnn_Wv_t"],
                           "wo": a[f"L{n}_gnn_Wo"], "bo": a[f"L{n}_gnn_bo"], "g": a[f"L{n}_gnn_gamma"],
                           "b": a[f"L{n}_gnn_beta"]}, target)
    w3 = {k.lower(): a["L3_gnn_" + k] for k in ("Wq", "Wk", "Wv", "Wo", "bq", "bk", "bv", "bo")}
    multi_head_layer(nc, "l3", after_2, adj, ident, w3 | {"g": a["L3_gnn_gamma"], "b": a["L3_gnn_beta"]}, out, False)


def kernel(**inputs):
    import numpy as np
    import concourse.bacc as bacc
    from concourse.bass_utils import run_bass_kernel_spmd

    nc = bacc.Bacc("TRN2", target_bir_lowering=False, num_devices=1)
    turned = {f"L{n}_gnn_{w}" for n in (1, 2) for w in ("Wq", "Wk", "Wv")}
    arrays = {}
    for name, value in inputs.items():
        value = np.asarray(value)
        if name in turned:
            name, value = name + "_t", value.T
        arrays[name] = np.ascontiguousarray(value)
    arrays["ident"] = np.eye(P, dtype=np.float32)
    drams = {name: nc.dram_tensor(name, value.shape, mybir.dt.from_np(value.dtype), kind="ExternalInput").ap()
             for name, value in arrays.items()}
    out = nc.dram_tensor("hidden_out", (BATCH, SEQ, DIM), F32, kind="ExternalOutput").ap()
    graph_layers(nc, drams, out)
    r = run_bass_kernel_spmd(nc, [arrays], core_ids=[0])
    return r.results[0]["hidden_out"]
```

```python
from contextlib import ExitStack

import concourse.bass as bass
from concourse import mybir

F32 = mybir.dt.float32
F32R = mybir.dt.float32r
I32 = mybir.dt.int32
ALU = mybir.AluOpType
ACT = mybir.ActivationFunctionType

P = 128
BATCH, SEQ, DIM = 8, 1024, 256
HEADS = 8
HEAD_DIM = DIM // HEADS
HIDDEN = 4 * DIM
TILES = SEQ // P
DIM_TILES = DIM // P
GROUP = P // HEAD_DIM
GROUPS = HEADS // GROUP
STACK = 3 * HEAD_DIM
BANK = 512
HALVES = SEQ // BANK
PENALTY = 1.0e30
MASK = 1.0e28
EPS = 1e-5
SPAN = 4
STATS = 6


class Pool:

    def __init__(self, nc, ctx, tag):
        self.nc, self.ctx, self.tag = nc, ctx, tag
        self.sems = []

    def sb(self, name, shape, dtype=F32):
        return self.ctx.enter_context(self.nc.sbuf_tensor(f"{self.tag}_{name}", shape, dtype))

    def ps(self, name, shape):
        return self.ctx.enter_context(self.nc.psum_tensor(f"{self.tag}_{name}", shape, F32))

    def sem(self, name):
        s = self.ctx.enter_context(self.nc.semaphore(f"{self.tag}_{name}"))
        self.sems.append(s)
        return s

    def clear(self):
        for s in self.sems:
            self.nc.gpsimd.sem_clear(s)
        self.nc.all_engine_barrier()


def of_batch(dram, b):
    return dram[bass.ds(b, 1)].rearrange("a s n -> (a s) n")


def split_matmul(nc, out, lhs_high, lhs_low, rhs_high, rhs_low, start, stop):
    nc.tensor.matmul(out, lhs_high, rhs_high, start=start, stop=False)
    nc.tensor.matmul(out, lhs_high, rhs_low, start=False, stop=False)
    return nc.tensor.matmul(out, lhs_low, rhs_high, start=False, stop=stop)


def split_weights(nc, weights, tag):
    def scaled(n):
        return sum(w[3] is not None for w in weights[:n])

    with ExitStack() as ctx:
        m = Pool(nc, ctx, tag)
        s_scaled, s_high, s_low = m.sem("scaled"), m.sem("high"), m.sem("low")
        with nc.Block() as block:

            @block.vector
            def _(dve):
                for raw, _, _, factor, gain in weights:
                    if factor is None:
                        continue
                    for k in range(raw.shape[1]):
                        if gain is None:
                            op = nc.vector.tensor_scalar(raw[:, k, :], raw[:, k, :], factor, None, ALU.mult)
                        else:
                            op = nc.vector.tensor_scalar(raw[:, k, :], raw[:, k, :], gain[:, k:k + 1], factor,
                                                         ALU.mult, ALU.mult)
                    op.then_inc(s_scaled, 1)
                dve.wait_ge(s_scaled, scaled(len(weights)))
                for n, (raw, high, low, _, _) in enumerate(weights):
                    dve.wait_ge(s_high, n + 1)
                    nc.vector.tensor_tensor(low, raw, high.bitcast(F32), ALU.subtract).then_inc(s_low, 1)
                dve.wait_ge(s_low, len(weights))

            @block.scalar
            def _(act):
                for n, (raw, high, _, factor, _) in enumerate(weights):
                    if factor is not None:
                        act.wait_ge(s_scaled, scaled(n + 1))
                    nc.scalar.copy(high, raw).then_inc(s_high, 1)
                act.wait_ge(s_high, len(weights))

        m.clear()


def load_all(nc, pairs, tag):
    with ExitStack() as ctx:
        m = Pool(nc, ctx, tag)
        s_loaded = m.sem("loaded")
        with nc.Block() as block:

            @block.sync
            def _(sp):
                for destination, source in pairs:
                    sp.dma_start(destination, source, allow_slow_non_contiguous=True).then_inc(s_loaded, 16)
                sp.wait_ge(s_loaded, 16 * len(pairs))

        m.clear()


def matrix(dram):
    return dram.rearrange("(k p) n -> p k n", p=P)


def matrices(dram):
    return dram.rearrange("w (k p) n -> p (w k) n", p=P)


def column(dram):
    return dram.rearrange("(k p) -> p k", p=P)


def spread(dram):
    return dram.rearrange("(a n) -> a n", a=1).partition_broadcast(P)


def fold_shift(nc, shift, columns, rows, tag):
    with ExitStack() as ctx:
        m = Pool(nc, ctx, tag)
        spread_shift = m.sb("spread_shift", [P, DIM_TILES, P])
        ones = m.sb("ones", [P, P])
        col = m.ps("col", [P, BANK])
        row = [m.ps(f"row{n}", [P, DIM]) for n in range(len(rows))]
        s_ones, s_spread, s_product, s_added = m.sem("ones"), m.sem("spread"), m.sem("product"), m.sem("added")
        with nc.Block() as block:

            @block.vector
            def _(dve):
                if rows:
                    nc.vector.memset(ones[:], 1.0).then_inc(s_ones, 1)
                    dve.wait_ge(s_ones, 1)
                    for k in range(DIM_TILES):
                        nc.vector.tensor_scalar(spread_shift[:, k, :], ones[:], shift[:, k:k + 1], None,
                                                ALU.mult).then_inc(s_spread, 1)
                dve.wait_ge(s_product, 1)
                at = 0
                for _, bias in columns:
                    w = bias.shape[1]
                    nc.vector.tensor_tensor(bias[:, :], bias[:, :], col[:, at:at + w], ALU.add).then_inc(s_added, 1)
                    at += w
                for n, (_, bias) in enumerate(rows):
                    nc.vector.tensor_tensor(bias[:], bias[:], row[n][:], ALU.add).then_inc(s_added, 1)
                dve.wait_ge(s_added, len(columns) + len(rows))

            @block.tensor
            def _(pe):
                if rows:
                    pe.wait_ge(s_spread, DIM_TILES)
                at = 0
                for raw, bias in columns:
                    for j in range(bias.shape[1]):
                        for k in range(DIM_TILES):
                            op = nc.tensor.matmul(col[:, at:at + 1], raw[:, k, j * P:(j + 1) * P], shift[:, k:k + 1],
                                                  start=(k == 0), stop=(k == DIM_TILES - 1))
                        at += 1
                for n, (raw, _) in enumerate(rows):
                    for k in range(DIM_TILES):
                        op = nc.tensor.matmul(row[n][:], spread_shift[:, k, :], raw[:, k, :],
                                              start=(k == 0), stop=(k == DIM_TILES - 1))
                op.then_inc(s_product, 1)

        m.clear()


def tile_moments(nc, dve, source, stats, moments, s_stats, i, s_moments):
    nc.vector.bn_stats(stats, source).then_inc(s_stats, 1)
    dve.wait_ge(s_stats, i + 1)
    nc.vector.bn_aggr(moments, stats).then_inc(s_moments, 1)


def inverse_deviation(nc, pool, variance, exponent, s_shifted, i, s_deviation):
    nc.gpsimd.tensor_scalar(variance, variance, EPS, None, ALU.add).then_inc(s_shifted, 1)
    pool.wait_ge(s_shifted, i + 1)
    nc.gpsimd.tensor_tensor(variance, variance, exponent, ALU.pow).then_inc(s_deviation, 1)


def center_and_scale(nc, out, source, moments):
    return nc.vector.tensor_scalar(out, source, moments[:, 0:1], moments[:, 1:2], ALU.subtract, ALU.mult)


def center_and_gain(nc, out, source, moments, gamma):
    return nc.vector.scalar_tensor_tensor(out, source, moments[:, 0:1], gamma, ALU.subtract, ALU.mult)


def scale_and_shift(nc, out, source, moments, beta):
    return nc.vector.scalar_tensor_tensor(out, source, moments[:, 1:2], beta, ALU.mult, ALU.add)


def fill(nc, tile, value, tag):
    with ExitStack() as ctx:
        m = Pool(nc, ctx, tag)
        s_filled = m.sem("filled")
        with nc.Block() as block:

            @block.gpsimd
            def _(pool):
                nc.gpsimd.memset(tile, value).then_inc(s_filled, 1)
                pool.wait_ge(s_filled, 1)

        m.clear()



ITEMS = TILES * HEADS
GROUP_ITEMS = ITEMS // GROUPS
RING = 3
TURN_LAG = 2
VALUE_LAG = 6
LATE = 16
EARLY = TILES // 2
MOVES = 3 * GROUP
INPUT_RING = 3

BLOCKS = [("k", 0), ("k", 1), ("q", 0), ("q", 1)]
SIDE = {step: ("block", n) for n, step in enumerate((0, 3, 8, 11))}
SIDE |= {step: ("value", n) for n, step in enumerate((7, 10))}
TURN_STEP = 17
SIDE |= {TURN_STEP + 2 * t: ("turn", t) for t in range(TILES)}
SIDE |= {GROUP_ITEMS + step: ("block", 4 + n) for n, step in enumerate((1, 3, 9, 11))}
SIDE |= {GROUP_ITEMS + step: ("value", 2 + n) for n, step in enumerate((6, 12))}
FACTOR_STEP = GROUP_ITEMS + VALUE_LAG + GROUP
SIDE |= {FACTOR_STEP + 4 * t: ("factor", t) for t in range(TILES)}
SIDE |= {FACTOR_STEP + 3 + 4 * t: ("output", t) for t in range(TILES)}


def on_act(n):
    return n % 2 == 0 or n % 4 == 3


def halves_on_act(n):
    return sum(on_act(i) for i in range(n))


def place(item):
    group, rest = divmod(item % ITEMS, GROUP_ITEMS)
    return rest // GROUP, group * GROUP + rest % GROUP


def multi_head_layer(nc, tag, x_dram, adj_dram, ident_dram, w, out_dram, pre_norm):
    scale = float(HEAD_DIM) ** -0.5
    OUT_RING = 2 if pre_norm else 4
    with ExitStack() as ctx:
        m = Pool(nc, ctx, tag)
        ident = m.sb("ident", [P, P])
        names = ["q", "k", "v", "o"]
        high = {n: m.sb(f"w{n}_high", [P, DIM_TILES, DIM], F32R) for n in names}
        low = {n: m.sb(f"w{n}_low", [P, DIM_TILES, DIM], F32R) for n in names}
        columns = m.sb("columns", [P, (5 if pre_norm else 3) * DIM_TILES])
        spreads = m.sb("spreads", [P, 1 if pre_norm else 3, DIM])
        bias_q, bias_k, bias_v = (columns[:, i * DIM_TILES:(i + 1) * DIM_TILES] for i in range(3))
        bias_o = spreads[:, 0, :]
        exponent = m.sb("exponent", [P, 1])
        fill(nc, exponent[:], -0.5, tag + "_exponent")
        if not pre_norm:
            gamma, beta = spreads[:, 1, :], spreads[:, 2, :]

        with ExitStack() as prep:
            t = Pool(nc, prep, tag + "_prep")
            raw_all = t.sb("raw", [P, len(names) * DIM_TILES, DIM])
            raw = {n: raw_all[:, i * DIM_TILES:(i + 1) * DIM_TILES, :] for i, n in enumerate(names)}
            load_all(nc, [(columns[:], column(w["columns"])), (raw_all[:], matrices(w["matrices"])),
                          (ident[:], ident_dram), (spreads[:].rearrange("p v n -> p (v n)"), spread(w["spreads"]))],
                     tag + "_load")
            gain = None
            if pre_norm:
                gain, shift = (columns[:, i * DIM_TILES:(i + 1) * DIM_TILES] for i in (3, 4))
            if pre_norm:
                fold_shift(nc, shift, [(raw["q"], bias_q), (raw["k"], bias_k), (raw["v"], bias_v)], [],
                           tag + "_fold")
            fold_shift(nc, bias_v, [], [(raw["o"], bias_o)], tag + "_fold_v")
            split_weights(nc, [(raw[n], high[n][:], low[n][:],
                                -scale if n == "q" else 1.0 if pre_norm and n != "o" else None,
                                gain if n != "o" else None) for n in names], tag + "_split")
            s_bias = t.sem("bias")
            with nc.Block() as block:

                @block.vector
                def _(dve):
                    nc.vector.tensor_scalar(bias_q, bias_q, -scale, None, ALU.mult).then_inc(s_bias, 1)
                    dve.wait_ge(s_bias, 1)

            t.clear()

        q_stack = m.sb("q_stack", [P, HEADS, SEQ], F32R)
        k_stack = m.sb("k_stack", [P, HEADS, SEQ], F32R)
        part_high, part_low = (m.sb(f"part_{s}", [P, 2, BANK], F32R) for s in ("high", "low"))
        xt_high, xt_low = (m.sb(f"xt_{s}", [P, DIM_TILES, SEQ], F32R) for s in ("high", "low"))
        values = m.sb("values", [P, GROUPS, TILES, P])
        penalty = m.sb("penalty", [P, TILES, SEQ])
        x_in = m.sb("x_in", [P, INPUT_RING, DIM])
        probs = m.sb("probs", [P, RING, SEQ])
        probs_t = m.sb("probs_t", [P, 2, TILES, GROUP, P])
        row_min, row_sum = m.sb("row_min", [P, HEADS]), m.sb("row_sum", [P, TILES, HEADS])
        inverse = m.sb("inverse", [P, GROUPS, P])
        heads_0, heads_1 = m.sb("heads_0", [P, TILES, P]), m.sb("heads_1", [P, 2, P])
        heads_high, heads_low = (m.sb(f"heads_{s}", [P, GROUPS, P], F32R) for s in ("high", "low"))
        rows = m.sb("rows", [P, OUT_RING, DIM])
        stats = m.sb("stats", [P, TILES, STATS])
        moments = m.sb("moments", [P, TILES, 2])
        if pre_norm:
            edge, mask = m.sb("edge", [P, SEQ]), m.sb("mask", [P, 1])
            fill(nc, mask[:], MASK, tag + "_mask")
        scores = [m.ps(f"scores{i}", [P, SEQ]) for i in range(2)]
        turned = [m.ps(f"turned{i}", [P, BANK]) for i in range(2)]
        summed = m.ps("summed", [P, P])
        side = m.ps("side", [P, BANK])

        s_scores, s_min, s_probs = m.sem("scores"), m.sem("min"), m.sem("probs")
        s_turned, s_copied_act, s_copied_dve = m.sem("turned"), m.sem("copied_act"), m.sem("copied_dve")
        s_summed, s_heads, s_inverse = m.sem("summed"), m.sem("heads"), m.sem("inverse")
        s_reciprocal = m.sem("reciprocal")
        s_side, s_rounded, s_side_free = m.sem("side"), m.sem("rounded"), m.sem("side_free")
        s_moved = m.sem("moved")
        s_x = [m.sem(f"x{i}") for i in range(INPUT_RING)]
        s_adj = [m.sem(f"adj{i}") for i in range(EARLY)]
        s_penalty, s_value, s_squared, s_edge, s_mask = (m.sem("penalty"), m.sem("value"), m.sem("squared"),
                                                        m.sem("edge"), m.sem("mask"))
        s_stats, s_moments, s_shifted, s_deviation = (m.sem("stats"), m.sem("moments"), m.sem("shifted"),
                                                      m.sem("deviation"))
        s_normed = m.sem("normed")
        s_heads_high, s_heads_low = m.sem("heads_high"), m.sem("heads_low")
        s_rows = [m.sem(f"rows{i}") for i in range(OUT_RING)]
        s_residual, s_gained, s_result = m.sem("residual"), m.sem("gained"), m.sem("result")
        s_out = [m.sem(f"out{i}") for i in range(OUT_RING)]

        def iteration(graphs, b_next, attend):
            successors = [*graphs[1:], b_next] if attend else [b_next]
            rounds = len(successors)
            items = ITEMS * rounds if attend else 0
            units = items // GROUP
            steps = ITEMS * rounds + VALUE_LAG + 2 * GROUP
            kinds = {s: v for s, v in SIDE.items()
                     if attend or v[0] == "turn" or (v[0] == "block" and v[1] >= 4) or (v[0] == "value" and v[1] >= 2)}
            per_graph = {"block": 8, "value": 4, "turn": TILES, "factor": TILES, "output": TILES}
            work = {s + ITEMS * g: (what, n + per_graph[what] * g)
                    for g in range(rounds) for s, (what, n) in kinds.items()}
            order = sorted(work)
            index = {work[s]: n for n, s in enumerate(order)}
            first_block = 0 if attend else 4

            penalty_at = {}
            for g in range(rounds):
                if attend:
                    penalty_at |= {ITEMS * g + 3 + 3 * n: (g, EARLY + n, False) for n in range(TILES - EARLY)}
                first = GROUP_ITEMS + 7 if attend else TURN_STEP + 2 * TILES - 4
                penalty_at |= {ITEMS * g + first + 4 * t: (g, t, True) for t in range(EARLY)}
            penalty_order = [penalty_at[s] for s in sorted(penalty_at)]

            def tile_at(step, first, every, condition=True):
                for g in range(rounds):
                    t, part = divmod(step - ITEMS * g - first, every)
                    if condition and part == 0 and 0 <= t < TILES:
                        return TILES * g + t
                return None

            side_banks = [side] if attend else [side, *turned]

            def side_bank(what, n):
                return side_banks[index[what, n] % len(side_banks)]

            def block_parts(n):
                if attend or BLOCKS[n % 4][0] == "k":
                    return part_high, part_low
                return tuple(probs[:, i, :].bitcast(F32R).rearrange("p (n c) -> p n c", c=BANK) for i in range(2))

            def rounded_before(what):
                return sum(work[s][0] in ("block", "turn") for s in order[:index[what]])

            def tiled(dram, b):
                return of_batch(dram, b).rearrange("(t p) d -> p t d", p=P)

            def of_block(n):
                which, half = BLOCKS[n % 4]
                return which, half, 1 if n % 8 < 4 else 0

            with nc.Block() as block:

                @block.sync
                def _(sp):
                    def load_x(n):
                        g, t = divmod(n, TILES)
                        sp.dma_start(x_in[:, n % INPUT_RING, :], tiled(x_dram, successors[g])[:, t, :]
                                     ).then_inc(s_x[n % INPUT_RING], 16)

                    def load_adj(g, t, ahead):
                        source = tiled(adj_dram, successors[g] if ahead else graphs[g])
                        sp.dma_start(penalty[:, t, :].bitcast(I32), source[:, t, :]).then_inc(s_adj[t % EARLY], 16)

                    def load_row(n):
                        g, t = divmod(n, TILES)
                        sp.dma_start(rows[:, n % OUT_RING, :], tiled(x_dram, graphs[g])[:, t, :]
                                     ).then_inc(s_rows[n % OUT_RING], 16)

                    for n in range(INPUT_RING):
                        load_x(n)
                    for step in range(steps + LATE):
                        g, s = divmod(step, ITEMS)
                        if attend and g < rounds and s < TILES - EARLY:
                            if g:
                                sp.wait_ge(s_min, ITEMS * (g - 1) + GROUP_ITEMS + GROUP * (EARLY + s + 1))
                            load_adj(g, EARLY + s, False)
                        what, n = work.get(step - 1, (None, 0))
                        if what == "block" and n % HALVES == HALVES - 1:
                            which, _, group = of_block(n)
                            p_high, p_low = block_parts(n)
                            stack, parts = ((k_stack, (p_high, p_low, p_high)) if which == "k" else
                                            (q_stack, (p_high, p_high, p_low)))
                            sp.wait_ge(s_side_free, index["block", n] + 1)
                            if attend and n % 4 == 1 and n > 1:
                                sp.wait_ge(s_scores, ITEMS * (n // 8) + (GROUP_ITEMS if group == 0 else 0))
                            for j in range(GROUP):
                                head = GROUP * group + j
                                for s, part in enumerate(parts):
                                    sp.dma_start(stack[s * HEAD_DIM:(s + 1) * HEAD_DIM, head, :].bitcast(F32),
                                                 part[j * HEAD_DIM:(j + 1) * HEAD_DIM].rearrange(
                                                     "p n c -> p (n c)").bitcast(F32)).then_inc(s_moved, 16)
                        if what == "turn" and n + INPUT_RING < TILES * rounds:
                            sp.wait_ge(s_side, index["turn", n] + 1)
                            load_x(n + INPUT_RING)
                        n = tile_at(step, GROUP_ITEMS + 4 if attend else TURN_STEP, 4)
                        if n is not None and n % TILES < EARLY:
                            g, t = divmod(n, TILES)
                            if attend:
                                sp.wait_ge(s_min, ITEMS * g + GROUP_ITEMS + GROUP * (t + 1))
                            load_adj(g, t, True)
                        n = tile_at(step, FACTOR_STEP - 10, 1, attend)
                        if n is not None and n % TILES < OUT_RING:
                            if n >= OUT_RING:
                                sp.wait_ge(s_out[n % OUT_RING], 16 * (n // OUT_RING))
                            load_row(n)
                        n = tile_at(step, FACTOR_STEP - 2, 4, attend)
                        if n is not None and n % TILES >= OUT_RING:
                            sp.wait_ge(s_out[n % OUT_RING], 16 * (n // OUT_RING))
                            load_row(n)
                        n = tile_at(step, FACTOR_STEP + (5 if pre_norm else 9), 4, attend)
                        if n is not None:
                            g, t = divmod(n, TILES)
                            if pre_norm:
                                sp.wait_ge(s_side_free, index["output", n] + 1)
                            else:
                                sp.wait_ge(s_result, n + 1)
                            sp.dma_start(tiled(out_dram, graphs[g])[:, t, :], rows[:, n % OUT_RING, :]
                                         ).then_inc(s_out[n % OUT_RING], 16)
                    if attend:
                        for i in range(OUT_RING):
                            sp.wait_ge(s_out[i], 16 * (TILES * rounds // OUT_RING))
                    sp.wait_ge(s_moved, 16 * MOVES * (8 * rounds - first_block) // 2)

                @block.gpsimd
                def _(pool):
                    def make_penalty(which):
                        n = penalty_order.index(which)
                        _, t, _ = which
                        adj = penalty[:, t, :].bitcast(I32)
                        loads_before = sum(other[1] % EARLY == t % EARLY for other in penalty_order[:n])
                        pool.wait_ge(s_adj[t % EARLY], 16 * (loads_before + 1))
                        if pre_norm:
                            if n:
                                pool.wait_ge(s_penalty, n)
                            nc.gpsimd.tensor_scalar(edge[:], adj, 1.0, 0.0, ALU.mult, ALU.add).then_inc(s_value, 1)
                            pool.wait_ge(s_value, n + 1)
                            nc.gpsimd.tensor_tensor(edge[:], edge[:], edge[:], ALU.mult).then_inc(s_squared, 1)
                            pool.wait_ge(s_squared, n + 1)
                            nc.gpsimd.tensor_scalar(edge[:], edge[:], -0.1, 0.0, ALU.mult, ALU.add).then_inc(s_edge, 1)
                            pool.wait_ge(s_edge, n + 1)
                            pool.wait_ge(s_mask, n + 1)
                            nc.gpsimd.tensor_tensor(penalty[:, t, :], penalty[:, t, :], edge[:],
                                                    ALU.add).then_inc(s_penalty, 1)
                        else:
                            nc.gpsimd.tensor_scalar(penalty[:, t, :], adj, 0.0, PENALTY, ALU.is_equal,
                                                    ALU.mult).then_inc(s_penalty, 1)

                    for step in range(steps + LATE):
                        n = tile_at(step, TURN_STEP - 3, 2, pre_norm)
                        if n is not None:
                            pool.wait_ge(s_moments, n + 1)
                            inverse_deviation(nc, pool, moments[:, n % TILES, 1:2], exponent[:], s_shifted, n,
                                              s_deviation)
                        n = tile_at(step, FACTOR_STEP, 4, attend)
                        if n is not None:
                            row = rows[:, n % OUT_RING, :]
                            pool.wait_ge(s_rows[n % OUT_RING], 16 * (n // OUT_RING + 1))
                            nc.gpsimd.tensor_tensor(row, row, bias_o, ALU.add).then_inc(s_residual, 1)
                        n = tile_at(step, FACTOR_STEP + 5, 4, attend and not pre_norm)
                        if n is not None:
                            pool.wait_ge(s_moments, n + 1)
                            inverse_deviation(nc, pool, moments[:, n % TILES, 1:2], exponent[:], s_shifted, n,
                                              s_deviation)
                        if step in penalty_at:
                            make_penalty(penalty_at[step])

                @block.tensor
                def _(pe):
                    for step in range(steps):
                        if step < items:
                            tile, head = place(step)
                            if step >= 2:
                                pe.wait_ge(s_min, step - 1)
                            if step and step % GROUP_ITEMS == 0:
                                pe.wait_ge(s_moved, 16 * MOVES * 2 * (step // GROUP_ITEMS))
                            for n in range(HALVES):
                                op = nc.tensor.matmul(scores[step % 2][:, n * BANK:(n + 1) * BANK],
                                                      q_stack[0:STACK, head, tile * P:(tile + 1) * P],
                                                      k_stack[0:STACK, head, n * BANK:(n + 1) * BANK],
                                                      start=True, stop=True)
                            op.then_inc(s_scores, 1)
                        item = step - TURN_LAG
                        if 0 <= item < items:
                            pe.wait_ge(s_probs, item + 1)
                            for half in range(2):
                                n = 2 * item + half
                                if n >= 2:
                                    if on_act(n - 2):
                                        pe.wait_ge(s_copied_act, halves_on_act(n - 1))
                                    else:
                                        pe.wait_ge(s_copied_dve, n - 1 - halves_on_act(n - 1))
                                for j in range(4):
                                    k = 4 * half + j
                                    op = nc.tensor.transpose(turned[n % 2][:, j * P:(j + 1) * P],
                                                             probs[:, item % RING, k * P:(k + 1) * P], ident[:])
                                op.then_inc(s_turned, 1)
                        unit, part = divmod(step - VALUE_LAG, GROUP)
                        if 0 <= unit < units:
                            group = unit // TILES % GROUPS
                            if part == 0:
                                n = 2 * GROUP * (unit + 1)
                                pe.wait_ge(s_copied_act, halves_on_act(n))
                                pe.wait_ge(s_copied_dve, n - halves_on_act(n))
                                if unit >= 1:
                                    pe.wait_ge(s_heads, unit)
                                if unit and unit % TILES == 0:
                                    pe.wait_ge(s_side_free, index["value", 2 * (unit // TILES) - 1] + 1)
                            for k in (2 * part, 2 * part + 1):
                                for j in range(GROUP):
                                    op = nc.tensor.matmul(summed[j * HEAD_DIM:(j + 1) * HEAD_DIM, :],
                                                          values[:, group, k, j * HEAD_DIM:(j + 1) * HEAD_DIM],
                                                          probs_t[:, unit % 2, k, j, :],
                                                          start=(k == 0), stop=(k == TILES - 1))
                            if part == GROUP - 1:
                                op.then_inc(s_summed, 1)
                        what, n = work.get(step, (None, 0))
                        if what is None:
                            continue
                        bank = side_bank(what, n)
                        if index[what, n] >= len(side_banks):
                            pe.wait_ge(s_side_free, index[what, n] - len(side_banks) + 1)
                        if not attend and what == "block" and n == first_block:
                            pe.wait_ge(s_side_free, index[what, n])
                        if what == "block":
                            which, half, group = of_block(n)
                            cols = slice(half * BANK, (half + 1) * BANK)
                            for k in range(DIM_TILES):
                                op = split_matmul(nc, bank[:], high[which][:, k, group * P:(group + 1) * P],
                                                  low[which][:, k, group * P:(group + 1) * P], xt_high[:, k, cols],
                                                  xt_low[:, k, cols], k == 0, k == DIM_TILES - 1)
                        if what == "value":
                            group = 1 if n % 4 < 2 else 0
                            for j in range(4):
                                tile = 4 * (n % 2) + j
                                for k in range(DIM_TILES):
                                    op = split_matmul(nc, bank[:, j * P:(j + 1) * P],
                                                      xt_high[:, k, tile * P:(tile + 1) * P],
                                                      xt_low[:, k, tile * P:(tile + 1) * P],
                                                      high["v"][:, k, group * P:(group + 1) * P],
                                                      low["v"][:, k, group * P:(group + 1) * P],
                                                      k == 0, k == DIM_TILES - 1)
                        if what == "turn":
                            if pre_norm:
                                pe.wait_ge(s_normed, n + 1)
                            else:
                                pe.wait_ge(s_x[n % INPUT_RING], 16 * (n // INPUT_RING + 1))
                            for k in range(DIM_TILES):
                                op = nc.tensor.transpose(bank[:, k * P:(k + 1) * P],
                                                         x_in[:, n % INPUT_RING, k * P:(k + 1) * P], ident[:])
                        if what == "factor":
                            pe.wait_ge(s_inverse, n + 1)
                            for g in range(GROUPS):
                                op = nc.tensor.transpose(bank[:, g * P:(g + 1) * P], inverse[:, g, :], ident[:])
                        if what == "output":
                            pe.wait_ge(s_heads_low, n + 1)
                            for g in range(GROUPS):
                                op = split_matmul(nc, bank[:, 0:DIM], heads_high[:, g, :], heads_low[:, g, :],
                                                  high["o"][:, g, :], low["o"][:, g, :], g == 0, g == GROUPS - 1)
                        op.then_inc(s_side, 1)

                def copy_half(eng, copy, n, sem):
                    item, half = n // 2, n % 2
                    unit = item // GROUP
                    eng.wait_ge(s_turned, n + 1)
                    if unit >= 2:
                        eng.wait_ge(s_summed, unit - 1)
                    copy(probs_t[:, unit % 2, 4 * half:4 * half + 4, item % GROUP, :],
                         turned[n % 2][:].rearrange("p (k q) -> p k q", q=P)).then_inc(sem, 1)

                def side_views(what, n, highs):
                    bank = side_bank(what, n)
                    if what == "block":
                        return block_parts(n)[0 if highs else 1][:, n % 2, :], bank[:]
                    xt, tile = xt_high if highs else xt_low, n % TILES
                    return xt[:, :, tile * P:(tile + 1) * P], bank[:, 0:DIM].rearrange("p (k q) -> p k q", q=P)

                def block_slots_free(eng, n):
                    if attend and n >= 2:
                        eng.wait_ge(s_moved, 16 * MOVES * (n // 2))

                @block.vector
                def _(dve):
                    for step in range(steps + LATE):
                        what, n = work.get(step - 1, (None, 0))
                        if what == "value":
                            group = 1 if n % 4 < 2 else 0
                            dve.wait_ge(s_side, index["value", n] + 1)
                            if attend and n and n % 2 == 0:
                                dve.wait_ge(s_summed, TILES * (n // 2))
                            nc.vector.tensor_copy(
                                values[:, group, 4 * (n % 2):4 * (n % 2) + 4, :].rearrange("p t d -> p (t d)"),
                                side_bank("value", n)[:]).then_inc(s_side_free, 1)
                        if what == "factor":
                            tile = n % TILES
                            dve.wait_ge(s_side, index["factor", n] + 1)
                            dve.wait_ge(s_heads, GROUPS * TILES * (n // TILES) + TILES + tile + 1)
                            nc.vector.tensor_tensor(heads_0[:, tile, :], heads_0[:, tile, :], side[:, 0:P], ALU.mult)
                            nc.vector.tensor_tensor(heads_1[:, tile % 2, :], heads_1[:, tile % 2, :],
                                                    side[:, P:2 * P], ALU.mult).then_inc(s_side_free, 1)
                        if what == "output":
                            row = rows[:, n % OUT_RING, :]
                            dve.wait_ge(s_side, index["output", n] + 1)
                            dve.wait_ge(s_residual, n + 1)
                            nc.vector.tensor_tensor(row, row, side[:, 0:DIM], ALU.add).then_inc(s_side_free, 1)
                        if step < items:
                            tile, head = place(step)
                            g, s = divmod(step, ITEMS)
                            dve.wait_ge(s_scores, step + 1)
                            if s < GROUP_ITEMS and s % GROUP == 0 and (g or tile >= EARLY):
                                ready = (g, tile, False) if tile >= EARLY else (g - 1, tile, True)
                                dve.wait_ge(s_penalty, penalty_order.index(ready) + 1)
                            if step >= RING:
                                dve.wait_ge(s_turned, 2 * (step - RING + 1))
                            nc.vector.tensor_tensor_reduce(
                                out=probs[:, step % RING, :], in0=scores[step % 2][:], in1=penalty[:, tile, :],
                                scale=1.0, scalar=3.0e38, op0=ALU.add, op1=ALU.min,
                                accum_out=row_min[:, head:head + 1]).then_inc(s_min, 1)
                        what, n = work.get(step - 1, (None, 0))
                        if what in ("block", "turn"):
                            dve.wait_ge(s_rounded, rounded_before((what, n)) + 1)
                            to, source = side_views(what, n, False)
                            of, _ = side_views(what, n, True)
                            if what == "block":
                                block_slots_free(dve, n)
                                which, _, group = of_block(n)
                                bias = bias_k if which == "k" else bias_q
                                nc.vector.scalar_tensor_tensor(to, source, bias[:, group:group + 1], of.bitcast(F32),
                                                               ALU.add, ALU.subtract).then_inc(s_side_free, 1)
                            else:
                                nc.vector.tensor_tensor(to, source, of.bitcast(F32),
                                                        ALU.subtract).then_inc(s_side_free, 1)
                        item = step - TURN_LAG
                        if 0 <= item < items:
                            for half in (2 * item, 2 * item + 1):
                                if not on_act(half):
                                    copy_half(dve, nc.vector.tensor_copy, half, s_copied_dve)
                        what, n = work.get(step - 2, (None, 0))
                        if what == "factor":
                            tile = n % TILES
                            dve.wait_ge(s_heads_high, n + 1)
                            nc.vector.tensor_tensor(heads_low[:, 0, :], heads_0[:, tile, :],
                                                    heads_high[:, 0, :].bitcast(F32), ALU.subtract)
                            nc.vector.tensor_tensor(heads_low[:, 1, :], heads_1[:, tile % 2, :],
                                                    heads_high[:, 1, :].bitcast(F32),
                                                    ALU.subtract).then_inc(s_heads_low, 1)
                        n = tile_at(step, FACTOR_STEP - 1, 4, attend)
                        if n is not None:
                            g, t = divmod(n, TILES)
                            dve.wait_ge(s_probs, ITEMS * g + GROUP_ITEMS + GROUP * (t + 1))
                            nc.vector.reciprocal(row_sum[:, t, :], row_sum[:, t, :]).then_inc(s_reciprocal, 1)
                            dve.wait_ge(s_reciprocal, n + 1)
                            if n:
                                dve.wait_ge(s_side, index["factor", n - 1] + 1)
                            nc.vector.tensor_copy(
                                inverse[:].rearrange("p g (h d) -> p g h d", d=HEAD_DIM),
                                row_sum[:, t, :].rearrange("p (g h) -> p g h", h=GROUP).unsqueeze(3)
                                .to_broadcast([P, GROUPS, GROUP, HEAD_DIM])).then_inc(s_inverse, 1)
                        n = tile_at(step, TURN_STEP - 4, 2, pre_norm)
                        if n is not None:
                            dve.wait_ge(s_x[n % INPUT_RING], 16 * (n // INPUT_RING + 1))
                            tile_moments(nc, dve, x_in[:, n % INPUT_RING, :], stats[:, n % TILES, :],
                                         moments[:, n % TILES, :], s_stats, n, s_moments)
                        n = tile_at(step, TURN_STEP - 1, 2, pre_norm)
                        if n is not None:
                            x = x_in[:, n % INPUT_RING, :]
                            dve.wait_ge(s_deviation, n + 1)
                            center_and_scale(nc, x, x, moments[:, n % TILES, :]).then_inc(s_normed, 1)
                        n = tile_at(step, FACTOR_STEP + 4, 4, attend and not pre_norm)
                        if n is not None:
                            dve.wait_ge(s_side_free, index["output", n] + 1)
                            tile_moments(nc, dve, rows[:, n % OUT_RING, :], stats[:, n % TILES, :],
                                         moments[:, n % TILES, :], s_stats, n, s_moments)
                        n = tile_at(step, FACTOR_STEP + 5, 4, attend and not pre_norm)
                        if n is not None:
                            row = rows[:, n % OUT_RING, :]
                            dve.wait_ge(s_moments, n + 1)
                            center_and_gain(nc, row, row, moments[:, n % TILES, :], gamma).then_inc(s_gained, 1)
                        n = tile_at(step, FACTOR_STEP + 7, 4, attend and not pre_norm)
                        if n is not None:
                            row = rows[:, n % OUT_RING, :]
                            dve.wait_ge(s_deviation, n + 1)
                            dve.wait_ge(s_gained, n + 1)
                            scale_and_shift(nc, row, row, moments[:, n % TILES, :], beta).then_inc(s_result, 1)

                @block.scalar
                def _(act):
                    for step in range(steps + LATE):
                        unit, part = divmod(step - VALUE_LAG - GROUP, GROUP)
                        if 0 <= unit < units and part == 0:
                            act.wait_ge(s_summed, unit + 1)
                            number, tile = divmod(unit, TILES)
                            g, group = divmod(number, GROUPS)
                            if group == 0 and g:
                                act.wait_ge(s_heads_low, TILES * (g - 1) + tile + 1)
                            if group == 1 and TILES * g + tile >= 2:
                                act.wait_ge(s_heads_low, TILES * g + tile - 1)
                            nc.scalar.copy(heads_0[:, tile, :] if group == 0 else heads_1[:, tile % 2, :],
                                           summed[:]).then_inc(s_heads, 1)
                        item = step - 1
                        if 0 <= item < items:
                            tile, head = place(item)
                            g, s = divmod(item, ITEMS)
                            act.wait_ge(s_min, item + 1)
                            if g and s < GROUP_ITEMS and s % GROUP == 0:
                                act.wait_ge(s_inverse, TILES * (g - 1) + tile + 1)
                            nc.scalar.activation(probs[:, item % RING, :], probs[:, item % RING, :], ACT.Exp,
                                                 bias=row_min[:, head:head + 1], scale=-1.0,
                                                 accum_out=row_sum[:, tile, head:head + 1]).then_inc(s_probs, 1)
                        what, n = work.get(step - 1, (None, 0))
                        if what in ("block", "turn"):
                            act.wait_ge(s_side, index[what, n] + 1)
                            to, source = side_views(what, n, True)
                            if what == "block":
                                block_slots_free(act, n)
                                which, _, group = of_block(n)
                                bias = bias_k if which == "k" else bias_q
                                nc.scalar.activation(to, source, ACT.Identity,
                                                     bias=bias[:, group:group + 1]).then_inc(s_rounded, 1)
                            else:
                                nc.scalar.copy(to, source).then_inc(s_rounded, 1)
                        if what == "factor":
                            act.wait_ge(s_side_free, index["factor", n] + 1)
                            if n:
                                act.wait_ge(s_side, index["output", n - 1] + 1)
                            nc.scalar.copy(heads_high[:, 0, :], heads_0[:, n % TILES, :])
                            nc.scalar.copy(heads_high[:, 1, :], heads_1[:, n % 2, :]).then_inc(s_heads_high, 1)
                        item = step - TURN_LAG
                        if 0 <= item < items:
                            for half in (2 * item, 2 * item + 1):
                                if on_act(half):
                                    copy_half(act, nc.scalar.copy, half, s_copied_act)
                        which = penalty_at.get(step - 2)
                        if pre_norm and which is not None:
                            t = which[1]
                            act.wait_ge(s_value, penalty_order.index(which) + 1)
                            nc.scalar.activation(penalty[:, t, :], penalty[:, t, :].bitcast(I32), ACT.Relu,
                                                 bias=mask[:], scale=-MASK).then_inc(s_mask, 1)

        iteration(None, 0, False)
        m.clear()
        with nc.Fori(0, BATCH // SPAN) as span:
            iteration([span * SPAN + g for g in range(SPAN)], (span * SPAN + SPAN) % BATCH, True)
            m.clear()



def mlp_layer(nc, tag, x_dram, ident_dram, w, out_dram):
    hid_tiles = HIDDEN // P
    with ExitStack() as ctx:
        m = Pool(nc, ctx, tag)
        ident = m.sb("ident", [P, P])
        w1_high, w1_low = (m.sb(f"w1_{s}", [P, DIM_TILES, HIDDEN], F32R) for s in ("high", "low"))
        w2_high, w2_low = (m.sb(f"w2_{s}", [P, hid_tiles, DIM], F32R) for s in ("high", "low"))
        columns = m.sb("columns", [P, 2 * DIM_TILES + hid_tiles])
        gain, shift, bias_1 = columns[:, 0:DIM_TILES], columns[:, DIM_TILES:2 * DIM_TILES], columns[:, 2 * DIM_TILES:]
        bias_2 = m.sb("bias_2", [P, DIM])
        with ExitStack() as prep:
            t = Pool(nc, prep, tag + "_prep")
            raw_1, raw_2 = t.sb("raw_1", [P, DIM_TILES, HIDDEN]), t.sb("raw_2", [P, hid_tiles, DIM])
            load_all(nc, [(columns[:], column(w["columns"])), (raw_1[:], matrix(w["w1"])),
                          (raw_2[:], matrix(w["w2"])), (ident[:], ident_dram), (bias_2[:], spread(w["b2"]))],
                     tag + "_load")
            fold_shift(nc, shift, [(raw_1, bias_1)], [], tag + "_fold")
            split_weights(nc, [(raw_1[:], w1_high[:], w1_low[:], 1.0, gain),
                               (raw_2[:], w2_high[:], w2_low[:], None, None)], tag + "_split")

        x_sb = m.sb("x", [P, 2, TILES, DIM])
        normed = m.sb("normed", [P, TILES, DIM])
        stats, moments = m.sb("stats", [P, TILES, STATS]), m.sb("moments", [P, TILES, 2])
        xt_high, xt_low = (m.sb(f"xt_{s}", [P, 2, DIM_TILES, SEQ], F32R) for s in ("high", "low"))
        act_full = m.sb("act_full", [P, 2, BANK])
        act_high, act_low = (m.sb(f"act_{s}", [P, hid_tiles, BANK], F32R) for s in ("high", "low"))
        turned = [m.ps(f"turned{i}", [P, BANK]) for i in range(2)]
        hidden = [m.ps(f"hidden{i}", [P, BANK]) for i in range(3)]
        projected = [m.ps(f"projected{i}", [P, DIM]) for i in range(3)]
        exponent = m.sb("exponent", [P, TILES])
        fill(nc, exponent[:], -0.5, tag + "_exponent")
        s_x, s_stats, s_normed, s_moments = m.sem("x"), m.sem("stats"), m.sem("normed"), m.sem("moments")
        s_shifted, s_deviation = m.sem("shifted"), m.sem("deviation")
        s_turned, s_turned_high, s_turned_low = m.sem("turned"), m.sem("turned_high"), m.sem("turned_low")
        s_hidden, s_gelu, s_high, s_low = m.sem("hidden"), m.sem("gelu"), m.sem("high"), m.sem("low")
        s_projected, s_sum, s_out, s_residual = m.sem("projected"), m.sem("sum"), m.sem("out"), m.sem("residual")

        TURNS = DIM_TILES * HALVES
        ROWS = BANK // P

        def iteration(graphs, b_next, attend):
            prepared = [*graphs[1:], b_next] if attend else [b_next]
            computed = range(SPAN if attend else 0)

            def parity(h):
                return (h + 1) % 2 if attend else 0

            def view(dram, b):
                return of_batch(dram, b).rearrange("(t p) d -> p t d", p=P)

            with nc.Block() as block:

                @block.sync
                def _(sp):
                    for h, b in enumerate(prepared):
                        if h:
                            sp.wait_ge(s_out, 16 * TILES * h)
                        sp.dma_start(x_sb[:, parity(h)], view(x_dram, b)).then_inc(s_x, 16)
                        if attend:
                            for i in range(TILES):
                                sp.wait_ge(s_sum, h * TILES + i + 1)
                                sp.dma_start(view(out_dram, graphs[h])[:, i, :], x_sb[:, h % 2, i, :]
                                             ).then_inc(s_out, 16)
                    if attend:
                        sp.wait_ge(s_out, 16 * TILES * SPAN)

                @block.gpsimd
                def _(pool):
                    for h in range(len(prepared)):
                        pool.wait_ge(s_moments, TILES * (h + 1))
                        inverse_deviation(nc, pool, moments[:, :, 1], exponent[:], s_shifted, h, s_deviation)
                        for i in range(TILES):
                            row = x_sb[:, parity(h), i, :]
                            pool.wait_ge(s_normed, h * TILES + i + 1)
                            nc.gpsimd.tensor_tensor(row, row, bias_2[:], ALU.add).then_inc(s_residual, 1)

                @block.tensor
                def _(pe):
                    def turn(h, k):
                        d, n, i = k % DIM_TILES, k // DIM_TILES, h * TURNS + k
                        pe.wait_ge(s_normed, h * TILES + 4 * n + 4)
                        if i >= 2:
                            pe.wait_ge(s_turned_low, i - 1)
                        for j in range(4):
                            op = nc.tensor.transpose(turned[i % 2][:, j * P:(j + 1) * P],
                                                     normed[:, 4 * n + j, d * P:(d + 1) * P], ident[:])
                        op.then_inc(s_turned, 1)

                    if not attend:
                        for k in range(TURNS):
                            turn(0, k)
                    for g in computed:
                        for n in range(HALVES):
                            cols = slice(n * BANK, (n + 1) * BANK)
                            if g and n == 0:
                                pe.wait_ge(s_turned_low, TURNS * g)
                            for f in range(hid_tiles):
                                i = (g * HALVES + n) * hid_tiles + f
                                if i >= 3:
                                    pe.wait_ge(s_gelu, i - 2)
                                for k in range(DIM_TILES):
                                    op = split_matmul(nc, hidden[i % 3][:], w1_high[:, k, f * P:(f + 1) * P],
                                                      w1_low[:, k, f * P:(f + 1) * P], xt_high[:, g % 2, k, cols],
                                                      xt_low[:, g % 2, k, cols], k == 0, k == DIM_TILES - 1)
                                op.then_inc(s_hidden, 1)
                            for j in range(ROWS):
                                if n == HALVES - 1:
                                    turn(g, j)
                                i = (g * HALVES + n) * ROWS + j
                                if i >= 3:
                                    pe.wait_ge(s_sum, i - 2)
                                for f in range(hid_tiles):
                                    if j == 0:
                                        pe.wait_ge(s_low, (g * HALVES + n) * hid_tiles + f + 1)
                                    op = split_matmul(nc, projected[i % 3][:], act_high[:, f, j * P:(j + 1) * P],
                                                      act_low[:, f, j * P:(j + 1) * P], w2_high[:, f, :],
                                                      w2_low[:, f, :], f == 0, f == hid_tiles - 1)
                                op.then_inc(s_projected, 1)

                def turned_view(xt, h, k):
                    d, n = k % DIM_TILES, k // DIM_TILES
                    return xt[:, parity(h), d, n * BANK:(n + 1) * BANK]

                @block.scalar
                def _(act):
                    def turned_to_high(h, k):
                        i = h * TURNS + k
                        act.wait_ge(s_turned, i + 1)
                        if h and k == 0:
                            act.wait_ge(s_hidden, HALVES * hid_tiles * h)
                        nc.scalar.copy(turned_view(xt_high, h, k), turned[i % 2][:]).then_inc(s_turned_high, 1)

                    if not attend:
                        for k in range(TURNS):
                            turned_to_high(0, k)
                    for g in computed:
                        for i in range(g * HALVES * hid_tiles, (g + 1) * HALVES * hid_tiles):
                            act.wait_ge(s_hidden, i + 1)
                            if i >= 2:
                                act.wait_ge(s_low, i - 1)
                            f = i % hid_tiles
                            nc.scalar.activation(act_full[:, i % 2, :], hidden[i % 3][:], ACT.Gelu,
                                                 bias=bias_1[:, f:f + 1]).then_inc(s_gelu, 1)
                        for k in range(TURNS):
                            turned_to_high(g, k)

                @block.vector
                def _(dve):
                    def take_moments(h):
                        dve.wait_ge(s_x, 16 * (h + 1))
                        for i in range(TILES):
                            tile_moments(nc, dve, x_sb[:, parity(h), i, :], stats[:, i, :], moments[:, i, :], s_stats,
                                         h * TILES + i, s_moments)

                    def norm(h):
                        dve.wait_ge(s_deviation, h + 1)
                        if h:
                            dve.wait_ge(s_turned, TURNS * h)
                        for i in range(TILES):
                            center_and_scale(nc, normed[:, i, :], x_sb[:, parity(h), i, :],
                                             moments[:, i, :]).then_inc(s_normed, 1)

                    def turned_to_low(h, k):
                        i = h * TURNS + k
                        dve.wait_ge(s_turned_high, i + 1)
                        nc.vector.tensor_tensor(turned_view(xt_low, h, k), turned[i % 2][:],
                                                turned_view(xt_high, h, k).bitcast(F32),
                                                ALU.subtract).then_inc(s_turned_low, 1)

                    if not attend:
                        take_moments(0)
                        norm(0)
                        for k in range(TURNS):
                            turned_to_low(0, k)
                    for g in computed:
                        for n in range(HALVES):
                            for f in range(hid_tiles):
                                i = (g * HALVES + n) * hid_tiles + f
                                dve.wait_ge(s_gelu, i + 1)
                                if i >= hid_tiles and f == 0:
                                    dve.wait_ge(s_projected, (g * HALVES + n) * ROWS)
                                nc.vector.tensor_copy(act_high[:, f, :], act_full[:, i % 2, :]).then_inc(s_high, 1)
                                dve.wait_ge(s_high, i + 1)
                                nc.vector.tensor_tensor(act_low[:, f, :], act_full[:, i % 2, :],
                                                        act_high[:, f, :].bitcast(F32), ALU.subtract).then_inc(s_low, 1)
                            if n == 0:
                                take_moments(g)
                            for j in range(ROWS):
                                i = (g * HALVES + n) * ROWS + j
                                row = x_sb[:, g % 2, n * ROWS + j, :]
                                if n == HALVES - 1:
                                    turned_to_low(g, j)
                                dve.wait_ge(s_projected, i + 1)
                                if g:
                                    dve.wait_ge(s_residual, (g - 1) * TILES + n * ROWS + j + 1)
                                nc.vector.tensor_tensor(row, projected[i % 3][:], row, ALU.add).then_inc(s_sum, 1)
                            if n == 0:
                                norm(g)

        iteration(None, 0, False)
        m.clear()
        with nc.Fori(0, BATCH // SPAN) as span:
            iteration([span * SPAN + g for g in range(SPAN)], (span * SPAN + SPAN) % BATCH, True)
            m.clear()



def single_head_layer(nc, tag, x_dram, adj_dram, ident_dram, w, out_dram):
    scale = float(DIM) ** -0.5
    with ExitStack() as ctx:
        m = Pool(nc, ctx, tag)
        ident = m.sb("ident", [P, P])
        qk_high, qk_low, vo_high, vo_low = (m.sb(n, [P, DIM_TILES, DIM], F32R)
                                            for n in ("qk_high", "qk_low", "vo_high", "vo_low"))
        spreads = m.sb("spreads", [P, 3, DIM])
        bias_o, gamma, beta = (spreads[:, i, :] for i in range(3))
        with ExitStack() as prep:
            t = Pool(nc, prep, tag + "_prep")
            raw = t.sb("raw", [P, 4 * DIM_TILES, DIM])
            wq_t, wk_t, wv_t, wo = (raw[:, i * DIM_TILES:(i + 1) * DIM_TILES, :] for i in range(4))
            raw_qk, raw_vo = t.sb("raw_qk", [P, DIM_TILES, DIM]), t.sb("raw_vo", [P, DIM_TILES, DIM])
            load_all(nc, [(raw[:], matrices(w["matrices"])), (ident[:], ident_dram),
                          (spreads[:].rearrange("p v n -> p (v n)"), spread(w["spreads"]))], tag + "_load")
            product = [t.ps(f"product{i}", [P, DIM]) for i in range(4)]
            s_product, s_copied = t.sem("product"), t.sem("copied")
            with nc.Block() as block:

                @block.tensor
                def _(pe):
                    for i, (left, right) in enumerate(((wq_t, wk_t), (wv_t, wo))):
                        for r in range(DIM_TILES):
                            for k in range(DIM_TILES):
                                op = nc.tensor.matmul(product[2 * i + r][:], left[:, k, r * P:(r + 1) * P],
                                                      right[:, k, :], start=(k == 0), stop=(k == DIM_TILES - 1))
                            op.then_inc(s_product, 1)

                @block.vector
                def _(dve):
                    for i, raw in enumerate((raw_qk, raw_vo)):
                        for r in range(DIM_TILES):
                            dve.wait_ge(s_product, 2 * i + r + 1)
                            nc.vector.tensor_copy(raw[:, r, :], product[2 * i + r][:]).then_inc(s_copied, 1)
                    dve.wait_ge(s_copied, 4)

            t.clear()
            split_weights(nc, [(raw_qk[:], qk_high[:], qk_low[:], -scale, None),
                               (raw_vo[:], vo_high[:], vo_low[:], None, None)], tag + "_split")

        x_in = m.sb("x_in", [P, TILES, DIM])
        result = m.sb("result", [P, 2, TILES, DIM])
        adj_sb = m.sb("adj", [P, 2, SEQ], I32)
        penalty = m.sb("penalty", [P, 2, SEQ])
        xt_high, xt_low, q_high, q_low = (m.sb(n, [P, 2, DIM_TILES, SEQ], F32R)
                                          for n in ("xt_high", "xt_low", "q_high", "q_low"))
        v_high, v_low = (m.sb(n, [P, 2, TILES, DIM], F32R) for n in ("v_high", "v_low"))
        probs = m.sb("probs", [P, 3, SEQ])
        probs_t_high, probs_t_low = (m.sb(n, [P, 2, TILES, P], F32R) for n in ("probs_t_high", "probs_t_low"))
        row_min, row_sum, inverse = (m.sb(n, [P, TILES]) for n in ("row_min", "row_sum", "inverse"))
        stats, moments = m.sb("stats", [P, TILES, STATS]), m.sb("moments", [P, TILES, 2])
        exponent = m.sb("exponent", [P, 1])
        fill(nc, exponent[:], -0.5, tag + "_exponent")
        scores = [m.ps(f"scores{i}", [P, BANK]) for i in range(4)]
        turned = [m.ps(f"turned{i}", [P, BANK]) for i in range(2)]
        summed, side = m.ps("summed", [P, DIM]), m.ps("side", [P, BANK])

        s_x, s_residual = m.sem("x"), m.sem("residual")
        s_adj = [m.sem(f"adj{i}") for i in range(2)]
        s_penalty = m.sem("penalty")
        s_side, s_side_high, s_side_free = m.sem("side"), m.sem("side_high"), m.sem("side_free")
        s_scores, s_first_min, s_min, s_probs = m.sem("scores"), m.sem("first_min"), m.sem("min"), m.sem("probs")
        s_turned, s_turned_high, s_turned_low = m.sem("turned"), m.sem("turned_high"), m.sem("turned_low")
        s_inverse, s_summed, s_sum = m.sem("inverse"), m.sem("summed"), m.sem("sum")
        s_stats, s_moments, s_shifted, s_deviation = (m.sem("stats"), m.sem("moments"), m.sem("shifted"),
                                                      m.sem("deviation"))
        s_gained, s_result = m.sem("gained"), m.sem("result")
        s_out = [m.sem(f"out{i}") for i in range(4)]

        AHEAD = 2
        TURNS = DIM_TILES * HALVES
        QUERY_BLOCKS = DIM_TILES * HALVES
        VALUE_BLOCKS = TILES * DIM // BANK
        UNITS = TURNS + QUERY_BLOCKS + VALUE_BLOCKS
        FIRST_SLOT = 4
        TAIL = 4

        def iteration(graphs, b_next, attend):
            prepared = [*graphs[1:], b_next] if attend else [b_next]
            items = SPAN * TILES if attend else 0
            steps = items + TAIL if attend else TILES

            def units_of(step, slot):
                h, k = step // TILES, 2 * (step % TILES) + slot - FIRST_SLOT
                return [(h * UNITS + k, h, k)] if h < len(prepared) and 0 <= k < UNITS else []

            side_banks = [side] if attend else [*scores, side]

            def parity(h):
                return (h + 1) % 2 if attend else 0

            def view(dram, b):
                return of_batch(dram, b).rearrange("(t p) k -> p t k", p=P)

            def side_places(h, k):
                g = parity(h)
                if k < TURNS + QUERY_BLOCKS:
                    d, n = k % DIM_TILES, (k // DIM_TILES) % HALVES
                    cols = slice(n * BANK, (n + 1) * BANK)
                    high, low = (xt_high, xt_low) if k < TURNS else (q_high, q_low)
                    return high[:, g, d, cols], low[:, g, d, cols]
                n = k - TURNS - QUERY_BLOCKS
                rows = slice(2 * n, 2 * n + 2)
                return (v_high[:, g, rows, :].rearrange("p t d -> p (t d)"),
                        v_low[:, g, rows, :].rearrange("p t d -> p (t d)"))

            with nc.Block() as block:

                @block.sync
                def _(sp):
                    def load_adj(item):
                        g, tile = divmod(item, TILES)
                        source = view(adj_dram, graphs[g] if attend and g < SPAN else b_next)
                        sp.dma_start(adj_sb[:, item % 2, :], source[:, tile, :]).then_inc(s_adj[item % 2], 16)

                    for step in range(steps):
                        if attend and step == 0:
                            load_adj(AHEAD)
                            load_adj(AHEAD + 1)
                        if step % TILES == 0 and step // TILES < len(prepared):
                            h = step // TILES
                            if h:
                                sp.wait_ge(s_side, UNITS * (h - 1) + TURNS)
                                sp.wait_ge(s_residual, TILES * h)
                            sp.dma_start(x_in[:], view(x_dram, prepared[h])).then_inc(s_x, 16)
                        if not attend:
                            if step < AHEAD:
                                load_adj(SPAN * TILES + step)
                            continue
                        item = step + AHEAD + 1
                        if AHEAD + 2 <= item < items + AHEAD:
                            sp.wait_ge(s_penalty, step)
                            load_adj(item)
                        item = step - TAIL
                        if 0 <= item < items:
                            g, tile = divmod(item, TILES)
                            sp.wait_ge(s_result, item + 1)
                            sp.dma_start(view(out_dram, graphs[g])[:, tile, :], result[:, g % 2, tile, :]
                                         ).then_inc(s_out[item % len(s_out)], 16)
                    if attend:
                        for slot in s_out:
                            sp.wait_ge(slot, 16 * items // len(s_out))

                @block.gpsimd
                def _(pool):
                    made = 0
                    for step in range(steps):
                        item = step - 3
                        if attend and 0 <= item < items:
                            pool.wait_ge(s_moments, item + 1)
                            inverse_deviation(nc, pool, moments[:, item % TILES, 1:2], exponent[:], s_shifted, item,
                                              s_deviation)
                        item = step + AHEAD if attend else SPAN * TILES + step
                        if item < SPAN * TILES + AHEAD:
                            pool.wait_ge(s_adj[item % 2], 16 * (made // 2 + 1))
                            if attend:
                                pool.wait_ge(s_min, item - AHEAD + 1)
                            nc.gpsimd.tensor_scalar(penalty[:, item % 2, :], adj_sb[:, item % 2, :], 0.0, PENALTY,
                                                    ALU.is_equal, ALU.mult).then_inc(s_penalty, 1)
                            made += 1
                        h = step // TILES
                        if h >= len(prepared):
                            continue
                        for tile in range(TILES):
                            if step % TILES != 3 + tile // 2:
                                continue
                            if tile == 0:
                                pool.wait_ge(s_x, 16 * (h + 1))
                            if h:
                                item = TILES * (h - 1) + tile
                                pool.wait_ge(s_out[item % len(s_out)], 16 * (item // len(s_out) + 1))
                            nc.gpsimd.tensor_tensor(result[:, parity(h), tile, :], x_in[:, tile, :], bias_o,
                                                    ALU.add).then_inc(s_residual, 1)

                @block.tensor
                def _(pe):
                    def side_product(number, h, k):
                        g = parity(h)
                        bank = side_banks[number % len(side_banks)]
                        if number >= len(side_banks):
                            pe.wait_ge(s_side_free, number - len(side_banks) + 1)
                        if k >= TURNS and number < TURNS + len(side_banks):
                            pe.wait_ge(s_side_free, h * UNITS + TURNS)
                        if k == 0:
                            pe.wait_ge(s_x, 16 * (h + 1))
                        if k < TURNS:
                            d, n = k % DIM_TILES, k // DIM_TILES
                            for j in range(4):
                                op = nc.tensor.transpose(bank[:, j * P:(j + 1) * P],
                                                         x_in[:, 4 * n + j, d * P:(d + 1) * P], ident[:])
                        elif k < TURNS + QUERY_BLOCKS:
                            d, n = k % DIM_TILES, (k - TURNS) // DIM_TILES
                            cols = slice(n * BANK, (n + 1) * BANK)
                            for c in range(DIM_TILES):
                                op = split_matmul(nc, bank[:], qk_high[:, c, d * P:(d + 1) * P],
                                                  qk_low[:, c, d * P:(d + 1) * P], xt_high[:, g, c, cols],
                                                  xt_low[:, g, c, cols], c == 0, c == DIM_TILES - 1)
                        else:
                            for j in range(BANK // DIM):
                                tile = (k - TURNS - QUERY_BLOCKS) * (BANK // DIM) + j
                                for c in range(DIM_TILES):
                                    op = split_matmul(nc, bank[:, j * DIM:(j + 1) * DIM],
                                                      xt_high[:, g, c, tile * P:(tile + 1) * P],
                                                      xt_low[:, g, c, tile * P:(tile + 1) * P],
                                                      vo_high[:, c, :], vo_low[:, c, :], c == 0, c == DIM_TILES - 1)
                        op.then_inc(s_side, 1)

                    def score(item):
                        g, tile = divmod(item, TILES)
                        if item >= 2:
                            pe.wait_ge(s_min, item - 1)
                        if g and tile == 0:
                            pe.wait_ge(s_side_free, UNITS * (g - 1) + TURNS + QUERY_BLOCKS)
                        for n in range(HALVES):
                            for k in range(DIM_TILES):
                                op = split_matmul(nc, scores[2 * (item % 2) + n][:],
                                                  q_high[:, g % 2, k, tile * P:(tile + 1) * P],
                                                  q_low[:, g % 2, k, tile * P:(tile + 1) * P],
                                                  xt_high[:, g % 2, k, n * BANK:(n + 1) * BANK],
                                                  xt_low[:, g % 2, k, n * BANK:(n + 1) * BANK],
                                                  k == 0, k == DIM_TILES - 1)
                        op.then_inc(s_scores, 1)

                    def turn(item):
                        pe.wait_ge(s_probs, item + 1)
                        for half in range(2):
                            n = 2 * item + half
                            if n >= 2:
                                pe.wait_ge(s_turned_low, n - 1)
                            for j in range(4):
                                k = 4 * half + j
                                op = nc.tensor.transpose(turned[n % 2][:, j * P:(j + 1) * P],
                                                         probs[:, item % 3, k * P:(k + 1) * P], ident[:])
                            op.then_inc(s_turned, 1)

                    def weigh(item):
                        g, tile = divmod(item, TILES)
                        if item >= 1:
                            pe.wait_ge(s_sum, item)
                        if g and tile == 0:
                            pe.wait_ge(s_side_free, UNITS * g)
                        for k in range(TILES):
                            if k % 4 == 0:
                                pe.wait_ge(s_turned_low, 2 * item + k // 4 + 1)
                            op = split_matmul(nc, summed[:], probs_t_high[:, item % 2, k, :],
                                              probs_t_low[:, item % 2, k, :], v_high[:, g % 2, k, :],
                                              v_low[:, g % 2, k, :], k == 0, k == TILES - 1)
                        op.then_inc(s_summed, 1)

                    for step in range(steps):
                        if step < items:
                            score(step)
                        for unit in units_of(step, 0):
                            side_product(*unit)
                        if 1 <= step <= items:
                            turn(step - 1)
                        if 2 <= step <= items + 1:
                            weigh(step - 2)
                        for unit in units_of(step, 1):
                            side_product(*unit)

                @block.scalar
                def _(act):
                    def side_high(number, h, k):
                        act.wait_ge(s_side, number + 1)
                        if h and k == 0:
                            act.wait_ge(s_scores, TILES * h)
                        if h and k == TURNS + QUERY_BLOCKS:
                            act.wait_ge(s_summed, TILES * h)
                        bank = side_banks[number % len(side_banks)]
                        nc.scalar.copy(side_places(h, k)[0], bank[:]).then_inc(s_side_high, 1)

                    for step in range(steps):
                        if step < items:
                            act.wait_ge(s_min, step + 1)
                            nc.scalar.activation(probs[:, step % 3, :], probs[:, step % 3, :], ACT.Exp,
                                                 bias=row_min[:, step % TILES:step % TILES + 1], scale=-1.0,
                                                 accum_out=row_sum[:, step % TILES:step % TILES + 1]
                                                 ).then_inc(s_probs, 1)
                        for unit in units_of(step, 0):
                            side_high(*unit)
                        item = step - 1
                        if 0 <= item < items:
                            for half in range(2):
                                n = 2 * item + half
                                act.wait_ge(s_turned, n + 1)
                                if item >= 2:
                                    act.wait_ge(s_summed, item - 1)
                                nc.scalar.copy(
                                    probs_t_high[:, item % 2, 4 * half:4 * half + 4, :].rearrange("p k q -> p (k q)"),
                                    turned[n % 2][:]).then_inc(s_turned_high, 1)
                        for unit in units_of(step, 1):
                            side_high(*unit)

                @block.vector
                def _(dve):
                    def side_low(number, h, k):
                        high, low = side_places(h, k)
                        dve.wait_ge(s_side_high, number + 1)
                        nc.vector.tensor_tensor(low, side_banks[number % len(side_banks)][:], high.bitcast(F32),
                                                ALU.subtract).then_inc(s_side_free, 1)

                    for step in range(steps):
                        if step < items:
                            dve.wait_ge(s_scores, step + 1)
                            if step >= AHEAD:
                                dve.wait_ge(s_penalty, step - AHEAD + 1)
                            if step >= 3:
                                dve.wait_ge(s_turned, 2 * (step - 2))
                            least = row_min[:, step % TILES:step % TILES + 1]
                            for n in range(HALVES):
                                cols = slice(n * BANK, (n + 1) * BANK)
                                nc.vector.tensor_tensor_reduce(
                                    out=probs[:, step % 3, cols], in0=scores[2 * (step % 2) + n][:],
                                    in1=penalty[:, step % 2, cols], scale=1.0, scalar=3.0e38 if n == 0 else least,
                                    op0=ALU.add, op1=ALU.min, accum_out=least
                                    ).then_inc(s_first_min if n == 0 else s_min, 1)
                                if n == 0:
                                    dve.wait_ge(s_first_min, step + 1)
                        for unit in units_of(step, 0):
                            side_low(*unit)
                        item = step - 1
                        if 0 <= item < items:
                            for half in range(2):
                                n = 2 * item + half
                                dve.wait_ge(s_turned_high, n + 1)
                                part = slice(4 * half, 4 * half + 4)
                                nc.vector.tensor_tensor(
                                    probs_t_low[:, item % 2, part, :].rearrange("p k q -> p (k q)"), turned[n % 2][:],
                                    probs_t_high[:, item % 2, part, :].rearrange("p k q -> p (k q)").bitcast(F32),
                                    ALU.subtract).then_inc(s_turned_low, 1)
                            dve.wait_ge(s_probs, item + 1)
                            nc.vector.reciprocal(inverse[:, item % TILES:item % TILES + 1],
                                                 row_sum[:, item % TILES:item % TILES + 1]).then_inc(s_inverse, 1)
                        item = step - 3
                        if 0 <= item < items:
                            row = result[:, item // TILES % 2, item % TILES, :]
                            dve.wait_ge(s_deviation, item + 1)
                            dve.wait_ge(s_gained, item + 1)
                            scale_and_shift(nc, row, row, moments[:, item % TILES, :], beta).then_inc(s_result, 1)
                        item = step - 2
                        if 0 <= item < items:
                            g, tile = divmod(item, TILES)
                            row = result[:, g % 2, tile, :]
                            dve.wait_ge(s_summed, item + 1)
                            dve.wait_ge(s_inverse, item + 1)
                            if g:
                                dve.wait_ge(s_residual, TILES * (g - 1) + tile + 1)
                            nc.vector.scalar_tensor_tensor(row, summed[:], inverse[:, tile:tile + 1], row, ALU.mult,
                                                           ALU.add).then_inc(s_sum, 1)
                            dve.wait_ge(s_sum, item + 1)
                            tile_moments(nc, dve, row, stats[:, tile, :], moments[:, tile, :], s_stats, item,
                                         s_moments)
                            dve.wait_ge(s_moments, item + 1)
                            center_and_gain(nc, row, row, moments[:, tile, :], gamma).then_inc(s_gained, 1)
                        for unit in units_of(step, 1):
                            side_low(*unit)

        iteration(None, 0, False)
        m.clear()
        with nc.Fori(0, BATCH // SPAN) as span:
            iteration([span * SPAN + g for g in range(SPAN)], (span * SPAN + SPAN) % BATCH, True)
            m.clear()


def named(layer, *names):
    return [f"{layer}_gnn_{name}" for name in names]


PACKED = {
    "L0": {"matrices": named("L0", "wq", "wk", "wv", "wo"), "columns": named("L0", "bq", "bk", "bv", "ln1_g", "ln1_b"),
           "spreads": named("L0", "bo")},
    "MLP": {"columns": named("L0", "ln2_g", "ln2_b", "b1")},
    "L1": {"matrices": named("L1", "Wq", "Wk", "Wv", "Wo"), "spreads": named("L1", "bo", "gamma", "beta")},
    "L2": {"matrices": named("L2", "Wq", "Wk", "Wv", "Wo"), "spreads": named("L2", "bo", "gamma", "beta")},
    "L3": {"matrices": named("L3", "Wq", "Wk", "Wv", "Wo"), "columns": named("L3", "bq", "bk", "bv"),
           "spreads": named("L3", "bo", "gamma", "beta")},
}
TURNED = [name for layer in ("L1", "L2") for name in named(layer, "Wq", "Wk", "Wv")]


def graph_layers(nc, a, out):
    def scratch(name):
        return nc.dram_tensor(name, [BATCH, SEQ, DIM], F32).ap()

    attended, after_0, after_1, after_2 = (scratch(n) for n in ("attended", "after_0", "after_1", "after_2"))
    adj, ident = a["adj"], a["ident"]

    def packed(layer):
        return {k: a[f"{layer}_{k}"] for k in PACKED[layer]}

    multi_head_layer(nc, "l0", a["x"], adj, ident, packed("L0"), attended, True)
    mlp_layer(nc, "mlp", attended, ident,
              packed("MLP") | {"w1": a["L0_gnn_w1"], "w2": a["L0_gnn_w2"], "b2": a["L0_gnn_b2"]}, after_0)
    single_head_layer(nc, "l1", after_0, adj, ident, packed("L1"), after_1)
    single_head_layer(nc, "l2", after_1, adj, ident, packed("L2"), after_2)
    multi_head_layer(nc, "l3", after_2, adj, ident, packed("L3"), out, False)


def kernel(**inputs):
    import numpy as np
    import concourse.bacc as bacc
    from concourse.bass_utils import run_bass_kernel_spmd

    nc = bacc.Bacc("TRN2", target_bir_lowering=False, num_devices=1)
    arrays = {name: np.ascontiguousarray(value) for name, value in inputs.items()}
    for layer, packs in PACKED.items():
        for kind, names in packs.items():
            parts = [arrays.pop(name) for name in names]
            if kind == "matrices":
                arrays[f"{layer}_{kind}"] = np.stack([part.T if name in TURNED else part
                                                      for name, part in zip(names, parts)])
            else:
                arrays[f"{layer}_{kind}"] = np.concatenate(parts)
    arrays["ident"] = np.eye(P, dtype=np.float32)
    drams = {name: nc.dram_tensor(name, value.shape, mybir.dt.from_np(value.dtype), kind="ExternalInput").ap()
             for name, value in arrays.items()}
    out = nc.dram_tensor("hidden_out", (BATCH, SEQ, DIM), F32, kind="ExternalOutput").ap()
    graph_layers(nc, drams, out)
    r = run_bass_kernel_spmd(nc, [arrays], core_ids=[0])
    return r.results[0]["hidden_out"]
```
